# Optimizing a Trainium2 kernel written in Bass

```python
import numpy as np
import jax
import jax.numpy as jnp

def _softmax(x, axis=-1):
    return jax.nn.softmax(x, axis=axis)

def _gelu(x):
    return jax.nn.gelu(x, approximate=True)

def _silu(x):
    return jax.nn.silu(x)

def _sigmoid(x):
    return jax.nn.sigmoid(x)

def _layernorm(x, axis=-1, eps=1e-05):
    m = jnp.mean(x, axis=axis, keepdims=True)
    v = jnp.var(x, axis=axis, keepdims=True)
    return (x - m) / jnp.sqrt(v + eps)

def _scatter_add(tgt, idx, src, axis=0):
    return tgt.at[idx].add(src)

def _segment_sum(src, seg, n):
    return jax.ops.segment_sum(src, seg, n)
kernel_name = 'mk_xattn_ffn_d2_seqx_r4_407cd9'

def setup_inputs(seed: int=0):
    np.random.seed(seed)
    _w = jnp.asarray

    def _rec_inputs():
        import jax
        import jax.numpy as jnp
        _rk = jax.random.key(seed)
        x = -0.0002928 + 1 * jax.random.normal(jax.random.fold_in(_rk, 1), (2, 1024, 256), jnp.float32)
        _lenS = 1024 - jax.random.randint(jax.random.fold_in(_rk, 7), (2,), 0, max(1, 1024 // 4) + 1, jnp.int32)
        _lenS2 = 77 - jax.random.randint(jax.random.fold_in(_rk, 8), (2,), 0, max(1, 77 // 4) + 1, jnp.int32)
        _ctx_1024P = jax.random.normal(jax.random.fold_in(_rk, 11), (2, 16, 256), jnp.float32)
        _ctx_1024c = jax.random.dirichlet(jax.random.fold_in(_rk, 511), 0.3 * jnp.ones((16,), jnp.float32), (2, 77))
        _ctx_1024t = jnp.einsum('bsk,bkd->bsd', _ctx_1024c, _ctx_1024P)
        _ctx_1024t = _ctx_1024t * jax.lax.rsqrt(jnp.mean(jnp.square(_ctx_1024t)) + 1e-12) * 0.953939
        ctx_1024 = -1.39393e-06 + 0.999914 * (_ctx_1024t + 0.3 * jax.random.normal(jax.random.fold_in(_rk, 611), (2, 77, 256), jnp.float32))
        return (x, ctx_1024)
    x, ctx_1024 = _rec_inputs()

    def _L0_xattn_setup():
        import jax, jax.numpy as jnp
        import numpy as np
        D_MODEL = 256
        N_HEAD = 16
        D_HEAD = D_MODEL // N_HEAD
        key = jax.random.key(seed)
        ks = jax.random.split(key, 6)
        B, L, M = (2, 512, 512)
        q = jax.random.normal(ks[0], (B, L, D_MODEL), dtype=jnp.float32)
        kv = jax.random.normal(ks[1], (B, L, D_MODEL), dtype=jnp.float32)
        mem = jax.random.normal(ks[2], (B, M, D_MODEL), dtype=jnp.float32)
        s = 1.0 / np.sqrt(D_MODEL)
        w_q = jax.random.normal(ks[3], (D_MODEL, D_MODEL), dtype=jnp.float32) * s
        w_kv = jax.random.normal(ks[4], (D_MODEL, 2 * D_HEAD), dtype=jnp.float32) * s
        w_concat = jax.random.normal(ks[5], (D_MODEL, D_MODEL), dtype=jnp.float32) * s
        return {'q': q, 'kv': kv, 'mem': mem, 'w_q': w_q, 'w_kv': w_kv, 'w_concat': w_concat}
    _L0_xattn_all = _L0_xattn_setup()
    _L0_xattn_in = {k: v for k, v in _L0_xattn_all.items() if k in ('w_q', 'w_kv', 'w_concat')}
    del _L0_xattn_all

    def _L0_ffn_setup():
        import jax, jax.numpy as jnp
        import numpy as np
        TOP_K = 2
        key = jax.random.key(seed)
        ks = jax.random.split(key, 5)
        B, S, H, I, E = (4, 512, 256, 1024, 8)
        scale_hi = (2.0 / (H + I)) ** 0.5
        scale_he = (2.0 / (H + E)) ** 0.5
        return {'x': jax.random.normal(ks[0], (B, S, H), dtype=jnp.float32), 'router_w': jax.random.normal(ks[1], (E, H), dtype=jnp.float32) * scale_he, 'gate_w': jax.random.normal(ks[2], (E, I, H), dtype=jnp.float32) * scale_hi, 'up_w': jax.random.normal(ks[3], (E, I, H), dtype=jnp.float32) * scale_hi, 'down_w': jax.random.normal(ks[4], (E, H, I), dtype=jnp.float32) * scale_hi}
    _L0_ffn_all = _L0_ffn_setup()
    _L0_ffn_in = {k: v for k, v in _L0_ffn_all.items() if k in ('router_w', 'gate_w', 'up_w', 'down_w')}
    del _L0_ffn_all

    def _L1_xattn_setup():
        import jax, jax.numpy as jnp
        import numpy as np
        B, S, D_IN, D_MODEL = (4, 512, 256, 256)
        key = jax.random.key(seed)
        ks = jax.random.split(key, 9)
        return {'q': jax.random.normal(ks[0], (B, S, D_IN), jnp.float32), 'k': jax.random.normal(ks[1], (B, S, D_IN), jnp.float32), 'v': jax.random.normal(ks[2], (B, S, D_IN), jnp.float32), 'Wq': jax.random.normal(ks[3], (D_IN, D_MODEL), jnp.float32) * 0.02, 'bq': jax.random.normal(ks[4], (D_MODEL,), jnp.float32) * 0.02, 'Wk': jax.random.normal(ks[5], (D_IN, D_MODEL), jnp.float32) * 0.02, 'bk': jax.random.normal(ks[6], (D_MODEL,), jnp.float32) * 0.02, 'Wv': jax.random.normal(ks[7], (D_IN, D_MODEL), jnp.float32) * 0.02, 'bv': jax.random.normal(ks[8], (D_MODEL,), jnp.float32) * 0.02}
    _L1_xattn_all = _L1_xattn_setup()
    _L1_xattn_in = {k: v for k, v in _L1_xattn_all.items() if k in ('Wq', 'bq', 'Wk', 'bk', 'Wv', 'bv')}
    del _L1_xattn_all

    def _L1_ffn_setup():
        import jax, jax.numpy as jnp
        import numpy as np
        DIM = 256
        HIDDEN = 256
        NUM_EXPERTS = 8
        TOP_K = 2
        key = jax.random.key(seed)
        ks = jax.random.split(key, 8)
        std = 0.02
        x = jax.random.normal(ks[0], (2, 256, DIM), dtype=jnp.float32)
        gate_w = jax.random.normal(ks[1], (NUM_EXPERTS, DIM), dtype=jnp.float32) * std
        w1 = jax.random.normal(ks[2], (NUM_EXPERTS, DIM, HIDDEN), dtype=jnp.float32) * std
        w2 = jax.random.normal(ks[3], (NUM_EXPERTS, HIDDEN, DIM), dtype=jnp.float32) * std
        w3 = jax.random.normal(ks[4], (NUM_EXPERTS, DIM, HIDDEN), dtype=jnp.float32) * std
        w1s = jax.random.normal(ks[5], (1, DIM, HIDDEN), dtype=jnp.float32) * std
        w2s = jax.random.normal(ks[6], (1, HIDDEN, DIM), dtype=jnp.float32) * std
        w3s = jax.random.normal(ks[7], (1, DIM, HIDDEN), dtype=jnp.float32) * std
        return {'x': x, 'gate_w': gate_w, 'w1': w1, 'w2': w2, 'w3': w3, 'w1s': w1s, 'w2s': w2s, 'w3s': w3s}
    _L1_ffn_all = _L1_ffn_setup()
    _L1_ffn_in = {k: v for k, v in _L1_ffn_all.items() if k in ('gate_w', 'w1', 'w2', 'w3', 'w1s', 'w2s', 'w3s')}
    del _L1_ffn_all
    return {'x': x, 'ctx_1024': ctx_1024, 'L0_xattn_w_q': _L0_xattn_in['w_q'], 'L0_xattn_w_kv': _L0_xattn_in['w_kv'], 'L0_xattn_w_concat': _L0_xattn_in['w_concat'], 'L0_ffn_router_w': _L0_ffn_in['router_w'], 'L0_ffn_gate_w': _L0_ffn_in['gate_w'], 'L0_ffn_up_w': _L0_ffn_in['up_w'], 'L0_ffn_down_w': _L0_ffn_in['down_w'], 'L1_xattn_Wq': _L1_xattn_in['Wq'], 'L1_xattn_bq': _L1_xattn_in['bq'], 'L1_xattn_Wk': _L1_xattn_in['Wk'], 'L1_xattn_bk': _L1_xattn_in['bk'], 'L1_xattn_Wv': _L1_xattn_in['Wv'], 'L1_xattn_bv': _L1_xattn_in['bv'], 'L1_ffn_gate_w': _L1_ffn_in['gate_w'], 'L1_ffn_w1': _L1_ffn_in['w1'], 'L1_ffn_w2': _L1_ffn_in['w2'], 'L1_ffn_w3': _L1_ffn_in['w3'], 'L1_ffn_w1s': _L1_ffn_in['w1s'], 'L1_ffn_w2s': _L1_ffn_in['w2s'], 'L1_ffn_w3s': _L1_ffn_in['w3s']}

def reference(x, ctx_1024, L0_xattn_w_q, L0_xattn_w_kv, L0_xattn_w_concat, L0_ffn_router_w, L0_ffn_gate_w, L0_ffn_up_w, L0_ffn_down_w, L1_xattn_Wq, L1_xattn_bq, L1_xattn_Wk, L1_xattn_bk, L1_xattn_Wv, L1_xattn_bv, L1_ffn_gate_w, L1_ffn_w1, L1_ffn_w2, L1_ffn_w3, L1_ffn_w1s, L1_ffn_w2s, L1_ffn_w3s):
    import jax
    import jax.numpy as jnp

    def _L0_xattn_ref(q, kv, mem, w_q, w_kv, w_concat):
        import jax, jax.numpy as jnp
        import numpy as np
        D_MODEL = 256
        N_HEAD = 16
        D_HEAD = D_MODEL // N_HEAD
        B, L, D = q.shape
        c = jnp.concatenate([mem, kv], axis=1)
        qh = (q @ w_q).reshape(B, L, N_HEAD, D_HEAD).transpose(0, 2, 1, 3)
        kvp = c @ w_kv
        k, v = (kvp[..., :D_HEAD], kvp[..., D_HEAD:])
        attn_score = jnp.einsum('bhid,bjd->bhij', qh, k) / np.sqrt(D_HEAD)
        attn_prob = jax.nn.softmax(attn_score, axis=-1)
        out = jnp.einsum('bhij,bjd->bhid', attn_prob, v)
        out = out.transpose(0, 2, 1, 3).reshape(B, L, D)
        return out @ w_concat

    def _L0_ffn_ref(x, router_w, gate_w, up_w, down_w):
        import jax, jax.numpy as jnp
        import numpy as np
        TOP_K = 2
        B, S, H = x.shape
        E = router_w.shape[0]
        xf = x.reshape(-1, H)
        logits = xf @ router_w.T
        probs = jax.nn.softmax(logits, axis=-1)
        topk_p, topk_i = jax.lax.top_k(probs, TOP_K)
        topk_p = topk_p / topk_p.sum(axis=-1, keepdims=True)

        def body(out, inputs):
            e, gw, uw, dw = inputs
            sel = topk_i == e
            mask = sel.any(axis=-1)
            w_tok = (topk_p * sel).sum(axis=-1)
            cnt = mask.sum().astype(xf.dtype)
            mean_w = jnp.where(cnt > 0, w_tok.sum() / jnp.maximum(cnt, 1.0), 0.0)
            h = jax.nn.silu(xf @ gw.T) * (xf @ uw.T)
            eo = h @ dw.T
            out = out + mask[:, None].astype(xf.dtype) * eo * mean_w
            return (out, None)
        out0 = jnp.zeros_like(xf)
        out, _ = jax.lax.scan(body, out0, (jnp.arange(E), gate_w, up_w, down_w))
        return out.reshape(B, S, H)

    def _L1_xattn_ref(q, k, v, Wq, bq, Wk, bk, Wv, bv):
        import jax, jax.numpy as jnp
        import numpy as np
        B, S, D_IN, D_MODEL = (4, 512, 256, 256)
        qp = jnp.einsum('bsd,de->bse', q, Wq) + bq
        kp = jnp.einsum('bsd,de->bse', k, Wk) + bk
        vp = jnp.einsum('bsd,de->bse', v, Wv) + bv
        scale = 1.0 / jnp.sqrt(jnp.asarray(kp.shape[-1], jnp.float32))
        logits = jnp.einsum('bqe,bke->bqk', qp, kp) * scale
        attn = jax.nn.softmax(logits, axis=-1)
        return jnp.einsum('bqk,bke->bqe', attn, vp)

    def _L1_ffn_ref(x, gate_w, w1, w2, w3, w1s, w2s, w3s):
        import jax, jax.numpy as jnp
        import numpy as np
        DIM = 256
        HIDDEN = 256
        NUM_EXPERTS = 8
        TOP_K = 2
        bs, slen, dim = x.shape
        xt = x.reshape(bs * slen, dim)
        logits = xt @ gate_w.T
        scores = jax.nn.softmax(logits.astype(jnp.float32), axis=1).astype(x.dtype)
        top_scores, sel = jax.lax.top_k(scores, TOP_K)
        sel_flat = sel.reshape(-1)
        order = jnp.argsort(sel_flat, stable=True)
        top_scores_sorted = top_scores.reshape(-1)[order]
        token_idx = order // TOP_K
        eid = sel_flat[order]
        routed_in = xt[token_idx] * top_scores_sorted[:, None]
        out_routed = jnp.zeros_like(routed_in)
        for e in range(NUM_EXPERTS):
            m = (eid == e)[:, None]
            xe = jnp.where(m, routed_in, 0.0)
            h = jax.nn.silu(xe @ w1[e]) * (xe @ w3[e])
            out_routed = out_routed + jnp.where(m, h @ w2[e], 0.0)
        hs = jax.nn.silu(xt @ w1s[0]) * (xt @ w3s[0])
        out = hs @ w2s[0]
        out = out.at[token_idx].add(out_routed)
        return out.reshape(bs, slen, dim)
    x = x + _L0_xattn_ref(_layernorm(x, axis=-1), ctx_1024, ctx_1024, L0_xattn_w_q, L0_xattn_w_kv, L0_xattn_w_concat)
    x = x + _L0_ffn_ref(_layernorm(x, axis=-1), L0_ffn_router_w, L0_ffn_gate_w, L0_ffn_up_w, L0_ffn_down_w)
    x = x + _L1_xattn_ref(_layernorm(x, axis=-1), ctx_1024, ctx_1024, L1_xattn_Wq, L1_xattn_bq, L1_xattn_Wk, L1_xattn_bk, L1_xattn_Wv, L1_xattn_bv)
    x = x + _L1_ffn_ref(_layernorm(x, axis=-1), L1_ffn_gate_w, L1_ffn_w1, L1_ffn_w2, L1_ffn_w3, L1_ffn_w1s, L1_ffn_w2s, L1_ffn_w3s)
    return x

_drawn_inputs = setup_inputs


def setup_inputs(seed=0):
    import zlib

    import numpy as np

    out = dict(_drawn_inputs(seed))
    spreads = {}
    factors = {'L1_xattn_Wq': 8.0,
     'L1_xattn_bq': 8.0,
     'L1_xattn_Wk': 8.0,
     'L1_xattn_bk': 8.0,
     'L1_xattn_bv': 3.603,
     'L1_ffn_gate_w': 8.0,
     'L1_ffn_w1': 8.0,
     'L1_ffn_w2': 8.0,
     'L1_ffn_w3': 8.0,
     'L1_ffn_w1s': 4.168,
     'L1_ffn_w2s': 4.141,
     'L1_ffn_w3s': 4.117}
    for name, (base, spread) in spreads.items():
        noise = np.random.default_rng([zlib.crc32(name.encode()), seed]).standard_normal(out[name].shape)
        drawn = base * np.exp(spread * noise) if base else spread * noise
        out[name] = jnp.asarray(drawn.astype(out[name].dtype))
    for name, factor in factors.items():
        out[name] = (out[name] * factor).astype(out[name].dtype)
    return out
```

```python
import numpy as np
import concourse.bass as bass
from concourse import mybir
from contextlib import ExitStack

P = 128
D = 256
KC = D // P
BATCH, SEQ, NKEY = 2, 1024, 77
NT = BATCH * SEQ // P
GT = 4
NG = NT // GT
GW = GT * P
HEADS, DH = 16, 16
UH = 8
UW = UH * NKEY
HB = UW // 2
NW = -(-UW // P)
VW = DH + 2
WINH = 3
KP = NKEY + 1
E = 8
FT = 256
ST = (NT * P * 2 + E * (FT - 1)) // FT
SH = ST * 2
ROWS = NT * P + P
F0, F1 = 1024, 256
G0 = F0 // (2 * P)
WB = 1024
NB0 = 6
EPS = 1e-5


class Count:

    def __init__(self, sem):
        self.sem, self.base, self.n, self.start = sem, 0, 0, 0

    def up(self, k=1):
        self.n += k
        return self.base + self.n

    def now(self):
        return self.base + self.n

    def enter(self, i, per, first=0):
        self.start = self.base + self.n
        self.per, self.base, self.n = per, (i - first) * per + self.start, 0

    def leave(self, trips):
        assert self.n == self.per, (self.n, self.per)
        self.base, self.n = self.start + trips * self.per, 0


def build_program(nc, A):
    f32, f32r, bf16, i32 = (mybir.dt.float32, mybir.dt.float32r, mybir.dt.bfloat16, mybir.dt.int32)
    ALU, ACT, AX = mybir.AluOpType, mybir.ActivationFunctionType, mybir.AxisListType
    ds = bass.ds
    ctx = ExitStack()
    with ctx:
        sem = lambda name: ctx.enter_context(nc.semaphore(name))

        kblk_d = nc.dram_tensor("kblk_d", [BATCH, P, UW], f32).ap()
        vblk_d = nc.dram_tensor("vblk_d", [BATCH, NW * P, UH * VW], f32).ap()
        xn_d = nc.dram_tensor("xn_d", [NT * P, D], f32).ap()
        xm_d = nc.dram_tensor("xm_d", [NT * P, D], f32).ap()
        res_d = nc.dram_tensor("res_d", [ROWS, D], f32).ap()
        out_d = A["out"]

        def sb(name, shape, dt=f32, stack=ctx):
            return stack.enter_context(nc.sbuf_tensor(name, shape, dt))

        ident = sb("ident", [P, P])
        iota_p = sb("iota_p", [P, P])
        iota_h = sb("iota_h", [P, SH])
        tok1 = sb("tok1", [P, NT])
        rank_e = sb("rank_e", [P, NT, E])
        step_k = sb("step_k", [P, E, E])
        tile_t = sb("tile_t", [P, ST + 1, E - 1])
        pad_row = sb("pad_row", [P, 1])
        ones = sb("ones", [P, P])
        upper = sb("upper", [P, P])
        onesb = sb("onesb", [P, P], bf16)
        upperb = sb("upperb", [P, P], bf16)
        eps = sb("eps", [P, 1])
        nege = sb("nege", [UH, UW])
        neg_head = sb("neg_head", [UH, UW], f32r)
        zeros = sb("zeros", [P, 2 * NW * UH * VW])

        ctxT = sb("ctxT", [P, KC, BATCH * NKEY])
        wkv = sb("wkv", [P, KC, 2 * DH])
        wraw = sb("wraw", [P, KC, D])
        wq_hi, wq_lo = sb("wq_hi", [P, KC, D], f32r), sb("wq_lo", [P, KC, D], f32r)
        wraw2 = sb("wraw2", [P, KC, D])
        wc_hi, wc_lo = sb("wc_hi", [P, KC, D], f32r), sb("wc_lo", [P, KC, D], f32r)
        rw = sb("rw", [P, 2, KC, E])
        rw_hi, rw_lo = sb("rw_hi", [P, 2, KC, E], f32r), sb("rw_lo", [P, 2, KC, E], f32r)
        bk = sb("bk", [P, KC])
        bq = sb("bq", [P, KC])
        bv = sb("bv", [1, D])
        g_hi, g_lo = sb("g_hi", [P, KC, BATCH, KP], f32r), sb("g_lo", [P, KC, BATCH, KP], f32r)
        c0 = sb("c0", [1, BATCH, KP])
        vp_hi, vp_lo = sb("vp_hi", [NKEY, BATCH, D], f32r), sb("vp_lo", [NKEY, BATCH, D], f32r)

        x_all = sb("x_all", [P, NT, D])
        lg = sb("lg", [P, NT, E])
        xn_cur = sb("xn_cur", [P, GT, D])
        t_hi, t_lo = sb("t_hi", [P, KC, GW], f32r), sb("t_lo", [P, KC, GW], f32r)
        st6 = sb("st6", [P, GT, 6])
        mv = sb("mv", [P, GT, 2])
        std = sb("std", [P, GT])
        rstd = sb("rstd", [P, GT])

        mx = sb("mx", [P, NT])
        pr = sb("pr", [P, NT, E])
        key = sb("key", [P, NT, E])
        top = sb("top", [P, 2, NT])
        oh = sb("oh", [P, 2, NT, E])
        msk = sb("msk", [P, NT, E], bf16)
        tmp3 = sb("tmp3", [P, NT, E])
        tot = sb("tot", [P, E, NT])
        cum = sb("cum", [P, E, NT])
        n_e = sb("n_e", [P, E])
        c_e = sb("c_e", [P, E])
        cb_e = sb("cb_e", [P, E])
        d_e = sb("d_e", [P, E])
        cmp_k = sb("cmp_k", [P, E, E])
        slot = sb("slot", [P, NT, E])
        slot2 = sb("slot2", [P, 2, NT])
        slot_i = sb("slot_i", [P, 2, NT], i32)
        sa_i = sb("sa_i", [P, 2, NT], i32)
        sb_i = sb("sb_i", [P, 2, NT], i32)
        sa_f = sb("sa_f", [P, 2, NT])
        sb_f = sb("sb_f", [P, 2, NT])
        cmp_t = sb("cmp_t", [P, ST + 1, E - 1])
        eid_f = sb("eid_f", [P, ST + 1])
        eid = [sb(f"eid{n}", [1, ST + 1], i32) for n in range(2)]
        ohb = sb("ohb", [P, 2, P], f32r)
        oha = sb("oha", [P, 2, 3, SH], f32r)
        inv = sb("inv", [P, 3, SH])
        gat_f = sb("gat_f", [P, SH])
        gat = [sb(f"gat{n}", [P, SH], i32) for n in range(2)]
        sca = [sb(f"sca{n}", [P, SH], i32) for n in range(2)]
        score = sb("score", [P, SH])
        s_hi, s_lo = sb("s_hi", [P, 2, NT], f32r), sb("s_lo", [P, 2, NT], f32r)
        wts = sb("wts", [P, 2, NT])
        wsum = sb("wsum", [P, E])
        mw_e = sb("mw_e", [P, E])
        mw_t = sb("mw_t", [P, ST + 1])
        cmp_m = sb("cmp_m", [P, ST + 1, E])
        iota_m = sb("iota_m", [P, ST + 1, E])

        zpad = sb("zpad", [P, BATCH])

        a0 = ExitStack()
        q_all = sb("q_all", [P, 4, NT * P], f32r, a0)
        a_all = sb("a_all", [P, NT, D], f32, a0)
        a_cur = sb("a_cur", [P, GT, D], f32, a0)
        qc = [sb(f"qc{u}", [P, 2, P], f32r, a0) for u in range(2)]
        pb_ = sb("pb_", [P, 2, UW], f32, a0)
        pt_hi, pt_lo = sb("pt_hi", [P, NW, P], f32r, a0), sb("pt_lo", [P, NW, P], f32r, a0)
        m_u = sb("m_u", [P, 2, UH], f32, a0)
        mT = sb("mT", [UH, 2, P], f32r, a0)
        rden = sb("rden", [P, 2, UH], f32, a0)
        kraw = sb("kraw", [P, BATCH, UW], f32, a0)
        k_hi, k_lo = sb("k_hi", [P, BATCH, UW], f32r, a0), sb("k_lo", [P, BATCH, UW], f32r, a0)
        vraw = sb("vraw", [P, BATCH, NW, UH * VW], f32, a0)
        v_hi, v_lo = (sb("v_hi", [P, BATCH, NW, UH * VW], f32r, a0), sb("v_lo", [P, BATCH, NW, UH * VW], f32r, a0))
        ksb = sb("ksb", [DH, BATCH, NKEY], f32, a0)
        vsb = sb("vsb", [NKEY, BATCH, VW], f32, a0)
        w1qT = sb("w1qT", [P, KC, D], f32, a0)
        w1k = sb("w1k", [P, KC, D], f32, a0)
        w1v = sb("w1v", [P, KC, D], f32, a0)
        kpT = sb("kpT", [P, KC, BATCH * NKEY], f32, a0)
        a0.close()
        xr = sb("xr", [P, 2, D])
        xe_hi, xe_lo = sb("xe_hi", [P, KC, FT], f32r), sb("xe_lo", [P, KC, FT], f32r)
        sg = sb("sg", [P, 2, 512])
        hf = sb("hf", [P, 2, 512])
        h_hi, h_lo = sb("h_hi", [P, G0, 2, FT], f32r), sb("h_lo", [P, G0, 2, FT], f32r)
        ye = sb("ye", [P, 2, D])
        gidx, sidx = sb("gidx", [P, 2], i32), sb("sidx", [P, 2], i32)
        wr = sb("wr", [P, NB0, WB])

        t1 = ExitStack()
        pt1_hi, pt1_lo = sb("pt1_hi", [NKEY, GT, P], f32r, t1), sb("pt1_lo", [NKEY, GT, P], f32r, t1)
        p1 = sb("p1", [P, GT, KP], f32, t1)
        m1 = sb("m1", [P, GT], f32, t1)
        den1 = sb("den1", [P, GT], f32, t1)
        ws_hi, ws_lo = sb("ws_hi", [P, 3, KC, D], f32r, t1), sb("ws_lo", [P, 3, KC, D], f32r, t1)
        sgs = sb("sgs", [P, KC, GW], f32, t1)
        hfs = sb("hfs", [P, KC, GW], f32, t1)
        hs_hi, hs_lo = sb("hs_hi", [P, KC, GW], f32r, t1), sb("hs_lo", [P, KC, GW], f32r, t1)
        t1.close()
        w_hi, w_lo = sb("w_hi", [P, NB0, WB], f32r), sb("w_lo", [P, NB0, WB], f32r)
        wsr = wr[:, 0:2, :].rearrange("p b n -> p (b n)")[:, 0:3 * KC * D].rearrange("p (w c n) -> p w c n", w=3, c=KC)

        ps = ctx.enter_context(nc.psum_tensor("ps", [P, 8, 512], f32))

        x_in, c_in, w_in0, l1_in, ws_in = sem("x_in"), sem("c_in"), sem("w_in0"), sem("l1_in"), sem("ws_in")
        zeros_ok, const_ok = sem("zeros_ok"), sem("const_ok")
        pool_ch, dve_ch = sem("pool_ch"), sem("dve_ch")
        zero_st, pad_st, kv_mm, kv_sb, kv_st, kv_ld, kv_hi, kv_lo = (sem(n) for n in (
            "zero_st", "pad_st", "kv_mm", "kv_sb", "kv_st", "kv_ld", "kv_hi", "kv_lo"))
        ws0_hi, ws0_lo = sem("ws0_hi"), sem("ws0_lo")
        kp_mm, kp_sb, g_mm, g_hs, g_ls, v1_mm, v1_hs, v1_ls = (sem(n) for n in (
            "kp_mm", "kp_sb", "g_mm", "g_hs", "g_ls", "v1_mm", "v1_hs", "v1_ls"))

        def norm_sems(n):
            return {k: sem(f"n{n}_{k}") for k in ("var", "std", "xn", "mm", "hi", "lo")}

        n0, n1, n2, n3 = (norm_sems(n) for n in range(4))
        q_mm, q_hi, q_lo = sem("q_mm"), sem("q_hi"), sem("q_lo")
        q_cp, s_mm, s_max, pt0_mm, pt1_mm, mt_mm, mt_ok, pt_hs, pt_ls, sh_mm, s_exp, pv_mm, a_ok = (sem(n) for n in (
            "q_cp", "s_mm", "s_max", "pt0_mm", "pt1_mm", "mt_mm", "mt_ok", "pt_hs", "pt_ls", "sh_mm", "s_exp",
            "pv_mm", "a_ok"))
        ac_ok, at_mm, at_hi, at_lo, cc_mm, x1_ok, x1_st, xn_st, xm_st = (sem(n) for n in (
            "ac_ok", "at_mm", "at_hi", "at_lo", "cc_mm", "x1_ok", "x1_st", "xn_st", "xm_st"))
        lg_mm, lg_ok = [sem(f"lg_mm{n}") for n in range(2)], sem("lg_ok")

        def route_sems(n):
            return {k: sem(f"r{n}_{k}") for k in ("sub", "exp", "msk", "mm", "one", "inv", "tab")}

        r0, r1 = route_sems(0), route_sems(1)
        ws_ok, ws_mm = sem("ws_ok"), sem("ws_mm")
        x2_in = sem("x2_in")
        l_mm, l_max, l_exp, p1_mm, p1_hs, p1_ls, o1_mm, x3_ok = (sem(n) for n in (
            "l_mm", "l_max", "l_exp", "p1_mm", "p1_hs", "p1_ls", "o1_mm", "x3_ok"))
        sgu_mm, ss_ok, shf_ok, sh_hi, sh_lo, sd_mm, so_ok, so_st, wss_hi, wss_lo = (sem(n) for n in (
            "sgu_mm", "ss_ok", "shf_ok", "sh_hi", "sh_lo", "sd_mm", "so_ok", "so_st", "wss_hi", "wss_lo"))

        def ffn_sems(n, blocks):
            f = {k: sem(f"f{n}_{k}") for k in ("idx", "x_in", "w_hi", "w_lo", "xt_mm", "xt_hi", "xt_lo", "gu_mm",
                                               "silu", "h_mul", "h_hi", "h_lo", "d_mm", "y_ok", "y_st")}
            f["w_in"] = [sem(f"f{n}_w_in{b}") for b in range(blocks)]
            return f

        f0, f1 = ffn_sems(0, NB0), ffn_sems(1, 2)
        x_sc = sem("x_sc")
        wd_hi = sem("wd_hi")
        passed = sem("passed")
        block = ctx.enter_context(nc.Block())

        def mm(out, w, x, start, stop):
            return nc.tensor.matmul(out, w, x, start=start, stop=stop, skip_group_check=True)

        def mm3(out, pairs):
            for n, (wh, wl, xh, xl) in enumerate(pairs):
                mm(out, wh, xh, n == 0, False)
                mm(out, wh, xl, False, False)
                last = mm(out, wl, xh, False, n == len(pairs) - 1)
            return last

        def win(j):
            return min(P * j, UW - P)

        def head(j):
            return min(win(j) // NKEY, UH - WINH)

        def group(t, g):
            return t[:, ds(g * GT, GT), :]

        def rows(t, g):
            return t[ds(g * GW, GW), :].rearrange("(t p) d -> p t d", p=P)

        def alone(engine):
            engine.sem_inc(passed, 1)

        @block.sync
        def _(sp):
            for g in range(NG):
                sp.dma_start(x_all[:, g * GT:(g + 1) * GT, :], A["x"][:, g * GT:(g + 1) * GT, :]).then_inc(x_in, 16)
                if g == 0:
                    sp.dma_start(ctxT[:, :, :], A["ctxT"]).then_inc(c_in, 16)
                    sp.dma_start(wkv[:, :, :], A["wkv"]).then_inc(c_in, 16)
                    sp.dma_start(wraw[:, :, :], A["wq"]).then_inc(w_in0, 16)
                    sp.dma_start(wraw2[:, :, :], A["wc"]).then_inc(w_in0, 16)
                    sp.dma_start(rw[:, :, :, :], A["rw"]).then_inc(w_in0, 16)
            sp.wait_ge(zeros_ok, 1)
            sp.dma_start(kblk_d.rearrange("b p n -> p b n"),
                         zeros[:, 0:BATCH * UW].rearrange("p (b n) -> p b n", b=BATCH)).then_inc(zero_st, 16)
            sp.dma_start(vblk_d.rearrange("b (j p) n -> p (b j) n", p=P),
                         zeros[:, :].rearrange("p (b n) -> p b n", n=UH * VW)).then_inc(zero_st, 16)
            sp.dma_start(res_d[NT * P:ROWS, :], zeros[:, 0:D]).then_inc(pad_st, 16)
            sp.dma_start(out_d[NT * P:ROWS, :], zeros[:, 0:D]).then_inc(pad_st, 16)
            for dst, name in ((w1k, "w1k"), (w1qT, "w1qT"), (w1v, "w1v")):
                sp.dma_start(dst[:, :, :], A[name]).then_inc(l1_in, 16)
            sp.dma_start(bk[:, :], A["bk"]).then_inc(l1_in, 16)
            sp.dma_start(bq[:, :], A["bq"]).then_inc(l1_in, 16)
            sp.dma_start(bv[:, :], A["bv"]).then_inc(l1_in, 16)
            sp.wait_ge(zero_st, 32)
            sp.wait_ge(kv_sb, 2)
            cut = 4 * P - 6 * NKEY
            skip = NW * P - UW
            for b in range(BATCH):
                kd = bass.AP(tensor=kblk_d.tensor, offset=b * P * UW, ap=[[UW, DH], [DH * UW + NKEY, UH], [1, NKEY]])
                sp.dma_start(kd, ksb[:, b:b + 1, :].to_broadcast([DH, UH, NKEY])).then_inc(kv_st, 16)
                base, w = b * NW * P * UH * VW, UH * VW
                vd = bass.AP(tensor=vblk_d.tensor, offset=base, ap=[[w, NKEY], [NKEY * w + VW, 6], [1, VW]])
                sp.dma_start(vd, vsb[:, b:b + 1, :].to_broadcast([NKEY, 6, VW])).then_inc(kv_st, 16)
                for head_, k0, k1, up in ((6, 0, cut, 0), (6, cut, NKEY, skip), (7, 0, NKEY, skip)):
                    r = head_ * NKEY + up
                    sp.dma_start(vblk_d[b, r + k0:r + k1, head_ * VW:(head_ + 1) * VW],
                                 vsb[k0:k1, b, :]).then_inc(kv_st, 16)
            sp.wait_ge(kv_st, 16 * 5 * BATCH)
            sp.dma_start(kraw[:, :, :], kblk_d.rearrange("b p n -> p b n")).then_inc(kv_ld, 16)
            sp.dma_start(vraw[:, :, :, :], vblk_d.rearrange("b (j p) n -> p b j n", p=P)).then_inc(kv_ld, 16)

            with sp.Fori(0, NG) as g:
                sp.wait_ge(x1_ok, 2 * g + 2)
                sp.dma_start(rows(res_d, g), group(x_all, g)).then_inc(x1_st, 16)
                sp.wait_ge(n1["xn"], GT * (g + 1))
                sp.dma_start(rows(xn_d, g), xn_cur[:, :, :]).then_inc(xn_st, 16)

            sp.wait_ge(r0["tab"], 1)

            def load0(t, first=False):
                e = sp.value_load(eid[0][0:1, ds(t, 1)], min_val=0, max_val=E - 1)
                for b in range(NB0):
                    if not first:
                        sp.wait_ge(f0["w_lo"], (t - 1) * NB0 + b + 1)
                    sp.dma_start(wr[:, b, :], A["w0"][ds(e * (NB0 * P) + b * P, P), :]).then_inc(f0["w_in"][b], 16)

            load0(0, True)
            with sp.Fori(1, ST) as t:
                load0(t)

            sp.wait_ge(f0["w_lo"], NB0 * ST)
            sp.dma_start(wsr, A["ws"]).then_inc(ws_in, 16)
            sp.wait_ge(f0["y_st"], 32 * ST)
            with sp.Fori(0, NG) as g:
                sp.wait_ge(x2_in, 16 * g)
                sp.dma_start(group(x_all, g), rows(res_d, g)).then_inc(x2_in, 16)
            with sp.Fori(0, NG) as g:
                sp.wait_ge(n3["xn"], GT * (g + 1))
                sp.dma_start(rows(xm_d, g), xn_cur[:, :, :]).then_inc(xm_st, 16)
                sp.wait_ge(so_ok, 2 * g + 2)
                sp.dma_start(rows(out_d, g), group(x_all, g)).then_inc(so_st, 16)

            sp.wait_ge(r1["tab"], 1)

            def load1(t, first=False):
                e = sp.value_load(eid[1][0:1, ds(t, 1)], min_val=0, max_val=E - 1)
                for b, (name, n) in enumerate((("w1gu", WB), ("w1d", WB // 2))):
                    if not first:
                        sp.wait_ge(f1["w_lo"], (t - 1) * 2 + b + 1)
                    sp.dma_start(wr[:, b, 0:n], A[name][ds(e * P, P), :]).then_inc(f1["w_in"][b], 16)

            load1(0, True)
            with sp.Fori(1, ST) as t:
                load1(t)
            for s, v in ((f1["y_st"], 32 * ST), (so_st, 16 * NG), (pad_st, 32), (xm_st, 16 * NG), (xn_st, 16 * NG),
                         (x1_st, 16 * NG)):
                sp.wait_ge(s, v)

        @block.gpsimd
        def _(pool):
            g = nc.gpsimd
            ch = Count(pool_ch)

            def link(ins):
                ins.then_inc(ch.sem, 1)
                pool.wait_ge(ch.sem, ch.up())

            g.memset(zeros[:, :], 0.0).then_inc(zeros_ok, 1)
            link(g.memset(ones[:, :], 1.0))
            link(g.memset(nege[:, :], -1.0))
            g.affine_select(out=ident[:, :], in_=ones[:, :], compare_op=ALU.is_equal, fill=0.0, base=0,
                            pattern=[[1, P]], channel_multiplier=-1)
            link(g.affine_select(out=upper[:, :], in_=ones[:, :], compare_op=ALU.is_gt, fill=0.0, base=0,
                                 pattern=[[1, P]], channel_multiplier=-1))
            link(g.affine_select(out=nege[:, :], in_=nege[:, :], compare_op=ALU.is_ge, fill=0.0, base=0,
                                 pattern=[[1, UW]], channel_multiplier=-NKEY))
            link(g.affine_select(out=nege[:, :], in_=nege[:, :], compare_op=ALU.is_gt, fill=0.0, base=NKEY,
                                 pattern=[[-1, UW]], channel_multiplier=NKEY))
            g.tensor_copy(neg_head[:, :], nege[:, :])
            g.tensor_copy(onesb[:, :], ones[:, :])
            g.tensor_copy(upperb[:, :], upper[:, :])
            g.memset(eps[:, :], EPS)
            io = dict(allow_small_or_imprecise_dtypes=True)
            g.iota(iota_p[:, :], pattern=[[1, P]], base=0, channel_multiplier=0, **io)
            g.iota(iota_h[:, :], pattern=[[1, SH]], base=0, channel_multiplier=0, **io)
            g.iota(tok1[:, :], pattern=[[P, NT]], base=1, channel_multiplier=1, **io)
            g.iota(rank_e[:, :, :], pattern=[[0, NT], [-1, E]], base=E, channel_multiplier=0, **io)
            g.iota(step_k[:, :, :], pattern=[[0, E], [FT, E]], base=0, channel_multiplier=0, **io)
            g.iota(tile_t[:, :, :], pattern=[[1, ST + 1], [0, E - 1]], base=0, channel_multiplier=0, **io)
            g.iota(iota_m[:, :, :], pattern=[[0, ST + 1], [1, E]], base=0, channel_multiplier=0, **io)
            g.iota(pad_row[:, :], pattern=[[0, 1]], base=NT * P, channel_multiplier=1, **io).then_inc(const_ok, 1)

            def copy_q(i, u, first=False):
                if not first:
                    pool.wait_ge(s_mm, 2 * i + u - 1)
                g.tensor_copy(qc[u][:, :, :], q_all[:, 2 * u:2 * u + 2, ds(i * P, P)]).then_inc(q_cp, 1)

            pool.wait_ge(q_lo, 2 * NG)
            copy_q(0, 0, True)
            copy_q(0, 1, True)
            with pool.Fori(1, NT) as i:
                copy_q(i, 0)
                copy_q(i, 1)

            pool.wait_ge(a_ok, 2 * NT)
            with pool.Fori(0, NG) as gr:
                pool.wait_ge(at_mm, 2 * gr)
                g.tensor_copy(a_cur[:, :, :], group(a_all, gr)).then_inc(ac_ok, 1)

            def expert_rows(f, n, src, dst, ahead):
                idx = Count(f["idx"])

                def fetch(t):
                    pool.wait_ge(f["x_in"], 32 * t)
                    pool.wait_ge(f["xt_mm"], t)
                    g.tensor_copy(gidx[:, :], gat[n][:, ds(2 * t, 2)]).then_inc(idx.sem, 1)
                    pool.wait_ge(idx.sem, idx.up())
                    alone(pool)
                    for half in range(2):
                        pool.indirect_dma_start(xr[:, half, :], None, src,
                                                bass.IndirectOffsetOnAxis(ap=gidx[:, half:half + 1], axis=0)
                                                ).then_inc(f["x_in"], 16)

                def add(t):
                    pool.wait_ge(f["y_st"], 32 * t)
                    g.tensor_copy(sidx[:, :], sca[n][:, ds(2 * t, 2)]).then_inc(idx.sem, 1)
                    pool.wait_ge(idx.sem, idx.up())
                    alone(pool)
                    for half in range(2):
                        pool.wait_ge(f["y_st"], 32 * t + 16 * half)
                        pool.wait_ge(f["y_ok"], 2 * t + half + 1)
                        alone(pool)
                        pool.indirect_dma_start(dst, bass.IndirectOffsetOnAxis(ap=sidx[:, half:half + 1], axis=0),
                                                ye[:, half, :], None, compute_op=ALU.add).then_inc(f["y_st"], 16)

                for t in range(ahead):
                    fetch(t)
                with pool.Fori(0, ST - ahead) as t:
                    idx.enter(t, 2)
                    fetch(t + ahead)
                    add(t)
                    idx.leave(ST - ahead)
                for t in range(ST - ahead, ST):
                    add(t)

            pool.wait_ge(r0["tab"], 1)
            pool.wait_ge(xn_st, 16 * NG)
            pool.wait_ge(x1_st, 16 * NG)
            pool.wait_ge(pad_st, 32)
            expert_rows(f0, 0, xn_d, res_d, 1)
            pool.wait_ge(r1["tab"], 1)
            pool.wait_ge(xm_st, 16 * NG)
            pool.wait_ge(so_st, 16 * NG)
            expert_rows(f1, 1, xm_d, out_d, 2)

        @block.scalar
        def _(act):
            s = nc.scalar

            def copy(o, i):
                return s.activation(o, i, ACT.Copy)

            def std_of(n, g):
                act.wait_ge(n["var"], GT * (g + 1))
                s.activation(std[:, :], mv[:, :, 1], ACT.Sqrt, bias=eps[:, :]).then_inc(n["std"], 1)

            def split_hi(n, g, b0):
                for c in range(KC):
                    act.wait_ge(n["mm"], KC * g + c + 1)
                    copy(t_hi[:, c, :], ps[:, b0 + c, :]).then_inc(n["hi"], 1)

            act.wait_ge(w_in0, 48)
            copy(wq_hi[:, :, :], wraw[:, :, :]).then_inc(ws0_hi, 1)
            copy(wc_hi[:, :, :], wraw2[:, :, :]).then_inc(ws0_hi, 1)
            copy(rw_hi[:, :, :, :], rw[:, :, :, :]).then_inc(ws0_hi, 1)
            act.wait_ge(const_ok, 1)
            with act.Fori(0, NG) as g:
                std_of(n0, g)
                split_hi(n0, g, 0)
                for c in range(KC):
                    act.wait_ge(q_mm, KC * g + c + 1)
                    alone(act)
                    copy(q_all[:, 2 * c, ds(g * GW, GW)], ps[:, 2 + c, :]).then_inc(q_hi, 1)

            act.wait_ge(kv_ld, 32)
            copy(k_hi[:, :, :], kraw[:, :, :]).then_inc(kv_hi, 1)
            copy(v_hi[:, :, :, :], vraw[:, :, :, :]).then_inc(kv_hi, 1)
            for c in range(KC):
                act.wait_ge(g_mm, KC)
                copy(g_hi[:, c, :, 0:NKEY], ps[:, 1 + c, 0:BATCH * NKEY].rearrange("p (b k) -> p b k", b=BATCH)
                     ).then_inc(g_hs, 1)
            act.wait_ge(v1_mm, BATCH)
            for b in range(BATCH):
                copy(vp_hi[:, b, :], ps[0:NKEY, 3 + b, 0:D]).then_inc(v1_hs, 1)

            def step(n, u, prev=True, cur=True):
                if prev:
                    act.wait_ge(pt0_mm, n)
                    copy(pt_hi[:, 0:3, :], ps[:, 4, 0:3 * P]).then_inc(pt_hs, 1)
                if cur:
                    act.wait_ge(mt_mm, n + 1)
                    copy(mT[:, u, :], ps[0:UH, 5, 3 * P:4 * P]).then_inc(mt_ok, 1)
                if prev:
                    act.wait_ge(pt1_mm, n)
                    copy(pt_hi[:, 3:5, :], ps[:, 5, 0:2 * P]).then_inc(pt_hs, 1)
                if cur:
                    act.wait_ge(sh_mm, n + 1)
                    s.activation(pb_[:, u, :].rearrange("p (a n) -> p a n", a=2),
                                 ps[:, 2 * u:2 * u + 2, 0:HB], ACT.Exp, scale=DH ** -0.5).then_inc(s_exp, 1)

            step(0, 0, prev=False)
            step(1, 1)
            with act.Fori(1, NT) as i:
                step(2 * i, 0)
                step(2 * i + 1, 1)
            step(2 * NT, 0, cur=False)

            with act.Fori(0, NG) as g:
                for c in range(KC):
                    act.wait_ge(at_mm, KC * g + c + 1)
                    copy(t_hi[:, c, :], ps[:, c, :]).then_inc(at_hi, 1)
                std_of(n1, g)
                split_hi(n1, g, 4)

            def route(r):
                act.wait_ge(r["sub"], 1)
                s.activation(pr[:, :, :], pr[:, :, :], ACT.Exp).then_inc(r["exp"], 1)

            route(r0)

            def w0_hi(t, b):
                act.wait_ge(f0["w_in"][b], 16 * (t + 1))
                copy(w_hi[:, b, :], wr[:, b, :]).then_inc(f0["w_hi"], 1)

            def x0_hi(t, f=f0):
                act.wait_ge(f["xt_mm"], t + 1)
                copy(xe_hi[:, :, :].rearrange("p c n -> p (c n)"), ps[:, 6, :]).then_inc(f["xt_hi"], 1)

            def tile0(t, more=True):
                for q in range(G0):
                    act.wait_ge(f0["gu_mm"], G0 * t + q + 1)
                    s.activation(sg[:, q % 2, :], ps[:, q % 2, :], ACT.Silu).then_inc(f0["silu"], 1)
                    if more and q < G0 - 1:
                        w0_hi(t + 1, q)
                    act.wait_ge(f0["h_mul"], G0 * t + q + 1)
                    copy(h_hi[:, q, :, :].rearrange("p c n -> p (c n)"), hf[:, q % 2, :]).then_inc(f0["h_hi"], 1)
                if more:
                    w0_hi(t + 1, G0 - 1)
                    x0_hi(t + 1)
                act.wait_ge(f0["y_st"], 32 * t)
                for half in range(2):
                    act.wait_ge(f0["d_mm"], 2 * t + half + 1)
                    alone(act)
                    s.activation(ye[:, half, :], ps[:, 4 + half, 0:D], ACT.Copy,
                                 scale=mw_t[:, ds(t, 1)]).then_inc(f0["y_ok"], 1)
                if more:
                    w0_hi(t + 1, G0)
                    w0_hi(t + 1, G0 + 1)

            for b in range(NB0):
                w0_hi(0, b)
            x0_hi(0)
            with act.Fori(0, ST - 1) as t:
                tile0(t)
            tile0(ST - 1, more=False)

            act.wait_ge(ws_in, 16)
            copy(ws_hi[:, :, :, :], wsr).then_inc(wss_hi, 1)
            with act.Fori(0, NG) as g:
                std_of(n2, g)
                split_hi(n2, g, 0)
                act.wait_ge(l_max, g + 1)
                for j in range(GT):
                    s.activation(p1[:, j, 0:NKEY], ps[:, 2, j * KP:j * KP + NKEY], ACT.Exp, bias=m1[:, j:j + 1],
                                 scale=D ** -0.5, accum_out=den1[:, j:j + 1]).then_inc(l_exp, 1)
                act.wait_ge(p1_mm, g + 1)
                copy(pt1_hi[:, :, :].rearrange("p c n -> p (c n)"), ps[0:NKEY, 3, :]).then_inc(p1_hs, 1)
                std_of(n3, g)
                split_hi(n3, g, 0)
                for c in range(KC):
                    act.wait_ge(sgu_mm, KC * g + c + 1)
                    s.activation(sgs[:, c, :], ps[:, 4 + 2 * c, :], ACT.Silu).then_inc(ss_ok, 1)
                for c in range(KC):
                    act.wait_ge(shf_ok, KC * g + c + 1)
                    copy(hs_hi[:, c, :], hfs[:, c, :]).then_inc(sh_hi, 1)
            route(r1)

            def w1_hi(t, b):
                act.wait_ge(f1["w_in"][b], 16 * (t + 1))
                n = WB if b == 0 else WB // 2
                copy(w_hi[:, b, 0:n], wr[:, b, 0:n]).then_inc((f1["w_hi"], wd_hi)[b], 1)

            def y1(t):
                act.wait_ge(f1["y_st"], 32 * t)
                for half in range(2):
                    act.wait_ge(f1["d_mm"], 2 * t + half + 1)
                    copy(ye[:, half, :], ps[:, 4 + half, 0:D]).then_inc(f1["y_ok"], 1)

            def tile1(t, prev=True, more=True):
                act.wait_ge(f1["gu_mm"], t + 1)
                s.activation(sg[:, 0, :], ps[:, 0, :], ACT.Silu).then_inc(f1["silu"], 1)
                if more:
                    w1_hi(t + 1, 0)
                if prev:
                    y1(t - 1)
                act.wait_ge(f1["h_mul"], t + 1)
                copy(h_hi[:, 0, :, :].rearrange("p c n -> p (c n)"), hf[:, 0, :]).then_inc(f1["h_hi"], 1)
                w1_hi(t, 1)
                if more:
                    x0_hi(t + 1, f1)

            w1_hi(0, 0)
            x0_hi(0, f1)
            tile1(0, prev=False)
            with act.Fori(1, ST - 1) as t:
                tile1(t)
            tile1(ST - 1, more=False)
            y1(ST - 1)

        @block.vector
        def _(dve):
            v = nc.vector
            ch = Count(dve_ch)

            def link(ins):
                ins.then_inc(ch.sem, 1)
                dve.wait_ge(ch.sem, ch.up())

            def sub(o, a, b):
                return v.tensor_tensor(o, a, b, ALU.subtract)

            def normalise(n, g, src):
                alone(dve)
                for j in range(GT):
                    ins = v.bn_stats(st6[:, j, :], src(j))
                link(ins)
                alone(dve)
                for j in range(GT):
                    v.bn_aggr(mv[:, j, :], st6[:, j, :]).then_inc(n["var"], 1)
                dve.wait_ge(n["std"], g + 1)
                link(v.reciprocal(rstd[:, :], std[:, :]))
                for j in range(GT):
                    v.tensor_scalar(xn_cur[:, j, :], src(j), mv[:, j, 0:1], rstd[:, j:j + 1],
                                    ALU.subtract, ALU.mult).then_inc(n["xn"], 1)

            def split_lo(n, g, b0):
                for c in range(KC):
                    dve.wait_ge(n["hi"], KC * g + c + 1)
                    sub(t_lo[:, c, :], ps[:, b0 + c, :], t_hi[:, c, :]).then_inc(n["lo"], 1)

            def tile_of(g):
                return lambda j: x_all[:, ds(g * GT + j, 1), :].rearrange("p a d -> p (a d)")

            v.memset(vsb[:, :, :], 0.0)
            v.memset(c0[:, :, :], 0.0)
            link(v.memset(zpad[:, :], 0.0))
            link(v.memset(vsb[:, :, DH:DH + 1], 1.0))
            dve.wait_ge(kv_mm, 1)
            v.tensor_copy(ksb[:, :, :], ps[0:DH, 0, 0:BATCH * NKEY].rearrange("p (b k) -> p b k", b=BATCH)).then_inc(kv_sb, 1)
            v.tensor_copy(vsb[:, :, 0:DH], ps[0:NKEY, 0, 2 * P:2 * P + BATCH * DH].rearrange("p (b k) -> p b k", b=BATCH)
                          ).then_inc(kv_sb, 1)
            dve.wait_ge(ws0_hi, 3)
            sub(wq_lo[:, :, :], wraw[:, :, :], wq_hi[:, :, :]).then_inc(ws0_lo, 1)
            sub(wc_lo[:, :, :], wraw2[:, :, :], wc_hi[:, :, :]).then_inc(ws0_lo, 1)
            sub(rw_lo[:, :, :, :], rw[:, :, :, :], rw_hi[:, :, :, :]).then_inc(ws0_lo, 1)

            dve.wait_ge(x_in, 16 * NG)
            with dve.Fori(0, NG) as g:
                ch.enter(g, 2)
                normalise(n0, g, tile_of(g))
                split_lo(n0, g, 0)
                for c in range(KC):
                    dve.wait_ge(q_hi, KC * g + c + 1)
                    sub(q_all[:, 2 * c + 1, ds(g * GW, GW)], ps[:, 2 + c, :], q_all[:, 2 * c, ds(g * GW, GW)]
                        ).then_inc(q_lo, 1)
                ch.leave(NG)
            dve.wait_ge(kv_hi, 2)
            sub(k_lo[:, :, :], kraw[:, :, :], k_hi[:, :, :]).then_inc(kv_lo, 1)
            sub(v_lo[:, :, :, :], vraw[:, :, :, :], v_hi[:, :, :, :]).then_inc(kv_lo, 1)
            for c in range(KC):
                dve.wait_ge(kp_mm, KC)
                v.tensor_scalar(kpT[:, c, :], ps[:, 4 + c, 0:BATCH * NKEY], bk[:, c:c + 1], None, ALU.add).then_inc(kp_sb, 1)
            for c in range(KC):
                dve.wait_ge(g_hs, KC)
                sub(g_lo[:, c, :, 0:NKEY], ps[:, 1 + c, 0:BATCH * NKEY].rearrange("p (b k) -> p b k", b=BATCH),
                    g_hi[:, c, :, 0:NKEY])
                v.tensor_copy(g_lo[:, c, :, NKEY:KP], zpad[:, 0:BATCH].rearrange("p (b k) -> p b k", b=BATCH))
                v.tensor_copy(g_hi[:, c, :, NKEY:KP], zpad[:, 0:BATCH].rearrange("p (b k) -> p b k", b=BATCH)).then_inc(g_ls, 1)
            v.tensor_copy(c0[:, :, 0:NKEY], ps[0:1, 0, 0:BATCH * NKEY].rearrange("p (b k) -> p b k", b=BATCH)).then_inc(g_ls, 1)
            dve.wait_ge(v1_hs, BATCH)
            for b in range(BATCH):
                sub(vp_lo[:, b, :], ps[0:NKEY, 3 + b, 0:D], vp_hi[:, b, :]).then_inc(v1_ls, 1)

            def top_of(n, u):
                dve.wait_ge(s_mm, n + 1)
                v.tensor_reduce(m_u[:, u, :].rearrange("p (a h) -> p a h", a=2),
                                ps[:, 2 * u:2 * u + 2, 0:HB].rearrange("p a (h k) -> p a h k", k=NKEY),
                                AX.X, ALU.max).then_inc(s_max, 1)

            def step(n, u, i1, prev=True, nxt=True):
                w = 1 - u
                if prev:
                    dve.wait_ge(pt_hs, 2 * n - 1)
                    sub(pt_lo[:, 0:3, :], ps[:, 4, 0:3 * P].rearrange("p (c n) -> p c n", c=3), pt_hi[:, 0:3, :]).then_inc(pt_ls, 1)
                    dve.wait_ge(pt_hs, 2 * n)
                    sub(pt_lo[:, 3:5, :], ps[:, 5, 0:2 * P].rearrange("p (c n) -> p c n", c=2), pt_hi[:, 3:5, :]).then_inc(pt_ls, 1)
                if nxt:
                    top_of(n + 1, w)
                if prev:
                    dve.wait_ge(pv_mm, n)
                    o = ps[:, 6 + w, 0:UH * VW].rearrange("p (h c) -> p h c", c=VW)
                    link(v.reciprocal(rden[:, w, :], o[:, :, DH:DH + 1].rearrange("p h c -> p (h c)")))
                    v.tensor_tensor(a_all[:, ds(i1, 1), w * P:(w + 1) * P].rearrange("p a (h c) -> p (a h) c", c=DH),
                                    o[:, :, 0:DH], rden[:, w, :].rearrange("p (h o) -> p h o", o=1).to_broadcast([P, UH, DH]),
                                    ALU.mult).then_inc(a_ok, 1)

            top_of(0, 0)
            step(0, 0, 0, prev=False)
            step(1, 1, 0)
            with dve.Fori(1, NT - 1) as i:
                ch.enter(i, 2, 1)
                step(2 * i, 0, i - 1)
                step(2 * i + 1, 1, i)
                ch.leave(NT - 2)
            step(2 * NT - 2, 0, NT - 2)
            step(2 * NT - 1, 1, NT - 1, nxt=False)
            step(2 * NT, 0, NT - 1, nxt=False)

            with dve.Fori(0, NG) as g:
                ch.enter(g, 2)
                for c in range(KC):
                    dve.wait_ge(at_hi, KC * g + c + 1)
                    sub(t_lo[:, c, :], ps[:, c, :], t_hi[:, c, :]).then_inc(at_lo, 1)
                for h in range(2):
                    dve.wait_ge(cc_mm, 2 * g + h + 1)
                    x2t = x_all[:, ds(g * GT + 2 * h, 2), :]
                    v.tensor_tensor(x2t, ps[:, 2 + h, :].rearrange("p (t d) -> p t d", t=2), x2t, ALU.add).then_inc(x1_ok, 1)
                dve.wait_ge(x1_ok, 2 * g + 2)
                dve.wait_ge(xn_st, 16 * g)
                normalise(n1, g, tile_of(g))
                split_lo(n1, g, 4)
                dve.wait_ge(lg_mm[0], g + 1)
                v.tensor_copy(group(lg, g), ps[:, 6, 0:GT * E].rearrange("p (t e) -> p t e", e=E)).then_inc(lg_ok, 1)
                ch.leave(NG)

            def b_tile(a, n=E):
                return a.rearrange("p (t o) -> p t o", o=1).to_broadcast([P, a.shape[1], n])

            def route(n, r):
                link(v.tensor_reduce(mx[:, :], lg[:, :, :], AX.X, ALU.max))
                sub(pr[:, :, :], lg[:, :, :], b_tile(mx[:, :])).then_inc(r["sub"], 1)
                dve.wait_ge(r["exp"], 1)
                link(v.tensor_reduce(mx[:, :], pr[:, :, :], AX.X, ALU.add))
                link(v.reciprocal(mx[:, :], mx[:, :]))
                link(v.tensor_tensor(pr[:, :, :], pr[:, :, :], b_tile(mx[:, :]), ALU.mult))
                for c in range(2):
                    link(v.tensor_reduce(top[:, c, :], pr[:, :, :], AX.X, ALU.max))
                    link(v.tensor_tensor(key[:, :, :], pr[:, :, :], b_tile(top[:, c, :]), ALU.is_equal))
                    link(v.tensor_tensor(key[:, :, :], key[:, :, :], rank_e[:, :, :], ALU.mult))
                    link(v.tensor_reduce(mx[:, :], key[:, :, :], AX.X, ALU.max))
                    link(v.tensor_tensor(oh[:, c, :, :], key[:, :, :], b_tile(mx[:, :]), ALU.is_equal))
                    if c == 0:
                        link(v.scalar_tensor_tensor(pr[:, :, :], oh[:, 0, :, :], -2.0, pr[:, :, :], ALU.mult, ALU.add))
                v.tensor_tensor(msk[:, :, :], oh[:, 0, :, :], oh[:, 1, :, :], ALU.add).then_inc(r["msk"], 1)
                if n == 0:
                    link(v.tensor_tensor(mx[:, :], top[:, 0, :], top[:, 1, :], ALU.add))
                    link(v.reciprocal(mx[:, :], mx[:, :]))
                    for c in range(2):
                        link(v.tensor_tensor(wts[:, c, :], top[:, c, :], mx[:, :], ALU.mult))
                    link(v.tensor_tensor(key[:, :, :], oh[:, 0, :, :], b_tile(wts[:, 0, :]), ALU.mult))
                    link(v.tensor_tensor(tmp3[:, :, :], oh[:, 1, :, :], b_tile(wts[:, 1, :]), ALU.mult))
                    link(v.tensor_tensor(key[:, :, :], key[:, :, :], tmp3[:, :, :], ALU.add))
                    v.tensor_reduce(wsum[:, :], key[:, :, :].rearrange("p t e -> p e t"), AX.X, ALU.add).then_inc(ws_ok, 1)
                else:
                    link(v.tensor_copy(s_hi[:, :, :], top[:, :, :]))
                    link(sub(s_lo[:, :, :], top[:, :, :], s_hi[:, :, :]))
                dve.wait_ge(r["mm"], 1)
                link(v.tensor_copy(tot[:, :, :], ps[:, 0, P:2 * P].rearrange("p (t e) -> p e t", e=E)))
                link(v.tensor_tensor_scan(cum[:, :, :].rearrange("p e t -> p (e t)"), ones[:, :],
                                          tot[:, :, :].rearrange("p e t -> p (e t)"), 0.0, ALU.mult, ALU.add))
                link(v.tensor_reduce(n_e[:, :], tot[:, :, :], AX.X, ALU.add))
                link(v.tensor_tensor(cmp_k[:, :, :], b_tile(n_e[:, :]), step_k[:, :, :], ALU.is_gt))
                link(v.tensor_reduce(c_e[:, :], cmp_k[:, :, :], AX.X, ALU.add))
                link(v.tensor_tensor_scan(cb_e[:, :], ones[:, 0:E], c_e[:, :], 0.0, ALU.mult, ALU.add))
                link(sub(d_e[:, :], cb_e[:, :], c_e[:, :]))
                link(v.scalar_tensor_tensor(d_e[:, :], d_e[:, :], float(FT),
                                            cum[:, :, NT - 1:NT].rearrange("p e o -> p (e o)"), ALU.mult, ALU.subtract))
                link(v.tensor_tensor(d_e[:, :], d_e[:, :], n_e[:, :], ALU.add))
                link(sub(cum[:, :, :], cum[:, :, :], tot[:, :, :]))
                link(v.tensor_tensor(cum[:, :, :], cum[:, :, :], b_tile(d_e[:, :], NT), ALU.add))
                link(v.tensor_tensor(slot[:, :, :], ps[:, 0, 0:P].rearrange("p (t e) -> p t e", e=E),
                                     cum[:, :, :].rearrange("p e t -> p t e"), ALU.add))
                for c in range(2):
                    link(v.tensor_tensor(key[:, :, :], oh[:, c, :, :], slot[:, :, :], ALU.mult))
                    link(v.tensor_reduce(slot2[:, c, :], key[:, :, :], AX.X, ALU.add))
                link(v.tensor_copy(slot_i[:, :, :], slot2[:, :, :]))
                link(v.tensor_scalar(sa_i[:, :, :], slot_i[:, :, :], 7, None, ALU.arith_shift_right))
                link(v.tensor_scalar(sb_i[:, :, :], slot_i[:, :, :], P - 1, None, ALU.bitwise_and))
                v.tensor_copy(sa_f[:, :, :], sa_i[:, :, :])
                link(v.tensor_copy(sb_f[:, :, :], sb_i[:, :, :]))
                link(v.tensor_tensor(cmp_t[:, :, :], tile_t[:, :, :],
                                     cb_e[:, 0:E - 1].rearrange("p (o e) -> p o e", o=1).to_broadcast([P, ST + 1, E - 1]),
                                     ALU.is_ge))
                link(v.tensor_reduce(eid_f[:, :], cmp_t[:, :, :], AX.X, ALU.add))
                link(v.tensor_copy(eid[n][:, :], eid_f[0:1, :]))
                if n == 0:
                    dve.wait_ge(ws_mm, 1)
                    link(v.tensor_scalar(d_e[:, :], n_e[:, :], 1.0, None, ALU.max))
                    link(v.reciprocal(d_e[:, :], d_e[:, :]))
                    link(v.tensor_tensor(mw_e[:, :], ps[:, 1, 0:E], d_e[:, :], ALU.mult))
                    link(v.tensor_tensor(cmp_m[:, :, :], iota_m[:, :, :], b_tile(eid_f[:, :]), ALU.is_equal))
                    link(v.tensor_tensor(cmp_m[:, :, :], cmp_m[:, :, :],
                                         mw_e[:, :].rearrange("p (o e) -> p o e", o=1).to_broadcast([P, ST + 1, E]), ALU.mult))
                    link(v.tensor_reduce(mw_t[:, :], cmp_m[:, :, :], AX.X, ALU.add))

                parts = 1 if n == 0 else 3

                def one_hots(t):
                    for c in range(2):
                        at = sa_f[:, c, ds(t, 1)]
                        v.tensor_scalar(ohb[:, c, :], iota_p[:, :], sb_f[:, c, ds(t, 1)], None, ALU.is_equal)
                        for k, val in enumerate((tok1[:, ds(t, 1)], s_hi32[:, c, ds(t, 1)], s_lo32[:, c, ds(t, 1)])[:parts]):
                            ins = v.tensor_scalar(oha[:, c, k, :], iota_h[:, :], at, val, ALU.is_equal, ALU.mult)
                        ins.then_inc(r["one"], 1)

                s_hi32, s_lo32 = s_hi[:, :, :].bitcast(f32), s_lo[:, :, :].bitcast(f32)
                with dve.Fori(0, NT) as t:
                    dve.wait_ge(r["inv"], 2 * t)
                    one_hots(t)
                dve.wait_ge(r["inv"], 2 * NT)
                link(v.tensor_copy(inv[:, 0:parts, :], ps[:, 2, 0:parts * SH].rearrange("p (k a) -> p k a", k=parts)))
                link(v.tensor_scalar(gat_f[:, :], inv[:, 0, :], -1.0, 0.0, ALU.add, ALU.max))
                link(v.tensor_copy(gat[n][:, :], gat_f[:, :]))
                link(v.tensor_scalar(inv[:, 0, :], inv[:, 0, :], 0.0, pad_row[:, 0:1], ALU.is_equal, ALU.mult))
                if n == 1:
                    link(v.tensor_tensor(score[:, :], inv[:, 1, :], inv[:, 2, :], ALU.add))
                link(v.tensor_tensor(gat_f[:, :], gat_f[:, :], inv[:, 0, :], ALU.add))
                v.tensor_copy(sca[n][:, :], gat_f[:, :]).then_inc(r["tab"], 1)

            dve.wait_ge(lg_ok, NG)
            route(0, r0)

            def w0_lo(t, b):
                dve.wait_ge(f0["w_hi"], NB0 * t + b + 1)
                sub(w_lo[:, b, :], wr[:, b, :], w_hi[:, b, :]).then_inc(f0["w_lo"], 1)

            def x_lo(t, f):
                dve.wait_ge(f["xt_hi"], t + 1)
                sub(xe_lo[:, :, :].rearrange("p c n -> p (c n)"), ps[:, 6, :],
                    xe_hi[:, :, :].rearrange("p c n -> p (c n)")).then_inc(f["xt_lo"], 1)

            def tile0(t, more=True):
                for q in range(G0):
                    dve.wait_ge(f0["silu"], G0 * t + q + 1)
                    v.tensor_tensor(hf[:, q % 2, :], ps[:, 2 + q % 2, :], sg[:, q % 2, :], ALU.mult).then_inc(f0["h_mul"], 1)
                    if more and q < G0 - 1:
                        w0_lo(t + 1, q)
                    dve.wait_ge(f0["h_hi"], G0 * t + q + 1)
                    sub(h_lo[:, q, :, :].rearrange("p c n -> p (c n)"), hf[:, q % 2, :],
                        h_hi[:, q, :, :].rearrange("p c n -> p (c n)")).then_inc(f0["h_lo"], 1)
                if more:
                    w0_lo(t + 1, G0 - 1)
                    x_lo(t + 1, f0)
                    w0_lo(t + 1, G0)
                    w0_lo(t + 1, G0 + 1)

            for b in range(NB0):
                w0_lo(0, b)
            x_lo(0, f0)
            with dve.Fori(0, ST - 1) as t:
                tile0(t)
            tile0(ST - 1, more=False)

            dve.wait_ge(wss_hi, 1)
            sub(ws_lo[:, :, :, :], wsr, ws_hi[:, :, :, :]).then_inc(wss_lo, 1)
            with dve.Fori(0, NG) as g:
                ch.enter(g, 7)
                dve.wait_ge(x2_in, 16 * g + 16)
                dve.wait_ge(xm_st, 16 * g)
                normalise(n2, g, tile_of(g))
                split_lo(n2, g, 0)
                dve.wait_ge(l_mm, g + 1)
                link(v.tensor_reduce(m1[:, :], ps[:, 2, 0:GT * KP].rearrange("p (t k) -> p t k", k=KP)[:, :, 0:NKEY],
                                     AX.X, ALU.max))
                v.tensor_scalar(m1[:, :], m1[:, :], -(D ** -0.5), None, ALU.mult).then_inc(l_max, 1)
                dve.wait_ge(l_exp, GT * (g + 1))
                dve.wait_ge(p1_hs, g + 1)
                sub(pt1_lo[:, :, :].rearrange("p c n -> p (c n)"), ps[0:NKEY, 3, :],
                    pt1_hi[:, :, :].rearrange("p c n -> p (c n)")).then_inc(p1_ls, 1)
                link(v.reciprocal(den1[:, :], den1[:, :]))
                for j in range(GT):
                    dve.wait_ge(o1_mm, GT * g + 2 * (j // 2) + 2)
                    xt = tile_of(g)(j)
                    v.scalar_tensor_tensor(xt, ps[:, 4 + j // 2, (j % 2) * D:(j % 2 + 1) * D], den1[:, j:j + 1], xt,
                                           ALU.mult, ALU.add).then_inc(x3_ok, 1)
                dve.wait_ge(x3_ok, GT * (g + 1))
                normalise(n3, g, tile_of(g))
                split_lo(n3, g, 0)
                dve.wait_ge(lg_mm[1], g + 1)
                link(v.tensor_copy(group(lg, g), ps[:, 2, 0:GT * E].rearrange("p (t e) -> p t e", e=E)))
                for c in range(KC):
                    dve.wait_ge(ss_ok, KC * g + c + 1)
                    v.tensor_tensor(hfs[:, c, :], ps[:, 5 + 2 * c, :], sgs[:, c, :], ALU.mult).then_inc(shf_ok, 1)
                for c in range(KC):
                    dve.wait_ge(sh_hi, KC * g + c + 1)
                    sub(hs_lo[:, c, :], hfs[:, c, :], hs_hi[:, c, :]).then_inc(sh_lo, 1)
                for h in range(2):
                    dve.wait_ge(sd_mm, 2 * g + h + 1)
                    x2t = x_all[:, ds(g * GT + 2 * h, 2), :]
                    v.tensor_tensor(x2t, ps[:, 2 + h, :].rearrange("p (t d) -> p t d", t=2), x2t, ALU.add).then_inc(so_ok, 1)
                ch.leave(NG)
            route(1, r1)

            def scale1(t):
                dve.wait_ge(f1["x_in"], 32 * (t + 1))
                for half in range(2):
                    v.tensor_scalar(xr[:, half, :], xr[:, half, :], score[:, ds(2 * t + half, 1)], None,
                                    ALU.mult).then_inc(x_sc, 1)

            def w1_lo(t, b):
                dve.wait_ge((f1["w_hi"], wd_hi)[b], t + 1)
                n = WB if b == 0 else WB // 2
                sub(w_lo[:, b, 0:n], wr[:, b, 0:n], w_hi[:, b, 0:n]).then_inc(f1["w_lo"], 1)

            def tile1(t, more=True):
                if more:
                    scale1(t + 1)
                dve.wait_ge(f1["silu"], t + 1)
                v.tensor_tensor(hf[:, 0, :], ps[:, 1, :], sg[:, 0, :], ALU.mult).then_inc(f1["h_mul"], 1)
                dve.wait_ge(f1["h_hi"], t + 1)
                sub(h_lo[:, 0, :, :].rearrange("p c n -> p (c n)"), hf[:, 0, :],
                    h_hi[:, 0, :, :].rearrange("p c n -> p (c n)")).then_inc(f1["h_lo"], 1)
                w1_lo(t, 1)
                if more:
                    w1_lo(t + 1, 0)
                    x_lo(t + 1, f1)

            scale1(0)
            w1_lo(0, 0)
            x_lo(0, f1)
            with dve.Fori(0, ST - 1) as t:
                tile1(t)
            tile1(ST - 1, more=False)

        @block.tensor
        def _(pe):
            T = nc.tensor

            def transpose_group(n, g, b0):
                pe.wait_ge(n["xn"], GT * (g + 1))
                for c in range(KC):
                    for j in range(GT):
                        ins = T.transpose(ps[:, b0 + c, j * P:(j + 1) * P], xn_cur[:, j, c * P:(c + 1) * P], ident[:, :])
                    ins.then_inc(n["mm"], 1)

            def w3(wh, wl, xh, xl, cols_w, cols_x):
                return [(wh[:, c, cols_w], wl[:, c, cols_w], xh[:, c, cols_x], xl[:, c, cols_x]) for c in range(KC)]

            pe.wait_ge(c_in, 32)
            for c in range(KC):
                mm(ps[0:DH, 0, 0:BATCH * NKEY], wkv[:, c, 0:DH], ctxT[:, c, :], c == 0, c == KC - 1)
            for b in range(BATCH):
                for c in range(KC):
                    ins = mm(ps[0:NKEY, 0, 2 * P + b * DH:2 * P + (b + 1) * DH], ctxT[:, c, b * NKEY:(b + 1) * NKEY],
                             wkv[:, c, DH:2 * DH], c == 0, c == KC - 1)
            ins.then_inc(kv_mm, 1)
            pe.wait_ge(const_ok, 1)
            pe.wait_ge(ws0_lo, 3)
            pe.wait_ge(kv_sb, 2)
            with pe.Fori(0, NG) as g:
                transpose_group(n0, g, 0)
                pe.wait_ge(n0["lo"], KC * (g + 1))
                for hc in range(2):
                    mm3(ps[:, 2 + hc, :], w3(wq_hi, wq_lo, t_hi, t_lo, slice(hc * P, (hc + 1) * P), slice(0, GW))
                        ).then_inc(q_mm, 1)

            pe.wait_ge(l1_in, 96)
            for e in range(KC):
                for c in range(KC):
                    ins = mm(ps[:, 4 + e, 0:BATCH * NKEY], w1k[:, c, e * P:(e + 1) * P], ctxT[:, c, :], c == 0, c == KC - 1)
                ins.then_inc(kp_mm, 1)
            pe.wait_ge(kp_sb, KC)
            pe.wait_ge(q_lo, 2 * NG)
            for e in range(KC):
                mm(ps[0:1, 0, 0:BATCH * NKEY], bq[:, e:e + 1], kpT[:, e, :], e == 0, e == KC - 1)
            for c in range(KC):
                for e in range(KC):
                    ins = mm(ps[:, 1 + c, 0:BATCH * NKEY], w1qT[:, e, c * P:(c + 1) * P], kpT[:, e, :], e == 0, e == KC - 1)
                ins.then_inc(g_mm, 1)
            for b in range(BATCH):
                mm(ps[0:NKEY, 3 + b, 0:D], ones[0:1, 0:NKEY], bv[:, :], True, False)
                for c in range(KC):
                    ins = mm(ps[0:NKEY, 3 + b, 0:D], ctxT[:, c, b * NKEY:(b + 1) * NKEY], w1v[:, c, :], False, c == KC - 1)
                ins.then_inc(v1_mm, 1)

            def scores(n, u, i):
                b = i // (NT // BATCH)
                pe.wait_ge(q_cp, n + 1)
                for half in range(2):
                    out = ps[:, 2 * u + half, 0:HB]
                    kh = k_hi[:, ds(b, 1), half * HB:(half + 1) * HB].rearrange("p a n -> p (a n)")
                    kl = k_lo[:, ds(b, 1), half * HB:(half + 1) * HB].rearrange("p a n -> p (a n)")
                    mm(out, qc[u][:, 0, :], kh, True, False)
                    mm(out, qc[u][:, 0, :], kl, False, False)
                    ins = mm(out, qc[u][:, 1, :], kh, False, False)
                ins.then_inc(s_mm, 1)

            def step(n, u, i1, i2, prev=True, cur=True, nxt=True):
                w = 1 - u
                if prev:
                    pe.wait_ge(s_exp, n)
                    for j in range(3):
                        ins = T.transpose(ps[:, 4, j * P:(j + 1) * P], pb_[:, w, win(j):win(j) + P], ident[:, :])
                    ins.then_inc(pt0_mm, 1)
                    for j in range(3, NW):
                        ins = T.transpose(ps[:, 5, (j - 3) * P:(j - 2) * P], pb_[:, w, win(j):win(j) + P], ident[:, :])
                    ins.then_inc(pt1_mm, 1)
                if cur:
                    pe.wait_ge(s_max, n + 1)
                    T.transpose(ps[0:UH, 5, 3 * P:4 * P], m_u[:, u, :], ident[:, :]).then_inc(mt_mm, 1)
                if nxt:
                    scores(n + 1, w, i2)
                if cur:
                    pe.wait_ge(mt_ok, n + 1)
                    for half in range(2):
                        ins = mm(ps[:, 2 * u + half, 0:HB], mT[:, u, :], neg_head[:, half * HB:(half + 1) * HB], False, True)
                    ins.then_inc(sh_mm, 1)
                if prev:
                    b = i1 // (NT // BATCH)
                    for j in range(NW):
                        pe.wait_ge(pt_ls, 2 * n - 1 if j < 3 else 2 * n)
                        cols = slice(head(j) * VW, (head(j) + WINH) * VW)
                        vh = v_hi[:, ds(b, 1), j, cols].rearrange("p a n -> p (a n)")
                        vl = v_lo[:, ds(b, 1), j, cols].rearrange("p a n -> p (a n)")
                        out = ps[:, 6 + w, cols]
                        mm(out, pt_hi[:, j, :], vh, j == 0, False)
                        mm(out, pt_hi[:, j, :], vl, False, False)
                        ins = mm(out, pt_lo[:, j, :], vh, False, j == NW - 1)
                    ins.then_inc(pv_mm, 1)

            pe.wait_ge(kv_lo, 2)
            pe.wait_ge(g_ls, KC + 1)
            pe.wait_ge(v1_ls, BATCH)
            scores(0, 0, 0)
            step(0, 0, 0, 0, prev=False)
            step(1, 1, 0, 1)
            with pe.Fori(1, NT - 1) as i:
                step(2 * i, 0, i - 1, i)
                step(2 * i + 1, 1, i, i + 1)
            step(2 * NT - 2, 0, NT - 2, NT - 1)
            step(2 * NT - 1, 1, NT - 1, NT - 1, nxt=False)
            step(2 * NT, 0, NT - 1, NT - 1, cur=False, nxt=False)

            def logits(L, g, bank_, n):
                pe.wait_ge(n["lo"], KC * (g + 1))
                for j in range(GT):
                    out = ps[:, bank_, j * E:(j + 1) * E]
                    ins = mm3(out, [(t_hi[:, c, j * P:(j + 1) * P], t_lo[:, c, j * P:(j + 1) * P],
                                     rw_hi[:, L, c, :], rw_lo[:, L, c, :]) for c in range(KC)])
                ins.then_inc(lg_mm[L], 1)

            pe.wait_ge(a_ok, 2 * NT)
            with pe.Fori(0, NG) as g:
                pe.wait_ge(ac_ok, g + 1)
                for c in range(KC):
                    for j in range(GT):
                        ins = T.transpose(ps[:, c, j * P:(j + 1) * P], a_cur[:, j, c * P:(c + 1) * P], ident[:, :])
                    ins.then_inc(at_mm, 1)
                pe.wait_ge(at_lo, KC * (g + 1))
                for j in range(GT):
                    ins = mm3(ps[:, 2 + j // 2, (j % 2) * D:(j % 2 + 1) * D],
                              [(t_hi[:, c, j * P:(j + 1) * P], t_lo[:, c, j * P:(j + 1) * P], wc_hi[:, c, :], wc_lo[:, c, :])
                               for c in range(KC)])
                    if j % 2:
                        ins.then_inc(cc_mm, 1)
                transpose_group(n1, g, 4)
                logits(0, g, 6, n1)

            def route(n, r, parts):
                pe.wait_ge(r["msk"], 1)
                m2 = msk[:, :, :].rearrange("p t e -> p (t e)")
                mm(ps[:, 0, 0:P], upperb[:, :], m2, True, True)
                mm(ps[:, 0, P:2 * P], onesb[:, :], m2, True, True).then_inc(r["mm"], 1)
                if n == 0:
                    pe.wait_ge(ws_ok, 1)
                    mm(ps[:, 1, 0:E], ones[:, :], wsum[:, :], True, True).then_inc(ws_mm, 1)
                with pe.Fori(0, NT) as t:
                    for c in range(2):
                        pe.wait_ge(r["one"], 2 * t + c + 1)
                        mm(ps[:, 2, 0:parts * SH], ohb[:, c, :], oha[:, c, 0:parts, :].rearrange("p k a -> p (k a)"),
                           False, False).then_inc(r["inv"], 1)

            def clear_bank2(n, r, parts):
                mm(ps[:, 2, 0:parts * SH], zeros[0:1, 0:P], zeros[0:1, 0:parts * SH], True, False)

            clear_bank2(0, r0, 1)
            route(0, r0, 1)

            def transpose_x(t, f, scaled):
                pe.wait_ge(f["x_in"], 32 * (t + 1))
                if scaled:
                    pe.wait_ge(x_sc, 2 * (t + 1))
                for c in range(KC):
                    for half in range(2):
                        ins = T.transpose(ps[:, 6, c * FT + half * P:c * FT + (half + 1) * P],
                                          xr[:, half, c * P:(c + 1) * P], ident[:, :])
                ins.then_inc(f["xt_mm"], 1)

            def gate_up(wb, bg, bu):
                for which, bk_ in ((0, bg), (1, bu)):
                    for j in range(2):
                        cols = [slice(c * 512 + which * 256 + j * P, c * 512 + which * 256 + (j + 1) * P) for c in range(KC)]
                        ins = mm3(ps[:, bk_, j * FT:(j + 1) * FT],
                                  [(w_hi[:, wb, cols[c]], w_lo[:, wb, cols[c]], xe_hi[:, c, :], xe_lo[:, c, :])
                                   for c in range(KC)])
                return ins

            def down(k, half, wb, start, stop):
                q, j = k // 2, k % 2
                out, hs = ps[:, 4 + half, 0:D], slice(half * P, (half + 1) * P)
                ws = slice((k % 4) * D, (k % 4 + 1) * D)
                mm(out, h_hi[:, q, j, hs], w_hi[:, wb, ws], start, False)
                mm(out, h_hi[:, q, j, hs], w_lo[:, wb, ws], False, False)
                return mm(out, h_lo[:, q, j, hs], w_hi[:, wb, ws], False, stop)

            def tile0(t, first=False, more=True):
                pe.wait_ge(f0["xt_lo"], t + 1)
                for q in range(G0):
                    pe.wait_ge(f0["w_lo"], NB0 * t + q + 1)
                    if not first or q >= 2:
                        pe.wait_ge(f0["h_mul"], G0 * t + q - 1)
                    gate_up(q, q % 2, 2 + q % 2).then_inc(f0["gu_mm"], 1)
                if more:
                    transpose_x(t + 1, f0, False)
                pe.wait_ge(f0["w_lo"], NB0 * t + NB0)
                pe.wait_ge(f0["y_ok"], 2 * t)
                for part in (range(0, 6), range(6, 8)):
                    for half in range(2):
                        for k in part:
                            pe.wait_ge(f0["h_lo"], G0 * t + k // 2 + 1)
                            ins = down(k, half, G0 + k // 4, k == 0, k == 7)
                        if k == 7:
                            ins.then_inc(f0["d_mm"], 1)

            transpose_x(0, f0, False)
            tile0(0, first=True)
            with pe.Fori(1, ST - 1) as t:
                tile0(t)
            tile0(ST - 1, more=False)

            pe.wait_ge(wss_lo, 1)
            with pe.Fori(0, NG) as g:
                b = g // (NG // BATCH)
                transpose_group(n2, g, 0)
                pe.wait_ge(n2["lo"], KC * (g + 1))
                for j in range(GT):
                    out = ps[:, 2, j * KP:(j + 1) * KP]
                    mm(out, ones[0:1, :], c0[:, ds(b, 1), :].rearrange("p a n -> p (a n)"), True, False)
                    for c in range(KC):
                        gh = g_hi[:, c, ds(b, 1), :].rearrange("p a n -> p (a n)")
                        gl = g_lo[:, c, ds(b, 1), :].rearrange("p a n -> p (a n)")
                        mm(out, t_hi[:, c, j * P:(j + 1) * P], gh, False, False)
                        mm(out, t_hi[:, c, j * P:(j + 1) * P], gl, False, False)
                        ins = mm(out, t_lo[:, c, j * P:(j + 1) * P], gh, False, c == KC - 1)
                ins.then_inc(l_mm, 1)
                pe.wait_ge(l_exp, GT * (g + 1))
                for j in range(GT):
                    ins = T.transpose(ps[0:NKEY, 3, j * P:(j + 1) * P], p1[:, j, 0:NKEY], ident[:, :])
                ins.then_inc(p1_mm, 1)
                pe.wait_ge(p1_ls, g + 1)
                for j in range(GT):
                    out = ps[:, 4 + j // 2, (j % 2) * D:(j % 2 + 1) * D]
                    vh = vp_hi[:, ds(b, 1), :].rearrange("p a n -> p (a n)")
                    vl = vp_lo[:, ds(b, 1), :].rearrange("p a n -> p (a n)")
                    mm(out, pt1_hi[:, j, :], vh, True, False)
                    mm(out, pt1_hi[:, j, :], vl, False, False)
                    mm(out, pt1_lo[:, j, :], vh, False, True).then_inc(o1_mm, 1)
                transpose_group(n3, g, 0)
                logits(1, g, 2, n3)
                pe.wait_ge(x3_ok, GT * (g + 1))
                for c in range(KC):
                    for which in range(2):
                        ins = mm3(ps[:, 4 + 2 * c + which, :],
                                  [(ws_hi[:, which, k, c * P:(c + 1) * P], ws_lo[:, which, k, c * P:(c + 1) * P],
                                    t_hi[:, k, :], t_lo[:, k, :]) for k in range(KC)])
                    ins.then_inc(sgu_mm, 1)
                pe.wait_ge(sh_lo, KC * (g + 1))
                for j in range(GT):
                    ins = mm3(ps[:, 2 + j // 2, (j % 2) * D:(j % 2 + 1) * D],
                              [(hs_hi[:, c, j * P:(j + 1) * P], hs_lo[:, c, j * P:(j + 1) * P],
                                ws_hi[:, 2, c, :], ws_lo[:, 2, c, :]) for c in range(KC)])
                    if j % 2:
                        ins.then_inc(sd_mm, 1)

            pe.wait_ge(so_ok, 2 * NG)
            clear_bank2(1, r1, 3)
            route(1, r1, 3)

            def down1(t):
                pe.wait_ge(f1["h_lo"], t + 1)
                pe.wait_ge(f1["w_lo"], 2 * (t + 1))
                pe.wait_ge(f1["y_ok"], 2 * t)
                for half in range(2):
                    for k in range(2):
                        ins = down(k, half, 1, k == 0, k == 1)
                    ins.then_inc(f1["d_mm"], 1)

            def tile1(t, prev=True, more=True):
                pe.wait_ge(f1["xt_lo"], t + 1)
                pe.wait_ge(f1["w_lo"], 2 * t + 1)
                pe.wait_ge(f1["h_mul"], t)
                gate_up(0, 0, 1).then_inc(f1["gu_mm"], 1)
                if more:
                    transpose_x(t + 1, f1, True)
                if prev:
                    down1(t - 1)

            transpose_x(0, f1, True)
            tile1(0, prev=False)
            with pe.Fori(1, ST - 1) as t:
                tile1(t)
            tile1(ST - 1, more=False)
            down1(ST - 1)


def kernel(**inputs):
    import numpy as _np
    import concourse.bacc as _bacc
    from concourse import mybir as _mybir
    from concourse.bass_utils import run_bass_kernel_spmd as _run

    a = {k: _np.asarray(v) for k, v in inputs.items()}

    def parts(w):
        return w.reshape(KC, P, -1).transpose(1, 0, 2)

    def expert_up(gate, up, groups):
        w = _np.stack([gate, up], axis=1).reshape(E, 2, KC, P, groups, 2 * P)
        return w.transpose(0, 4, 3, 2, 1, 5).reshape(E, groups, P, -1)

    def expert_down(w, groups):
        return w.reshape(E, groups, -1, P, D).transpose(0, 1, 3, 2, 4).reshape(E, groups, P, -1)

    up0 = expert_up(a["L0_ffn_gate_w"].transpose(0, 2, 1), a["L0_ffn_up_w"].transpose(0, 2, 1), G0)
    down0 = expert_down(a["L0_ffn_down_w"].transpose(0, 2, 1), NB0 - G0)
    arrays = {
        "x": a["x"].reshape(NT, P, D).transpose(1, 0, 2),
        "ctxT": parts(a["ctx_1024"].reshape(BATCH * NKEY, D).T),
        "wkv": parts(a["L0_xattn_w_kv"]),
        "wq": parts(a["L0_xattn_w_q"]),
        "wc": parts(a["L0_xattn_w_concat"]),
        "rw": _np.stack([parts(a["L0_ffn_router_w"].T), parts(a["L1_ffn_gate_w"].T)], axis=1),
        "w1k": parts(a["L1_xattn_Wk"]),
        "w1qT": parts(a["L1_xattn_Wq"].T),
        "w1v": parts(a["L1_xattn_Wv"]),
        "bk": a["L1_xattn_bk"].reshape(KC, P).T,
        "bq": a["L1_xattn_bq"].reshape(KC, P).T,
        "bv": a["L1_xattn_bv"].reshape(1, D),
        "w0": _np.concatenate([up0, down0], axis=1).reshape(E * NB0 * P, WB),
        "w1gu": expert_up(a["L1_ffn_w1"], a["L1_ffn_w3"], 1).reshape(E * P, WB),
        "w1d": expert_down(a["L1_ffn_w2"], 1).reshape(E * P, WB // 2),
        "ws": _np.stack([parts(a["L1_ffn_w1s"][0]), parts(a["L1_ffn_w3s"][0]), parts(a["L1_ffn_w2s"][0])], axis=1),
    }
    arrays = {k: _np.ascontiguousarray(v) for k, v in arrays.items()}
    nc = _bacc.Bacc("TRN2", target_bir_lowering=False, num_devices=1)
    A = {k: nc.dram_tensor(f"in_{k}", v.shape, _mybir.dt.from_np(v.dtype), kind="ExternalInput").ap()
         for k, v in arrays.items()}
    A["out"] = nc.dram_tensor("out", (ROWS, D), _mybir.dt.float32, kind="ExternalOutput").ap()
    build_program(nc, A)
    r = _run(nc, [{f"in_{k}": v for k, v in arrays.items()}], core_ids=[0])
    return r.results[0]["out"][:NT * P].reshape(BATCH, SEQ, D)
```

```python
import numpy as np
import concourse.bass as bass
from concourse import mybir
from contextlib import ExitStack

P = 128
D = 256
KC = D // P
BATCH, SEQ, NKEY = 2, 1024, 77
NT = BATCH * SEQ // P
GT = 4
NG = NT // GT
GW = GT * P
HEADS, DH = 16, 16
UH = 8
UW = UH * NKEY
HB = UW // 2
NW = -(-UW // P)
VW = DH + 2
WINH = 3
KP = NKEY + 1
E = 8
FT = 256
ST = (NT * P * 2 + E * (FT - 1)) // FT
SH = ST * 2
ROWS = NT * P + 2 * P
F0, F1 = 1024, 256
G0 = F0 // (2 * P)
WB = 1024
NB0 = 6
EPS = 1e-5


class Count:

    def __init__(self, sem):
        self.sem, self.base, self.n, self.start = sem, 0, 0, 0

    def up(self, k=1):
        self.n += k
        return self.base + self.n

    def now(self):
        return self.base + self.n

    def enter(self, i, per, first=0):
        self.start = self.base + self.n
        self.per, self.base, self.n = per, (i - first) * per + self.start, 0

    def leave(self, trips):
        assert self.n == self.per, (self.n, self.per)
        self.base, self.n = self.start + trips * self.per, 0


def build_program(nc, A):
    f32, f32r, bf16, i32 = (mybir.dt.float32, mybir.dt.float32r, mybir.dt.bfloat16, mybir.dt.int32)
    ALU, ACT, AX = mybir.AluOpType, mybir.ActivationFunctionType, mybir.AxisListType
    ds = bass.ds
    ctx = ExitStack()
    with ctx:
        sem = lambda name: ctx.enter_context(nc.semaphore(name))

        kblk_d = nc.dram_tensor("kblk_d", [BATCH, P, UW], f32).ap()
        vblk_d = nc.dram_tensor("vblk_d", [BATCH, NW * P, UH * VW], f32).ap()
        xn_d = nc.dram_tensor("xn_d", [NT * P, D], f32).ap()
        xm_d = nc.dram_tensor("xm_d", [NT * P, D], f32).ap()
        res_d = nc.dram_tensor("res_d", [ROWS, D], f32).ap()
        out_d = A["out"]

        def sb(name, shape, dt=f32, stack=ctx):
            return stack.enter_context(nc.sbuf_tensor(name, shape, dt))

        ident = sb("ident", [P, P])
        iota_p = sb("iota_p", [P, P])
        iota_h = sb("iota_h", [P, SH])
        tok1 = sb("tok1", [P, NT])
        rank_e = sb("rank_e", [P, NT, E])
        step_k = sb("step_k", [P, E, E])
        tile_t = sb("tile_t", [P, ST + 1, E - 1])
        pad_row = sb("pad_row", [P, ST, 2])
        ones = sb("ones", [P, P])
        upper = sb("upper", [P, P])
        onesb = sb("onesb", [P, P], bf16)
        upperb = sb("upperb", [P, P], bf16)
        nege = sb("nege", [UH, UW])
        neg_head = sb("neg_head", [UH, UW], f32r)
        zeros = sb("zeros", [P, 2 * NW * UH * VW])

        ctxT = sb("ctxT", [P, KC, BATCH * NKEY])
        wkv = sb("wkv", [P, KC, 2 * DH])
        wraw = sb("wraw", [P, KC, D])
        wq_hi, wq_lo = sb("wq_hi", [P, KC, D], f32r), sb("wq_lo", [P, KC, D], f32r)
        wraw2 = sb("wraw2", [P, KC, D])
        wc_hi, wc_lo = sb("wc_hi", [P, KC, D], f32r), sb("wc_lo", [P, KC, D], f32r)
        rw = sb("rw", [P, 2, KC, E])
        rw_hi, rw_lo = sb("rw_hi", [P, 2, KC, E], f32r), sb("rw_lo", [P, 2, KC, E], f32r)
        bk = sb("bk", [P, KC])
        bq = sb("bq", [P, KC])
        bv = sb("bv", [1, D])
        g_hi, g_lo = sb("g_hi", [P, KC, BATCH, KP], f32r), sb("g_lo", [P, KC, BATCH, KP], f32r)
        c0 = sb("c0", [1, BATCH, KP])
        vp_hi, vp_lo = sb("vp_hi", [NKEY, BATCH, D], f32r), sb("vp_lo", [NKEY, BATCH, D], f32r)

        x_all = sb("x_all", [P, NT, D])
        lg = sb("lg", [P, NT, E])
        mhalf = sb("mhalf", [P, GT])

        def norm_set(n):
            d = {k: sb(f"{k}_{n}", shape, dt) for k, shape, dt in (
                ("st", [P, GT, 6], f32), ("mv", [P, GT, 2], f32), ("rs", [P, GT], f32), ("x", [P, GT, D], f32),
                ("t_hi", [P, KC, GW], f32r), ("t_lo", [P, KC, GW], f32r))}
            d.update({k: sem(f"n{n}_{k}") for k in ("var", "rstd", "xn", "mm", "hi", "lo")})
            return d

        na, nb = norm_set("a"), norm_set("b")

        mx = sb("mx", [P, NT])
        pr = sb("pr", [P, NT, E])
        key = sb("key", [P, NT, E])
        top = sb("top", [P, 2, NT])
        oh = sb("oh", [P, 2, NT, E])
        msk = sb("msk", [P, NT, E], bf16)
        tmp3 = sb("tmp3", [P, NT, E])
        tot = sb("tot", [P, E, NT])
        cum = sb("cum", [P, E, NT])
        n_e = sb("n_e", [P, E])
        c_e = sb("c_e", [P, E])
        cb_e = sb("cb_e", [P, E])
        d_e = sb("d_e", [P, E])
        cmp_k = sb("cmp_k", [P, E, E])
        slot = sb("slot", [P, NT, E])
        slot2 = sb("slot2", [P, 2, NT])
        slot_i = sb("slot_i", [P, 2, NT], i32)
        sa_i = sb("sa_i", [P, 2, NT], i32)
        sb_i = sb("sb_i", [P, 2, NT], i32)
        sa_f = sb("sa_f", [P, 2, NT])
        sb_f = sb("sb_f", [P, 2, NT])
        cmp_t = sb("cmp_t", [P, ST + 1, E - 1])
        eid_f = sb("eid_f", [P, ST + 1])
        eid = [sb(f"eid{n}", [1, ST + 1], i32) for n in range(2)]
        inv = sb("inv", [P, 3, SH])
        gat_f = sb("gat_f", [P, SH])
        gat = [sb(f"gat{n}", [P, SH], i32) for n in range(2)]
        sca = [sb(f"sca{n}", [P, SH], i32) for n in range(2)]
        score = sb("score", [P, SH])
        s_hi, s_lo = sb("s_hi", [P, 2, NT], f32r), sb("s_lo", [P, 2, NT], f32r)
        wts = sb("wts", [P, 2, NT])
        wsum = sb("wsum", [P, E])
        mw_e = sb("mw_e", [P, E])
        mw_t = sb("mw_t", [P, ST + 1])
        cmp_m = sb("cmp_m", [P, ST + 1, E])
        iota_m = sb("iota_m", [P, ST + 1, E])

        zpad = sb("zpad", [P, BATCH])

        a0 = ExitStack()
        q_all = sb("q_all", [P, 4, NT * P], f32r, a0)
        a_all = sb("a_all", [P, NT, D], f32, a0)
        a_cur = sb("a_cur", [P, GT, D], f32, a0)
        qc = [sb(f"qc{u}", [P, 2, P], f32r, a0) for u in range(2)]
        pb_ = sb("pb_", [P, 2, UW], f32, a0)
        pt_hi, pt_lo = sb("pt_hi", [P, NW, P], f32r, a0), sb("pt_lo", [P, NW, P], f32r, a0)
        m_u = sb("m_u", [P, 2, UH], f32, a0)
        mT = sb("mT", [UH, 2, P], f32r, a0)
        rden = sb("rden", [P, 2, UH], f32, a0)
        kraw = sb("kraw", [P, BATCH, UW], f32, a0)
        k_hi, k_lo = sb("k_hi", [P, BATCH, UW], f32r, a0), sb("k_lo", [P, BATCH, UW], f32r, a0)
        vraw = sb("vraw", [P, BATCH, NW, UH * VW], f32, a0)
        v_hi, v_lo = (sb("v_hi", [P, BATCH, NW, UH * VW], f32r, a0), sb("v_lo", [P, BATCH, NW, UH * VW], f32r, a0))
        ksb = sb("ksb", [DH, BATCH, NKEY], f32, a0)
        vsb = sb("vsb", [NKEY, BATCH, VW], f32, a0)
        w1qT = sb("w1qT", [P, KC, D], f32, a0)
        w1k = sb("w1k", [P, KC, D], f32, a0)
        w1v = sb("w1v", [P, KC, D], f32, a0)
        kpT = sb("kpT", [P, KC, BATCH * NKEY], f32, a0)
        a0.close()
        rt = ExitStack()
        ohb = sb("ohb", [P, 2, NT, P], f32r, rt)
        oha = sb("oha", [P, 2, NT, 3, SH], f32r, rt)
        oh_a = sb("oh_a", [P, 2, NT, SH], f32, rt)
        rt.close()

        xr = sb("xr", [P, 2, 2, D])
        xe_hi, xe_lo = sb("xe_hi", [P, 2, KC, FT], f32r), sb("xe_lo", [P, 2, KC, FT], f32r)
        sg = sb("sg", [P, 2, 512])
        hf = sb("hf", [P, 2, 512])
        h_hi, h_lo = sb("h_hi", [P, G0, 2, FT], f32r), sb("h_lo", [P, G0, 2, FT], f32r)
        ye = sb("ye", [P, 2, 2, D])
        gidx, sidx = sb("gidx", [P, 2, 2], i32), sb("sidx", [P, 2, 2], i32)
        wr = sb("wr", [P, NB0, WB])

        t1 = ExitStack()
        pt1_hi, pt1_lo = sb("pt1_hi", [NKEY, GT, P], f32r, t1), sb("pt1_lo", [NKEY, GT, P], f32r, t1)
        p1 = sb("p1", [P, GT, KP], f32, t1)
        m1 = sb("m1", [P, GT], f32, t1)
        den1 = sb("den1", [P, GT], f32, t1)
        ws_hi, ws_lo = sb("ws_hi", [P, 3, KC, D], f32r, t1), sb("ws_lo", [P, 3, KC, D], f32r, t1)
        sgs = sb("sgs", [P, KC, GW], f32, t1)
        hfs = sb("hfs", [P, KC, GW], f32, t1)
        hs_hi, hs_lo = sb("hs_hi", [P, KC, GW], f32r, t1), sb("hs_lo", [P, KC, GW], f32r, t1)
        t1.close()
        w_hi, w_lo = sb("w_hi", [P, NB0, WB], f32r), sb("w_lo", [P, NB0, WB], f32r)
        wsr = wr[:, 0:2, :].rearrange("p b n -> p (b n)")[:, 0:3 * KC * D].rearrange("p (w c n) -> p w c n", w=3, c=KC)

        ps = ctx.enter_context(nc.psum_tensor("ps", [P, 8, 512], f32))

        x_first, x_in, c_in, w_in0, wc_in, l1_in, ws_in = sem("x_first"), sem("x_in"), sem("c_in"), sem("w_in0"), sem("wc_in"), sem("l1_in"), sem("ws_in")
        zeros_ok, ident_ok, const_ok = sem("zeros_ok"), sem("ident_ok"), sem("const_ok")
        pool_ch, dve_ch = sem("pool_ch"), sem("dve_ch")
        zero_st, pad_st, kv_mm, kv_sb, kv_st, kv_ld, kv_hi, kv_lo = (sem(n) for n in (
            "zero_st", "pad_st", "kv_mm", "kv_sb", "kv_st", "kv_ld", "kv_hi", "kv_lo"))
        ws0_hi, ws0_lo = sem("ws0_hi"), sem("ws0_lo")
        kp_mm, kp_sb, g_mm, g_hs, g_ls, v1_mm, v1_hs, v1_ls = (sem(n) for n in (
            "kp_mm", "kp_sb", "g_mm", "g_hs", "g_ls", "v1_mm", "v1_hs", "v1_ls"))

        q_mm, q_hi, q_lo = sem("q_mm"), sem("q_hi"), sem("q_lo")
        q_cp, s_mm, s_max, pt0_mm, pt1_mm, mt_mm, mt_ok, pt_hs, pt_ls, sh_mm, s_exp, pv_mm, a_ok = (sem(n) for n in (
            "q_cp", "s_mm", "s_max", "pt0_mm", "pt1_mm", "mt_mm", "mt_ok", "pt_hs", "pt_ls", "sh_mm", "s_exp",
            "pv_mm", "a_ok"))
        ac_ok, at_mm, at_hi, at_lo, cc_mm, x1_ok, x1_st, xn_st, xm_st = (sem(n) for n in (
            "ac_ok", "at_mm", "at_hi", "at_lo", "cc_mm", "x1_ok", "x1_st", "xn_st", "xm_st"))
        lg_mm, lg_ok = [sem(f"lg_mm{n}") for n in range(2)], sem("lg_ok")

        def route_sems(n):
            return {k: sem(f"r{n}_{k}") for k in ("sub", "exp", "msk", "mm", "place", "ohb", "oha", "inv", "eid", "tab")}

        r0, r1 = route_sems(0), route_sems(1)
        ws_ok, ws_mm = sem("ws_ok"), sem("ws_mm")
        x2_in = [sem(f"x2_in{n}") for n in range(3)]
        l_mm, l_max, l_exp, p1_mm, p1_hs, p1_ls, o1_mm, x3_ok = (sem(n) for n in (
            "l_mm", "l_max", "l_exp", "p1_mm", "p1_hs", "p1_ls", "o1_mm", "x3_ok"))
        sgu_mm, ss_ok, shf_ok, sh_hi, sh_lo, sd_mm, so_ok, so_st, wss_hi, wss_lo = (sem(n) for n in (
            "sgu_mm", "ss_ok", "shf_ok", "sh_hi", "sh_lo", "sd_mm", "so_ok", "so_st", "wss_hi", "wss_lo"))

        def ffn_sems(n):
            return {k: sem(f"f{n}_{k}") for k in ("idx", "w_hi", "w_lo", "xt_mm", "xt_hi", "xt_lo", "gu_mm",
                                                  "silu", "h_mul", "h_hi", "h_lo", "d_mm", "y_ok", "y_st")}

        f0, f1 = ffn_sems(0), ffn_sems(1)
        w_in = [sem(f"w_in_{b}") for b in range(NB0)]
        x0_in, x1_in = sem("x0_in"), [sem(f"x1_in{p}") for p in range(2)]
        x_sc = [sem(f"x_sc{h}") for h in range(2)]
        wd_hi, wd_lo = sem("wd_hi"), sem("wd_lo")
        passed = sem("passed")
        block = ctx.enter_context(nc.Block())

        def mm(out, w, x, start, stop):
            return nc.tensor.matmul(out, w, x, start=start, stop=stop, skip_group_check=True)

        def mm3(out, pairs):
            for n, (wh, wl, xh, xl) in enumerate(pairs):
                mm(out, wh, xh, n == 0, False)
                mm(out, wh, xl, False, False)
                last = mm(out, wl, xh, False, n == len(pairs) - 1)
            return last

        def win(j):
            return min(P * j, UW - P)

        def head(j):
            return min(win(j) // NKEY, UH - WINH)

        def group(t, g):
            return t[:, ds(g * GT, GT), :]

        def rows(t, g):
            return t[ds(g * GW, GW), :].rearrange("(t p) d -> p t d", p=P)

        def b_tile(a, n=E):
            return a.rearrange("p (t o) -> p t o", o=1).to_broadcast([P, a.shape[1], n])

        def b_row(a, n):
            return a.rearrange("p (o e) -> p o e", o=1).to_broadcast([P, n, a.shape[1]])

        def alone(engine):
            engine.sem_inc(passed, 1)

        @block.sync
        def _(sp):
            def load_x(g):
                sp.dma_start(x_all[:, g * GT:(g + 1) * GT, :], A["x"][:, g * GT:(g + 1) * GT, :]
                             ).then_inc(x_in if g else x_first, 16)

            sp.dma_start(ctxT[:, :, :], A["ctxT"]).then_inc(c_in, 16)
            sp.dma_start(wkv[:, :, :], A["wkv"]).then_inc(c_in, 16)
            load_x(0)
            for dst, name in ((w1k, "w1k"), (w1qT, "w1qT"), (w1v, "w1v")):
                sp.dma_start(dst[:, :, :], A[name]).then_inc(l1_in, 16)
            sp.dma_start(bk[:, :], A["bk"]).then_inc(l1_in, 16)
            sp.dma_start(bq[:, :], A["bq"]).then_inc(l1_in, 16)
            sp.dma_start(bv[:, :], A["bv"]).then_inc(l1_in, 16)
            sp.dma_start(wraw[:, :, :], A["wq"]).then_inc(w_in0, 16)
            for g in range(1, NG):
                load_x(g)
            sp.wait_ge(zeros_ok, 1)
            sp.dma_start(kblk_d.rearrange("b p n -> p b n"),
                         zeros[:, 0:BATCH * UW].rearrange("p (b n) -> p b n", b=BATCH)).then_inc(zero_st, 16)
            sp.dma_start(vblk_d.rearrange("b (j p) n -> p (b j) n", p=P),
                         zeros[:, :].rearrange("p (b n) -> p b n", n=UH * VW)).then_inc(zero_st, 16)
            sp.dma_start(res_d[NT * P:ROWS, :].rearrange("(h p) d -> p h d", p=P),
                         zeros[:, 0:2 * D].rearrange("p (h d) -> p h d", h=2)).then_inc(pad_st, 16)
            sp.dma_start(out_d[NT * P:ROWS, :].rearrange("(h p) d -> p h d", p=P),
                         zeros[:, 0:2 * D].rearrange("p (h d) -> p h d", h=2)).then_inc(pad_st, 16)
            sp.dma_start(wraw2[:, :, :], A["wc"]).then_inc(wc_in, 16)
            sp.dma_start(rw[:, :, :, :], A["rw"]).then_inc(wc_in, 16)
            sp.wait_ge(zero_st, 32)
            sp.wait_ge(kv_sb, 2)
            cut = 4 * P - 6 * NKEY
            skip = NW * P - UW
            for b in range(BATCH):
                kd = bass.AP(tensor=kblk_d.tensor, offset=b * P * UW, ap=[[UW, DH], [DH * UW + NKEY, UH], [1, NKEY]])
                sp.dma_start(kd, ksb[:, b:b + 1, :].to_broadcast([DH, UH, NKEY])).then_inc(kv_st, 16)
                base, w = b * NW * P * UH * VW, UH * VW
                vd = bass.AP(tensor=vblk_d.tensor, offset=base, ap=[[w, NKEY], [NKEY * w + VW, 6], [1, VW]])
                sp.dma_start(vd, vsb[:, b:b + 1, :].to_broadcast([NKEY, 6, VW])).then_inc(kv_st, 16)
                for head_, k0, k1, up in ((6, 0, cut, 0), (6, cut, NKEY, skip), (7, 0, NKEY, skip)):
                    r = head_ * NKEY + up
                    sp.dma_start(vblk_d[b, r + k0:r + k1, head_ * VW:(head_ + 1) * VW],
                                 vsb[k0:k1, b, :]).then_inc(kv_st, 16)
            sp.wait_ge(kv_st, 16 * 5 * BATCH)
            sp.dma_start(kraw[:, :, :], kblk_d.rearrange("b p n -> p b n")).then_inc(kv_ld, 16)
            sp.dma_start(vraw[:, :, :, :], vblk_d.rearrange("b (j p) n -> p b j n", p=P)).then_inc(kv_ld, 16)

            with sp.Fori(0, NG) as g:
                sp.wait_ge(x1_ok, 2 * g + 2)
                sp.dma_start(rows(res_d, g), group(x_all, g)).then_inc(x1_st, 16)
                sp.wait_ge(nb["xn"], g + 1)
                sp.dma_start(rows(xn_d, g), nb["x"][:, :, :]).then_inc(xn_st, 16)

            sp.wait_ge(r0["eid"], 1)

            def load0(t, first=False):
                e = sp.value_load(eid[0][0:1, ds(t, 1)], min_val=0, max_val=E - 1)
                for b in range(NB0):
                    if not first:
                        sp.wait_ge(f0["w_lo"], (t - 1) * NB0 + b + 1)
                    sp.dma_start(wr[:, b, :], A["w0"][ds(e * (NB0 * P) + b * P, P), :]).then_inc(w_in[b], 16)

            load0(0, True)
            with sp.Fori(1, ST) as t:
                load0(t)

            sp.wait_ge(f0["w_lo"], NB0 * ST)
            sp.dma_start(wsr, A["ws"]).then_inc(ws_in, 16)
            sp.wait_ge(f0["y_st"], 32 * ST)
            for g in range(NG):
                sp.dma_start(group(x_all, g), rows(res_d, g)).then_inc(x2_in[min(g, 2)], 16)
            with sp.Fori(0, NG) as g:
                sp.wait_ge(nb["xn"], NG + g + 1)
                sp.dma_start(rows(xm_d, g), nb["x"][:, :, :]).then_inc(xm_st, 16)
                sp.wait_ge(so_ok, 2 * g + 2)
                sp.dma_start(rows(out_d, g), group(x_all, g)).then_inc(so_st, 16)

            sp.wait_ge(r1["eid"], 1)

            def load1(t, p, first=False):
                e = sp.value_load(eid[1][0:1, ds(t, 1)], min_val=0, max_val=E - 1)
                for b, (name, n, lo) in enumerate((("w1gu", WB, f1["w_lo"]), ("w1d", WB // 2, wd_lo))):
                    if not first:
                        sp.wait_ge(lo, t - 1)
                    sp.dma_start(wr[:, 2 * p + b, 0:n], A[name][ds(e * P, P), :]).then_inc(w_in[2 * p + b], 16)

            load1(0, 0, True)
            load1(1, 1, True)
            with sp.Fori(1, ST // 2) as i:
                load1(2 * i, 0)
                load1(2 * i + 1, 1)
            load1(ST - 1, 0)
            for s, v in ((f1["y_st"], 32 * ST), (so_st, 16 * NG), (pad_st, 32), (xm_st, 16 * NG), (xn_st, 16 * NG),
                         (x1_st, 16 * NG)):
                sp.wait_ge(s, v)

        @block.gpsimd
        def _(pool):
            g = nc.gpsimd
            ch = Count(pool_ch)

            def link(ins):
                ins.then_inc(ch.sem, 1)
                pool.wait_ge(ch.sem, ch.up())

            def root(n, k):
                pool.wait_ge(n["var"], k + 1)
                alone(pool)
                link(g.tensor_scalar(n["rs"][:, :], n["mv"][:, :, 1], EPS, None, ALU.add))
                g.tensor_tensor(n["rs"][:, :], n["rs"][:, :], mhalf[:, :], ALU.pow).then_inc(n["rstd"], 1)

            link(g.memset(ones[:, :], 1.0))
            g.affine_select(out=ident[:, :], in_=ones[:, :], compare_op=ALU.is_equal, fill=0.0, base=0,
                            pattern=[[1, P]], channel_multiplier=-1)
            g.memset(mhalf[:, :], -0.5).then_inc(ident_ok, 1)
            g.memset(zeros[:, :], 0.0).then_inc(zeros_ok, 1)
            link(g.memset(nege[:, :], -1.0))
            root(na, 0)
            link(g.affine_select(out=upper[:, :], in_=ones[:, :], compare_op=ALU.is_gt, fill=0.0, base=0,
                                 pattern=[[1, P]], channel_multiplier=-1))
            link(g.affine_select(out=nege[:, :], in_=nege[:, :], compare_op=ALU.is_ge, fill=0.0, base=0,
                                 pattern=[[1, UW]], channel_multiplier=-NKEY))
            link(g.affine_select(out=nege[:, :], in_=nege[:, :], compare_op=ALU.is_gt, fill=0.0, base=NKEY,
                                 pattern=[[-1, UW]], channel_multiplier=NKEY))
            g.tensor_copy(neg_head[:, :], nege[:, :])
            g.tensor_copy(onesb[:, :], ones[:, :])
            g.tensor_copy(upperb[:, :], upper[:, :])
            io = dict(allow_small_or_imprecise_dtypes=True)
            g.iota(iota_p[:, :], pattern=[[1, P]], base=0, channel_multiplier=0, **io)
            g.iota(iota_h[:, :], pattern=[[1, SH]], base=0, channel_multiplier=0, **io)
            g.iota(tok1[:, :], pattern=[[P, NT]], base=1, channel_multiplier=1, **io)
            g.iota(rank_e[:, :, :], pattern=[[0, NT], [-1, E]], base=E, channel_multiplier=0, **io)
            g.iota(step_k[:, :, :], pattern=[[0, E], [FT, E]], base=0, channel_multiplier=0, **io)
            g.iota(tile_t[:, :, :], pattern=[[1, ST + 1], [0, E - 1]], base=0, channel_multiplier=0, **io)
            g.iota(iota_m[:, :, :], pattern=[[0, ST + 1], [1, E]], base=0, channel_multiplier=0, **io)
            g.iota(pad_row[:, :, :], pattern=[[0, ST], [P, 2]], base=NT * P, channel_multiplier=1, **io).then_inc(const_ok, 1)

            with pool.Fori(1, NG) as gr:
                ch.enter(gr, 1, 1)
                root(na, gr)
                ch.leave(NG - 1)

            def copy_q(i, u, first=False):
                if not first:
                    pool.wait_ge(s_mm, 2 * i + u - 1)
                g.tensor_copy(qc[u][:, :, :], q_all[:, 2 * u:2 * u + 2, ds(i * P, P)]).then_inc(q_cp, 1)

            pool.wait_ge(q_lo, KC)
            copy_q(0, 0, True)
            copy_q(0, 1, True)
            pool.wait_ge(q_lo, KC * NG)
            with pool.Fori(1, NT) as i:
                copy_q(i, 0)
                copy_q(i, 1)

            pool.wait_ge(a_ok, 2 * GT)

            def copy_a(gr):
                g.tensor_copy(a_cur[:, :, :], group(a_all, gr)).then_inc(ac_ok, 1)

            copy_a(0)
            pool.wait_ge(a_ok, 2 * NT)
            with pool.Fori(1, NG) as gr:
                ch.enter(gr, 1, 1)
                pool.wait_ge(at_mm, 2 * gr)
                copy_a(gr)
                root(nb, gr - 1)
                ch.leave(NG - 1)
            root(nb, NG - 1)

            s_hi32 = s_hi[:, :, :].bitcast(f32)

            def weigh_one_hots(n, r):
                for h in range(2):
                    pool.wait_ge(r["place"], h + 1)
                    ts = slice(h * NT // 2, (h + 1) * NT // 2)
                    for c in range(2):
                        for k, val in enumerate((tok1[:, ts], s_hi32[:, c, ts])[:1 if n == 0 else 2]):
                            ins = g.tensor_tensor(oha[:, c, ts, k, :], oh_a[:, c, ts, :], b_tile(val, SH), ALU.mult)
                    ins.then_inc(r["oha"], 1)

            def indices(idx, dst, src, t):
                g.tensor_copy(dst, src[:, ds(2 * t, 2)]).then_inc(idx.sem, 1)
                pool.wait_ge(idx.sem, idx.up())

            def gather(src, p, s):
                for half in range(2):
                    alone(pool)
                    pool.indirect_dma_start(xr[:, p, half, :], None, src,
                                            bass.IndirectOffsetOnAxis(ap=gidx[:, p, half:half + 1], axis=0)
                                            ).then_inc(s, 16)

            def scatter_add(dst, p, f):
                for half in range(2):
                    alone(pool)
                    pool.indirect_dma_start(dst, bass.IndirectOffsetOnAxis(ap=sidx[:, p, half:half + 1], axis=0),
                                            ye[:, p, half, :], None, compute_op=ALU.add).then_inc(f["y_st"], 16)

            weigh_one_hots(0, r0)
            pool.wait_ge(r0["tab"], 1)
            pool.wait_ge(xn_st, 16 * NG)
            pool.wait_ge(x1_st, 16 * NG)
            pool.wait_ge(pad_st, 32)
            idx = Count(f0["idx"])

            def fetch0(t, first=False):
                if not first:
                    pool.wait_ge(x0_in, 32 * t)
                    pool.wait_ge(f0["xt_mm"], t)
                indices(idx, gidx[:, 0, :], gat[0], t)
                gather(xn_d, 0, x0_in)

            def add0(t, first=False):
                if not first:
                    pool.wait_ge(f0["y_st"], 32 * t)
                indices(idx, sidx[:, 0, :], sca[0], t)
                pool.wait_ge(f0["y_ok"], 2 * t + 2)
                scatter_add(res_d, 0, f0)

            fetch0(0, True)
            fetch0(1)
            add0(0, True)
            with pool.Fori(1, ST - 1) as t:
                idx.enter(t, 2, 1)
                fetch0(t + 1)
                add0(t)
                idx.leave(ST - 2)
            add0(ST - 1)

            root(na, NG)
            root(na, NG + 1)
            with pool.Fori(0, NG - 2) as gr:
                ch.enter(gr, 2)
                root(nb, NG + gr)
                root(na, NG + gr + 2)
                ch.leave(NG - 2)
            root(nb, 2 * NG - 2)
            root(nb, 2 * NG - 1)

            weigh_one_hots(1, r1)
            pool.wait_ge(r1["tab"], 1)
            pool.wait_ge(xm_st, 16 * NG)
            pool.wait_ge(so_st, 16 * NG)
            idx = Count(f1["idx"])

            def fetch1(i, p, first=False):
                t = 2 * i + p
                if not first:
                    pool.wait_ge(x1_in[p], 32 * i)
                    pool.wait_ge(f1["xt_mm"], t - 1)
                indices(idx, gidx[:, p, :], gat[1], t)
                gather(xm_d, p, x1_in[p])

            def add1(i, p, first=False):
                t = 2 * i + p
                indices(idx, sidx[:, p, :], sca[1], t)
                pool.wait_ge(f1["y_ok"], 2 * t + 2)
                if not first:
                    pool.wait_ge(f1["y_st"], 32 * t)
                scatter_add(out_d, p, f1)

            for t in range(5):
                fetch1(t // 2, t % 2, t < 2)
            fetch1(2, 1)
            add1(0, 0, True)
            fetch1(3, 0)
            add1(0, 1)
            with pool.Fori(1, (ST - 5) // 2) as i:
                idx.enter(i, 4, 1)
                fetch1(i + 2, 1)
                add1(i, 0)
                fetch1(i + 3, 0)
                add1(i, 1)
                idx.leave((ST - 5) // 2 - 1)
            for t in range(ST - 5, ST):
                add1(t // 2, t % 2)

        @block.scalar
        def _(act):
            s = nc.scalar

            def copy(o, i):
                return s.activation(o, i, ACT.Copy)

            def split_hi(n, k, b0):
                for c in range(KC):
                    act.wait_ge(n["mm"], KC * k + c + 1)
                    copy(n["t_hi"][:, c, :], ps[:, b0 + c, :]).then_inc(n["hi"], 1)

            act.wait_ge(w_in0, 16)
            copy(wq_hi[:, :, :], wraw[:, :, :]).then_inc(ws0_hi, 1)

            def queries(g):
                for c in range(KC):
                    act.wait_ge(q_mm, KC * g + c + 1)
                    alone(act)
                    copy(q_all[:, 2 * c, ds(g * GW, GW)], ps[:, 2 + c, :]).then_inc(q_hi, 1)

            split_hi(na, 0, 0)
            with act.Fori(1, NG - 1) as g:
                queries(g - 1)
                split_hi(na, g, 0)
            act.wait_ge(kv_ld, 32)
            copy(k_hi[:, :, :], kraw[:, :, :]).then_inc(kv_hi, 1)
            copy(v_hi[:, :, :, :], vraw[:, :, :, :]).then_inc(kv_hi, 1)
            queries(NG - 2)
            split_hi(na, NG - 1, 0)
            queries(NG - 1)

            def step(n, u, prev=True, cur=True):
                if prev:
                    act.wait_ge(pt0_mm, n)
                    copy(pt_hi[:, 0:3, :], ps[:, 4, 0:3 * P]).then_inc(pt_hs, 1)
                if cur:
                    act.wait_ge(mt_mm, n + 1)
                    copy(mT[:, u, :], ps[0:UH, 5, 3 * P:4 * P]).then_inc(mt_ok, 1)
                if prev:
                    act.wait_ge(pt1_mm, n)
                    copy(pt_hi[:, 3:5, :], ps[:, 5, 0:2 * P]).then_inc(pt_hs, 1)
                if cur:
                    act.wait_ge(sh_mm, n + 1)
                    s.activation(pb_[:, u, :].rearrange("p (a n) -> p a n", a=2),
                                 ps[:, 2 * u:2 * u + 2, 0:HB], ACT.Exp, scale=DH ** -0.5).then_inc(s_exp, 1)

            step(0, 0, prev=False)
            act.wait_ge(v1_mm, 1)
            copy(vp_hi[:, :, :], ps[0:NKEY, 4, :].rearrange("p (b n) -> p b n", b=BATCH)).then_inc(v1_hs, 1)
            act.wait_ge(g_mm, KC)
            for c in range(KC):
                copy(g_hi[:, c, :, 0:NKEY], ps[:, 6 + c, 0:BATCH * NKEY].rearrange("p (b k) -> p b k", b=BATCH)
                     ).then_inc(g_hs, 1)
            step(1, 1)
            act.wait_ge(wc_in, 32)
            copy(wc_hi[:, :, :], wraw2[:, :, :]).then_inc(ws0_hi, 1)
            copy(rw_hi[:, :, :, :], rw[:, :, :, :]).then_inc(ws0_hi, 1)
            with act.Fori(1, NT) as i:
                step(2 * i, 0)
                step(2 * i + 1, 1)
            step(2 * NT, 0, cur=False)

            def project(g, cur=True, prev=True):
                if cur:
                    for c in range(KC):
                        act.wait_ge(at_mm, KC * g + c + 1)
                        copy(na["t_hi"][:, c, :], ps[:, c, :]).then_inc(at_hi, 1)
                if prev:
                    split_hi(nb, g - 1, 4)

            project(0, prev=False)
            with act.Fori(1, NG) as g:
                project(g)
            project(NG, cur=False)

            def route(r):
                act.wait_ge(r["sub"], 1)
                s.activation(pr[:, :, :], pr[:, :, :], ACT.Exp).then_inc(r["exp"], 1)

            route(r0)

            def w0_hi(t, b):
                act.wait_ge(w_in[b], 16 * (t + 1))
                copy(w_hi[:, b, :], wr[:, b, :]).then_inc(f0["w_hi"], 1)

            def x_hi(f, t, p=0):
                act.wait_ge(f["xt_mm"], t + 1)
                copy(xe_hi[:, p, :, :].rearrange("p c n -> p (c n)"), ps[:, 6 + p, :]).then_inc(f["xt_hi"], 1)

            def tile0(t, first=False, more=True):
                for q in range(G0):
                    act.wait_ge(f0["gu_mm"], G0 * t + q + 1)
                    s.activation(sg[:, q % 2, :], ps[:, q % 2, :], ACT.Silu).then_inc(f0["silu"], 1)
                    if more and q < G0 - 1:
                        w0_hi(t + 1, q)
                    act.wait_ge(f0["h_mul"], G0 * t + q + 1)
                    copy(h_hi[:, q, :, :].rearrange("p c n -> p (c n)"), hf[:, q % 2, :]).then_inc(f0["h_hi"], 1)
                if more:
                    w0_hi(t + 1, G0 - 1)
                    x_hi(f0, t + 1)
                if not first:
                    act.wait_ge(f0["y_st"], 32 * t)
                for half in range(2):
                    act.wait_ge(f0["d_mm"], 2 * t + half + 1)
                    alone(act)
                    s.activation(ye[:, 0, half, :], ps[:, 4 + half, 0:D], ACT.Copy,
                                 scale=mw_t[:, ds(t, 1)]).then_inc(f0["y_ok"], 1)
                if more:
                    w0_hi(t + 1, G0)
                    w0_hi(t + 1, G0 + 1)

            for b in range(NB0):
                w0_hi(0, b)
            x_hi(f0, 0)
            tile0(0, first=True)
            with act.Fori(1, ST - 1) as t:
                tile0(t)
            tile0(ST - 1, more=False)

            act.wait_ge(ws_in, 16)
            copy(ws_hi[:, :, :, :], wsr).then_inc(wss_hi, 1)

            def group1(g, a=True, b=True):
                if a:
                    split_hi(na, NG + g, 0)
                    act.wait_ge(l_max, g + 1)
                    for j in range(GT):
                        s.activation(p1[:, j, 0:NKEY], ps[:, 0, j * KP:j * KP + NKEY], ACT.Exp, bias=m1[:, j:j + 1],
                                     scale=D ** -0.5, accum_out=den1[:, j:j + 1]).then_inc(l_exp, 1)
                if b:
                    split_hi(nb, NG + g - 1, 2)
                if a:
                    act.wait_ge(p1_mm, g + 1)
                    copy(pt1_hi[:, :, :].rearrange("p c n -> p (c n)"), ps[0:NKEY, 1, :]).then_inc(p1_hs, 1)
                if not a:
                    route(r1)
                if b:
                    for c in range(KC):
                        act.wait_ge(sgu_mm, KC * (g - 1) + c + 1)
                        s.activation(sgs[:, c, :], ps[:, 4 + 2 * c, :], ACT.Silu).then_inc(ss_ok, 1)
                    for c in range(KC):
                        act.wait_ge(shf_ok, KC * (g - 1) + c + 1)
                        copy(hs_hi[:, c, :], hfs[:, c, :]).then_inc(sh_hi, 1)

            group1(0, b=False)
            with act.Fori(1, NG) as g:
                group1(g)
            group1(NG, a=False)

            def w1_hi(i, p, b):
                act.wait_ge(w_in[2 * p + b], 16 * (ST + i + 1))
                n = WB if b == 0 else WB // 2
                copy(w_hi[:, 2 * p + b, 0:n], wr[:, 2 * p + b, 0:n]).then_inc((f1["w_hi"], wd_hi)[b], 1)

            def scale1(i, p):
                act.wait_ge(x1_in[p], 32 * (i + 1))
                alone(act)
                s.activation(xr[:, p, 0, :], xr[:, p, 0, :], ACT.Copy, scale=score[:, ds(4 * i + 2 * p, 1)]
                             ).then_inc(x_sc[0], 1)

            def y1(t, p, first=False):
                if not first:
                    act.wait_ge(f1["y_st"], 32 * (t - 1))
                for half in range(2):
                    act.wait_ge(f1["d_mm"], 2 * t + half + 1)
                    copy(ye[:, p, half, :], ps[:, 4 + half, 0:D]).then_inc(f1["y_ok"], 1)

            def tile1(i, p, x1=True, x2=True, x3=True, prev=1):
                t, o = 2 * i + p, 1 - p
                act.wait_ge(f1["gu_mm"], t + 1)
                s.activation(sg[:, p, :], ps[:, 2 * p, :], ACT.Silu).then_inc(f1["silu"], 1)
                if x2:
                    x_hi(f1, t + 2, p)
                act.wait_ge(f1["h_mul"], t + 1)
                copy(h_hi[:, p, :, :].rearrange("p c n -> p (c n)"), hf[:, p, :]).then_inc(f1["h_hi"], 1)
                if x2:
                    w1_hi(i + 1, p, 0)
                if prev:
                    y1(t - 1, o, first=prev == 2)
                if x1:
                    w1_hi(i + p, o, 1)
                if x3:
                    scale1(i + 1 + p, o)

            w1_hi(0, 0, 0)
            w1_hi(0, 1, 0)
            w1_hi(0, 0, 1)
            scale1(0, 0)
            scale1(0, 1)
            x_hi(f1, 0, 0)
            x_hi(f1, 1, 1)
            scale1(1, 0)
            tile1(0, 0, prev=0)
            tile1(0, 1, prev=2)
            tile1(1, 0, prev=2)
            tile1(1, 1)
            with act.Fori(2, (ST - 3) // 2) as i:
                tile1(i, 0)
                tile1(i, 1)
            tile1((ST - 3) // 2, 0, x3=False)
            tile1((ST - 3) // 2, 1, x2=False, x3=False)
            tile1(ST // 2, 0, x1=False, x2=False, x3=False)
            y1(ST - 1, 0)

        @block.vector
        def _(dve):
            v = nc.vector
            ch = Count(dve_ch)

            def link(ins):
                ins.then_inc(ch.sem, 1)
                dve.wait_ge(ch.sem, ch.up())

            def sub(o, a, b):
                return v.tensor_tensor(o, a, b, ALU.subtract)

            def statistics(n, src):
                alone(dve)
                for j in range(GT):
                    ins = v.bn_stats(n["st"][:, j, :], src(j))
                link(ins)
                alone(dve)
                for j in range(GT):
                    ins = v.bn_aggr(n["mv"][:, j, :], n["st"][:, j, :])
                ins.then_inc(n["var"], 1)

            def normalise(n, k, src):
                dve.wait_ge(n["rstd"], k + 1)
                for j in range(GT):
                    ins = v.tensor_scalar(n["x"][:, j, :], src(j), n["mv"][:, j, 0:1], n["rs"][:, j:j + 1],
                                          ALU.subtract, ALU.mult)
                ins.then_inc(n["xn"], 1)

            def split_lo(n, k, b0):
                for c in range(KC):
                    dve.wait_ge(n["hi"], KC * k + c + 1)
                    sub(n["t_lo"][:, c, :], ps[:, b0 + c, :], n["t_hi"][:, c, :]).then_inc(n["lo"], 1)

            def tile_of(g):
                return lambda j: x_all[:, ds(g * GT + j, 1), :].rearrange("p a d -> p (a d)")

            dve.wait_ge(x_first, 16)
            statistics(na, tile_of(0))
            v.memset(vsb[:, :, :], 0.0)
            v.memset(c0[:, :, :], 0.0)
            link(v.memset(zpad[:, :], 0.0))
            link(v.memset(vsb[:, :, DH:DH + 1], 1.0))
            dve.wait_ge(kv_mm, 1)
            v.tensor_copy(ksb[:, :, :], ps[0:DH, 0, 0:BATCH * NKEY].rearrange("p (b k) -> p b k", b=BATCH)).then_inc(kv_sb, 1)
            v.tensor_copy(vsb[:, :, 0:DH], ps[0:NKEY, 0, 2 * P:2 * P + BATCH * DH].rearrange("p (b k) -> p b k", b=BATCH)
                          ).then_inc(kv_sb, 1)
            dve.wait_ge(kp_mm, KC)
            for c in range(KC):
                v.tensor_scalar(kpT[:, c, :], ps[:, 4 + c, 0:BATCH * NKEY], bk[:, c:c + 1], None, ALU.add).then_inc(kp_sb, 1)
            normalise(na, 0, tile_of(0))
            dve.wait_ge(ws0_hi, 1)
            sub(wq_lo[:, :, :], wraw[:, :, :], wq_hi[:, :, :]).then_inc(ws0_lo, 1)

            def queries(g, more=True, blocks=False):
                if more:
                    statistics(na, tile_of(g + 1))
                split_lo(na, g, 0)
                if more:
                    dve.wait_ge(na["mm"], KC * (g + 1))
                    normalise(na, g + 1, tile_of(g + 1))
                if blocks:
                    dve.wait_ge(kv_hi, 2)
                    sub(k_lo[:, :, :], kraw[:, :, :], k_hi[:, :, :]).then_inc(kv_lo, 1)
                    sub(v_lo[:, :, :, :], vraw[:, :, :, :], v_hi[:, :, :, :]).then_inc(kv_lo, 1)
                for c in range(KC):
                    dve.wait_ge(q_hi, KC * g + c + 1)
                    sub(q_all[:, 2 * c + 1, ds(g * GW, GW)], ps[:, 2 + c, :], q_all[:, 2 * c, ds(g * GW, GW)]
                        ).then_inc(q_lo, 1)

            dve.wait_ge(x_in, 16 * (NG - 1))
            with dve.Fori(0, NG - 2) as g:
                ch.enter(g, 1)
                queries(g)
                ch.leave(NG - 2)
            queries(NG - 2, blocks=True)
            queries(NG - 1, more=False)

            def top_of(n, u):
                dve.wait_ge(s_mm, n + 1)
                v.tensor_reduce(m_u[:, u, :].rearrange("p (a h) -> p a h", a=2),
                                ps[:, 2 * u:2 * u + 2, 0:HB].rearrange("p a (h k) -> p a h k", k=NKEY),
                                AX.X, ALU.max).then_inc(s_max, 1)

            def step(n, u, i1, prev=True, nxt=True):
                w = 1 - u
                if prev:
                    dve.wait_ge(pt_hs, 2 * n - 1)
                    sub(pt_lo[:, 0:3, :], ps[:, 4, 0:3 * P].rearrange("p (c n) -> p c n", c=3), pt_hi[:, 0:3, :]).then_inc(pt_ls, 1)
                    dve.wait_ge(pt_hs, 2 * n)
                    sub(pt_lo[:, 3:5, :], ps[:, 5, 0:2 * P].rearrange("p (c n) -> p c n", c=2), pt_hi[:, 3:5, :]).then_inc(pt_ls, 1)
                if nxt:
                    top_of(n + 1, w)
                if prev:
                    dve.wait_ge(pv_mm, n)
                    o = ps[:, 6 + w, 0:UH * VW].rearrange("p (h c) -> p h c", c=VW)
                    link(v.reciprocal(rden[:, w, :], o[:, :, DH:DH + 1].rearrange("p h c -> p (h c)")))
                    v.tensor_tensor(a_all[:, ds(i1, 1), w * P:(w + 1) * P].rearrange("p a (h c) -> p (a h) c", c=DH),
                                    o[:, :, 0:DH], rden[:, w, :].rearrange("p (h o) -> p h o", o=1).to_broadcast([P, UH, DH]),
                                    ALU.mult).then_inc(a_ok, 1)

            top_of(0, 0)
            step(0, 0, 0, prev=False)
            dve.wait_ge(v1_hs, 1)
            sub(vp_lo[:, :, :], ps[0:NKEY, 4, :].rearrange("p (b n) -> p b n", b=BATCH), vp_hi[:, :, :]).then_inc(v1_ls, 1)
            dve.wait_ge(g_hs, KC)
            for c in range(KC):
                sub(g_lo[:, c, :, 0:NKEY], ps[:, 6 + c, 0:BATCH * NKEY].rearrange("p (b k) -> p b k", b=BATCH),
                    g_hi[:, c, :, 0:NKEY])
            v.tensor_copy(c0[:, :, 0:NKEY], ps[0:1, 6, 2 * P:2 * P + BATCH * NKEY].rearrange("p (b k) -> p b k", b=BATCH)
                          ).then_inc(g_ls, 1)
            for c in range(KC):
                v.tensor_copy(g_lo[:, c, :, NKEY:KP], zpad[:, 0:BATCH].rearrange("p (b k) -> p b k", b=BATCH))
                v.tensor_copy(g_hi[:, c, :, NKEY:KP], zpad[:, 0:BATCH].rearrange("p (b k) -> p b k", b=BATCH)
                              ).then_inc(g_ls, 1)
            step(1, 1, 0)
            dve.wait_ge(ws0_hi, 3)
            sub(wc_lo[:, :, :], wraw2[:, :, :], wc_hi[:, :, :]).then_inc(ws0_lo, 1)
            sub(rw_lo[:, :, :, :], rw[:, :, :, :], rw_hi[:, :, :, :]).then_inc(ws0_lo, 1)
            with dve.Fori(1, NT - 1) as i:
                ch.enter(i, 2, 1)
                step(2 * i, 0, i - 1)
                step(2 * i + 1, 1, i)
                ch.leave(NT - 2)
            step(2 * NT - 2, 0, NT - 2)
            step(2 * NT - 1, 1, NT - 1, nxt=False)
            step(2 * NT, 0, NT - 1, nxt=False)

            def project(g, cur=True, prev=True, last=True):
                if cur:
                    for c in range(KC):
                        dve.wait_ge(at_hi, KC * g + c + 1)
                        sub(na["t_lo"][:, c, :], ps[:, c, :], na["t_hi"][:, c, :]).then_inc(at_lo, 1)
                if prev:
                    dve.wait_ge(x1_ok, 2 * g)
                    statistics(nb, tile_of(g - 1))
                    if last:
                        dve.wait_ge(xn_st, 16 * (g - 1))
                    normalise(nb, g - 1, tile_of(g - 1))
                if last:
                    dve.wait_ge(lg_mm[0], g - 1)
                    v.tensor_copy(group(lg, g - 2), ps[:, 6, 0:GT * E].rearrange("p (t e) -> p t e", e=E)
                                  ).then_inc(lg_ok, 1)
                if cur:
                    for h in range(2):
                        dve.wait_ge(cc_mm, 2 * g + h + 1)
                        x2t = x_all[:, ds(g * GT + 2 * h, 2), :]
                        v.tensor_tensor(x2t, ps[:, 2 + h, :].rearrange("p (t d) -> p t d", t=2), x2t, ALU.add
                                        ).then_inc(x1_ok, 1)
                if prev:
                    split_lo(nb, g - 1, 4)

            project(0, prev=False, last=False)
            project(1, last=False)
            with dve.Fori(2, NG) as g:
                ch.enter(g, 1, 2)
                project(g)
                ch.leave(NG - 2)
            project(NG, cur=False)
            dve.wait_ge(lg_mm[0], NG)
            v.tensor_copy(lg[:, (NG - 1) * GT:NG * GT, :], ps[:, 6, 0:GT * E].rearrange("p (t e) -> p t e", e=E)
                          ).then_inc(lg_ok, 1)

            s_lo32 = s_lo[:, :, :].bitcast(f32)

            def choose(n, r):
                link(v.tensor_reduce(mx[:, :], lg[:, :, :], AX.X, ALU.max))
                sub(pr[:, :, :], lg[:, :, :], b_tile(mx[:, :])).then_inc(r["sub"], 1)
                dve.wait_ge(r["exp"], 1)
                link(v.tensor_reduce(mx[:, :], pr[:, :, :], AX.X, ALU.add))
                link(v.reciprocal(mx[:, :], mx[:, :]))
                link(v.tensor_tensor(pr[:, :, :], pr[:, :, :], b_tile(mx[:, :]), ALU.mult))
                for c in range(2):
                    link(v.tensor_reduce(top[:, c, :], pr[:, :, :], AX.X, ALU.max))
                    link(v.tensor_tensor(key[:, :, :], pr[:, :, :], b_tile(top[:, c, :]), ALU.is_equal))
                    link(v.tensor_tensor(key[:, :, :], key[:, :, :], rank_e[:, :, :], ALU.mult))
                    link(v.tensor_reduce(mx[:, :], key[:, :, :], AX.X, ALU.max))
                    link(v.tensor_tensor(oh[:, c, :, :], key[:, :, :], b_tile(mx[:, :]), ALU.is_equal))
                    if c == 0:
                        link(v.scalar_tensor_tensor(pr[:, :, :], oh[:, 0, :, :], -2.0, pr[:, :, :], ALU.mult, ALU.add))
                v.tensor_tensor(msk[:, :, :], oh[:, 0, :, :], oh[:, 1, :, :], ALU.add).then_inc(r["msk"], 1)
                if n == 0:
                    link(v.tensor_tensor(mx[:, :], top[:, 0, :], top[:, 1, :], ALU.add))
                    link(v.reciprocal(mx[:, :], mx[:, :]))
                    for c in range(2):
                        link(v.tensor_tensor(wts[:, c, :], top[:, c, :], mx[:, :], ALU.mult))
                    link(v.tensor_tensor(key[:, :, :], oh[:, 0, :, :], b_tile(wts[:, 0, :]), ALU.mult))
                    link(v.tensor_tensor(tmp3[:, :, :], oh[:, 1, :, :], b_tile(wts[:, 1, :]), ALU.mult))
                    link(v.tensor_tensor(key[:, :, :], key[:, :, :], tmp3[:, :, :], ALU.add))
                    v.tensor_reduce(wsum[:, :], key[:, :, :].rearrange("p t e -> p e t"), AX.X, ALU.add).then_inc(ws_ok, 1)
                else:
                    link(v.tensor_copy(s_hi[:, :, :], top[:, :, :]))
                    link(sub(s_lo[:, :, :], top[:, :, :], s_hi[:, :, :]))

            def place(n, r):
                dve.wait_ge(r["mm"], 1)
                link(v.tensor_copy(tot[:, :, :], ps[:, 0, P:2 * P].rearrange("p (t e) -> p e t", e=E)))
                link(v.tensor_tensor_scan(cum[:, :, :].rearrange("p e t -> p (e t)"), ones[:, :],
                                          tot[:, :, :].rearrange("p e t -> p (e t)"), 0.0, ALU.mult, ALU.add))
                link(v.tensor_reduce(n_e[:, :], tot[:, :, :], AX.X, ALU.add))
                link(v.tensor_tensor(cmp_k[:, :, :], b_tile(n_e[:, :]), step_k[:, :, :], ALU.is_gt))
                link(v.tensor_reduce(c_e[:, :], cmp_k[:, :, :], AX.X, ALU.add))
                link(v.tensor_tensor_scan(cb_e[:, :], ones[:, 0:E], c_e[:, :], 0.0, ALU.mult, ALU.add))
                link(sub(d_e[:, :], cb_e[:, :], c_e[:, :]))
                link(v.scalar_tensor_tensor(d_e[:, :], d_e[:, :], float(FT),
                                            cum[:, :, NT - 1:NT].rearrange("p e o -> p (e o)"), ALU.mult, ALU.subtract))
                link(v.tensor_tensor(d_e[:, :], d_e[:, :], n_e[:, :], ALU.add))
                link(sub(cum[:, :, :], cum[:, :, :], tot[:, :, :]))
                link(v.tensor_tensor(cum[:, :, :], cum[:, :, :], b_tile(d_e[:, :], NT), ALU.add))
                link(v.tensor_tensor(slot[:, :, :], ps[:, 0, 0:P].rearrange("p (t e) -> p t e", e=E),
                                     cum[:, :, :].rearrange("p e t -> p t e"), ALU.add))
                for c in range(2):
                    link(v.tensor_tensor(key[:, :, :], oh[:, c, :, :], slot[:, :, :], ALU.mult))
                    link(v.tensor_reduce(slot2[:, c, :], key[:, :, :], AX.X, ALU.add))
                link(v.tensor_copy(slot_i[:, :, :], slot2[:, :, :]))
                v.tensor_scalar(sb_i[:, :, :], slot_i[:, :, :], P - 1, None, ALU.bitwise_and)
                link(v.tensor_scalar(sa_i[:, :, :], slot_i[:, :, :], 7, None, ALU.arith_shift_right))
                v.tensor_copy(sb_f[:, :, :], sb_i[:, :, :])
                link(v.tensor_copy(sa_f[:, :, :], sa_i[:, :, :]))
                for h in range(2):
                    ts = slice(h * NT // 2, (h + 1) * NT // 2)
                    for c in range(2):
                        ins = v.tensor_tensor(oh_a[:, c, ts, :], b_row(iota_h[:, :], NT // 2), b_tile(sa_f[:, c, ts], SH),
                                              ALU.is_equal)
                    ins.then_inc(r["place"], 1)
                link(v.tensor_tensor(cmp_t[:, :, :], tile_t[:, :, :], b_row(cb_e[:, 0:E - 1], ST + 1), ALU.is_ge))
                link(v.tensor_reduce(eid_f[:, :], cmp_t[:, :, :], AX.X, ALU.add))
                v.tensor_copy(eid[n][:, :], eid_f[0:1, :]).then_inc(r["eid"], 1)
                for h in range(2):
                    ts = slice(h * NT // 2, (h + 1) * NT // 2)
                    for c in range(2):
                        if n == 1:
                            v.tensor_tensor(oha[:, c, ts, 2, :], oh_a[:, c, ts, :], b_tile(s_lo32[:, c, ts], SH), ALU.mult)
                        v.tensor_tensor(ohb[:, c, ts, :], b_row(iota_p[:, :], NT // 2), b_tile(sb_f[:, c, ts], P),
                                        ALU.is_equal).then_inc(r["ohb"], 1)
                if n == 0:
                    dve.wait_ge(ws_mm, 1)
                    link(v.tensor_scalar(d_e[:, :], n_e[:, :], 1.0, None, ALU.max))
                    link(v.reciprocal(d_e[:, :], d_e[:, :]))
                    link(v.tensor_tensor(mw_e[:, :], ps[:, 1, 0:E], d_e[:, :], ALU.mult))
                    link(v.tensor_tensor(cmp_m[:, :, :], iota_m[:, :, :], b_tile(eid_f[:, :]), ALU.is_equal))
                    link(v.tensor_tensor(cmp_m[:, :, :], cmp_m[:, :, :],
                                         mw_e[:, :].rearrange("p (o e) -> p o e", o=1).to_broadcast([P, ST + 1, E]), ALU.mult))
                    link(v.tensor_reduce(mw_t[:, :], cmp_m[:, :, :], AX.X, ALU.add))

            def tables(n, r):
                parts = 1 if n == 0 else 3
                dve.wait_ge(r["inv"], 1)
                link(v.tensor_copy(inv[:, 0:parts, :], ps[:, 2, 0:parts * SH].rearrange("p (k a) -> p k a", k=parts)))
                link(v.tensor_scalar(gat_f[:, :], inv[:, 0, :], -1.0, 0.0, ALU.add, ALU.max))
                link(v.tensor_copy(gat[n][:, :], gat_f[:, :]))
                link(v.tensor_scalar(inv[:, 0, :], inv[:, 0, :], 0.0, None, ALU.is_equal))
                link(v.tensor_tensor(inv[:, 0, :], inv[:, 0, :], pad_row[:, :, :].rearrange("p t h -> p (t h)"), ALU.mult))
                if n == 1:
                    link(v.tensor_tensor(score[:, :], inv[:, 1, :], inv[:, 2, :], ALU.add))
                link(v.tensor_tensor(gat_f[:, :], gat_f[:, :], inv[:, 0, :], ALU.add))
                v.tensor_copy(sca[n][:, :], gat_f[:, :]).then_inc(r["tab"], 1)

            dve.wait_ge(lg_ok, NG)
            choose(0, r0)
            place(0, r0)
            tables(0, r0)

            def w0_lo(t, b):
                dve.wait_ge(f0["w_hi"], NB0 * t + b + 1)
                sub(w_lo[:, b, :], wr[:, b, :], w_hi[:, b, :]).then_inc(f0["w_lo"], 1)

            def x_lo(f, t, p=0):
                dve.wait_ge(f["xt_hi"], t + 1)
                sub(xe_lo[:, p, :, :].rearrange("p c n -> p (c n)"), ps[:, 6 + p, :],
                    xe_hi[:, p, :, :].rearrange("p c n -> p (c n)")).then_inc(f["xt_lo"], 1)

            def tile0(t, more=True):
                for q in range(G0):
                    dve.wait_ge(f0["silu"], G0 * t + q + 1)
                    v.tensor_tensor(hf[:, q % 2, :], ps[:, 2 + q % 2, :], sg[:, q % 2, :], ALU.mult).then_inc(f0["h_mul"], 1)
                    if more and q < G0 - 1:
                        w0_lo(t + 1, q)
                    dve.wait_ge(f0["h_hi"], G0 * t + q + 1)
                    sub(h_lo[:, q, :, :].rearrange("p c n -> p (c n)"), hf[:, q % 2, :],
                        h_hi[:, q, :, :].rearrange("p c n -> p (c n)")).then_inc(f0["h_lo"], 1)
                if more:
                    w0_lo(t + 1, G0 - 1)
                    x_lo(f0, t + 1)
                    w0_lo(t + 1, G0)
                    w0_lo(t + 1, G0 + 1)

            for b in range(NB0):
                w0_lo(0, b)
            x_lo(f0, 0)
            with dve.Fori(0, ST - 1) as t:
                tile0(t)
            tile0(ST - 1, more=False)

            dve.wait_ge(wss_hi, 1)
            sub(ws_lo[:, :, :, :], wsr, ws_hi[:, :, :, :]).then_inc(wss_lo, 1)

            def gated(g, i):
                dve.wait_ge(ss_ok, KC * (g - 1) + i + 1)
                v.tensor_tensor(hfs[:, i, :], ps[:, 5 + 2 * i, :], sgs[:, i, :], ALU.mult).then_inc(shf_ok, 1)

            def split_gated(g):
                for i in range(KC):
                    dve.wait_ge(sh_hi, KC * (g - 1) + i + 1)
                    sub(hs_lo[:, i, :], hfs[:, i, :], hs_hi[:, i, :]).then_inc(sh_lo, 1)

            def group1(g, a=True, b=True, c=True, d=True):
                if b:
                    dve.wait_ge(x3_ok, GT * g)
                    statistics(nb, tile_of(g - 1))
                if a:
                    split_lo(na, NG + g, 0)
                if c:
                    dve.wait_ge(x2_in[2] if b else x2_in[1], 16 * (NG - 2) if b else 16)
                    statistics(na, tile_of(g + 1))
                if b:
                    if d:
                        dve.wait_ge(xm_st, 16 * (g - 1))
                    normalise(nb, NG + g - 1, tile_of(g - 1))
                if d:
                    for h in range(2):
                        dve.wait_ge(sd_mm, 2 * (g - 2) + h + 1)
                        x2t = x_all[:, ds((g - 2) * GT + 2 * h, 2), :]
                        v.tensor_tensor(x2t, ps[:, 4 + h, :].rearrange("p (t d) -> p t d", t=2), x2t, ALU.add
                                        ).then_inc(so_ok, 1)
                if a:
                    dve.wait_ge(l_mm, g + 1)
                    link(v.tensor_reduce(m1[:, :], ps[:, 0, 0:GT * KP].rearrange("p (t k) -> p t k", k=KP)[:, :, 0:NKEY],
                                         AX.X, ALU.max))
                    v.tensor_scalar(m1[:, :], m1[:, :], -(D ** -0.5), None, ALU.mult).then_inc(l_max, 1)
                if b:
                    split_lo(nb, NG + g - 1, 2)
                if a:
                    dve.wait_ge(l_exp, GT * (g + 1))
                    dve.wait_ge(p1_hs, g + 1)
                    sub(pt1_lo[:, :, :].rearrange("p c n -> p (c n)"), ps[0:NKEY, 1, :],
                        pt1_hi[:, :, :].rearrange("p c n -> p (c n)")).then_inc(p1_ls, 1)
                    link(v.reciprocal(den1[:, :], den1[:, :]))
                if c:
                    normalise(na, NG + g + 1, tile_of(g + 1))

                if b and a:
                    gated(g, 0)
                if a:
                    for j in range(GT):
                        dve.wait_ge(o1_mm, GT * g + 2 * (j // 2) + 2)
                        xt = tile_of(g)(j)
                        v.scalar_tensor_tensor(xt, ps[:, j // 2, (j % 2) * D:(j % 2 + 1) * D], den1[:, j:j + 1], xt,
                                               ALU.mult, ALU.add).then_inc(x3_ok, 1)
                if b and a:
                    gated(g, 1)
                    split_gated(g)
                if b:
                    dve.wait_ge(lg_mm[1], g)
                    v.tensor_copy(group(lg, g - 1), ps[:, 2, 0:GT * E].rearrange("p (t e) -> p t e", e=E)
                                  ).then_inc(lg_ok, 1)

            dve.wait_ge(x2_in[0], 16)
            statistics(na, tile_of(0))
            normalise(na, NG, tile_of(0))
            group1(0, b=False, d=False)
            group1(1, d=False)
            with dve.Fori(2, NG - 1) as g:
                ch.enter(g, 4, 2)
                group1(g)
                ch.leave(NG - 3)
            group1(NG - 1, c=False)
            group1(NG, a=False, c=False)
            dve.wait_ge(lg_ok, 2 * NG)
            choose(1, r1)
            gated(NG, 0)
            gated(NG, 1)
            split_gated(NG)
            place(1, r1)
            group1(NG + 1, a=False, b=False, c=False)
            tables(1, r1)
            def scale1(i, p):
                dve.wait_ge(x1_in[p], 32 * (i + 1))
                v.tensor_scalar(xr[:, p, 1, :], xr[:, p, 1, :], score[:, ds(4 * i + 2 * p + 1, 1)], None,
                                ALU.mult).then_inc(x_sc[1], 1)

            def w1_lo(t, p, b):
                dve.wait_ge((f1["w_hi"], wd_hi)[b], t + 1)
                n = WB if b == 0 else WB // 2
                sub(w_lo[:, 2 * p + b, 0:n], wr[:, 2 * p + b, 0:n], w_hi[:, 2 * p + b, 0:n]
                    ).then_inc((f1["w_lo"], wd_lo)[b], 1)

            def tile1(i, p, x1=True, x2=True, x3=True):
                t, o = 2 * i + p, 1 - p
                dve.wait_ge(f1["silu"], t + 1)
                v.tensor_tensor(hf[:, p, :], ps[:, 2 * p + 1, :], sg[:, p, :], ALU.mult).then_inc(f1["h_mul"], 1)
                if x2:
                    x_lo(f1, t + 2, p)
                dve.wait_ge(f1["h_hi"], t + 1)
                sub(h_lo[:, p, :, :].rearrange("p c n -> p (c n)"), hf[:, p, :],
                    h_hi[:, p, :, :].rearrange("p c n -> p (c n)")).then_inc(f1["h_lo"], 1)
                if x2:
                    w1_lo(t + 2, p, 0)
                if x1:
                    w1_lo(t + 1, o, 1)
                if x3:
                    scale1(i + 1 + p, o)

            w1_lo(0, 0, 0)
            w1_lo(1, 1, 0)
            scale1(0, 0)
            scale1(0, 1)
            x_lo(f1, 0, 0)
            w1_lo(0, 0, 1)
            x_lo(f1, 1, 1)
            scale1(1, 0)
            with dve.Fori(0, (ST - 3) // 2) as i:
                tile1(i, 0)
                tile1(i, 1)
            tile1((ST - 3) // 2, 0, x3=False)
            tile1((ST - 3) // 2, 1, x2=False, x3=False)
            tile1(ST // 2, 0, x1=False, x2=False, x3=False)

        @block.tensor
        def _(pe):
            T = nc.tensor

            def transpose_group(n, k, b0):
                pe.wait_ge(n["xn"], k + 1)
                for c in range(KC):
                    for j in range(GT):
                        ins = T.transpose(ps[:, b0 + c, j * P:(j + 1) * P], n["x"][:, j, c * P:(c + 1) * P], ident[:, :])
                    ins.then_inc(n["mm"], 1)

            def w3(wh, wl, xh, xl, cols_w, cols_x):
                return [(wh[:, c, cols_w], wl[:, c, cols_w], xh[:, c, cols_x], xl[:, c, cols_x]) for c in range(KC)]

            pe.wait_ge(c_in, 32)
            for c in range(KC):
                mm(ps[0:DH, 0, 0:BATCH * NKEY], wkv[:, c, 0:DH], ctxT[:, c, :], c == 0, c == KC - 1)
            for b in range(BATCH):
                for c in range(KC):
                    ins = mm(ps[0:NKEY, 0, 2 * P + b * DH:2 * P + (b + 1) * DH], ctxT[:, c, b * NKEY:(b + 1) * NKEY],
                             wkv[:, c, DH:2 * DH], c == 0, c == KC - 1)
            ins.then_inc(kv_mm, 1)
            pe.wait_ge(l1_in, 96)
            for e in range(KC):
                for c in range(KC):
                    ins = mm(ps[:, 4 + e, 0:BATCH * NKEY], w1k[:, c, e * P:(e + 1) * P], ctxT[:, c, :], c == 0, c == KC - 1)
                ins.then_inc(kp_mm, 1)
            pe.wait_ge(ident_ok, 1)
            pe.wait_ge(kv_sb, 2)

            def layer1_values():
                for b in range(BATCH):
                    out = ps[0:NKEY, 4, b * D:(b + 1) * D]
                    mm(out, ones[0:1, 0:NKEY], bv[:, :], True, False)
                    for c in range(KC):
                        ins = mm(out, ctxT[:, c, b * NKEY:(b + 1) * NKEY], w1v[:, c, :], False, c == KC - 1)
                ins.then_inc(v1_mm, 1)

            def layer1_keys():
                for e in range(KC):
                    mm(ps[0:1, 6, 2 * P:2 * P + BATCH * NKEY], bq[:, e:e + 1], kpT[:, e, :], e == 0, e == KC - 1)
                for c in range(KC):
                    for e in range(KC):
                        ins = mm(ps[:, 6 + c, 0:BATCH * NKEY], w1qT[:, e, c * P:(c + 1) * P], kpT[:, e, :], e == 0, e == KC - 1)
                    ins.then_inc(g_mm, 1)

            pe.wait_ge(ws0_lo, 1)
            with pe.Fori(0, NG) as g:
                transpose_group(na, g, 0)
                pe.wait_ge(na["lo"], KC * (g + 1))
                for hc in range(2):
                    mm3(ps[:, 2 + hc, :], w3(wq_hi, wq_lo, na["t_hi"], na["t_lo"], slice(hc * P, (hc + 1) * P), slice(0, GW))
                        ).then_inc(q_mm, 1)

            def scores(n, u, i):
                b = i // (NT // BATCH)
                pe.wait_ge(q_cp, n + 1)
                for half in range(2):
                    out = ps[:, 2 * u + half, 0:HB]
                    kh = k_hi[:, ds(b, 1), half * HB:(half + 1) * HB].rearrange("p a n -> p (a n)")
                    kl = k_lo[:, ds(b, 1), half * HB:(half + 1) * HB].rearrange("p a n -> p (a n)")
                    mm(out, qc[u][:, 0, :], kh, True, False)
                    mm(out, qc[u][:, 0, :], kl, False, False)
                    ins = mm(out, qc[u][:, 1, :], kh, False, False)
                ins.then_inc(s_mm, 1)

            def step(n, u, i1, i2, prev=True, cur=True, nxt=True):
                w = 1 - u
                if prev:
                    pe.wait_ge(s_exp, n)
                    for j in range(3):
                        ins = T.transpose(ps[:, 4, j * P:(j + 1) * P], pb_[:, w, win(j):win(j) + P], ident[:, :])
                    ins.then_inc(pt0_mm, 1)
                    for j in range(3, NW):
                        ins = T.transpose(ps[:, 5, (j - 3) * P:(j - 2) * P], pb_[:, w, win(j):win(j) + P], ident[:, :])
                    ins.then_inc(pt1_mm, 1)
                if cur:
                    pe.wait_ge(s_max, n + 1)
                    T.transpose(ps[0:UH, 5, 3 * P:4 * P], m_u[:, u, :], ident[:, :]).then_inc(mt_mm, 1)
                if nxt:
                    scores(n + 1, w, i2)
                if cur:
                    pe.wait_ge(mt_ok, n + 1)
                    for half in range(2):
                        ins = mm(ps[:, 2 * u + half, 0:HB], mT[:, u, :], neg_head[:, half * HB:(half + 1) * HB], False, True)
                    ins.then_inc(sh_mm, 1)
                if prev:
                    b = i1 // (NT // BATCH)
                    for j in range(NW):
                        pe.wait_ge(pt_ls, 2 * n - 1 if j < 3 else 2 * n)
                        cols = slice(head(j) * VW, (head(j) + WINH) * VW)
                        vh = v_hi[:, ds(b, 1), j, cols].rearrange("p a n -> p (a n)")
                        vl = v_lo[:, ds(b, 1), j, cols].rearrange("p a n -> p (a n)")
                        out = ps[:, 6 + w, cols]
                        mm(out, pt_hi[:, j, :], vh, j == 0, False)
                        mm(out, pt_hi[:, j, :], vl, False, False)
                        ins = mm(out, pt_lo[:, j, :], vh, False, j == NW - 1)
                    ins.then_inc(pv_mm, 1)

            pe.wait_ge(kv_lo, 2)
            scores(0, 0, 0)
            pe.wait_ge(kp_sb, KC)
            layer1_values()
            pe.wait_ge(const_ok, 1)
            pe.wait_ge(q_lo, KC * NG)
            step(0, 0, 0, 0, prev=False)
            layer1_keys()
            pe.wait_ge(v1_ls, 1)
            pe.wait_ge(g_ls, 1)
            step(1, 1, 0, 1)
            with pe.Fori(1, NT - 1) as i:
                step(2 * i, 0, i - 1, i)
                step(2 * i + 1, 1, i, i + 1)
            step(2 * NT - 2, 0, NT - 2, NT - 1)
            step(2 * NT - 1, 1, NT - 1, NT - 1, nxt=False)
            step(2 * NT, 0, NT - 1, NT - 1, cur=False, nxt=False)

            def logits(L, n, k, bank_):
                pe.wait_ge(n["lo"], KC * (k + 1))
                for j in range(GT):
                    ins = mm3(ps[:, bank_, j * E:(j + 1) * E],
                              [(n["t_hi"][:, c, j * P:(j + 1) * P], n["t_lo"][:, c, j * P:(j + 1) * P],
                                rw_hi[:, L, c, :], rw_lo[:, L, c, :]) for c in range(KC)])
                ins.then_inc(lg_mm[L], 1)

            def project(g, cur=True, prev=True, last=True):
                if cur:
                    pe.wait_ge(ac_ok, g + 1)
                    for c in range(KC):
                        for j in range(GT):
                            ins = T.transpose(ps[:, c, j * P:(j + 1) * P], a_cur[:, j, c * P:(c + 1) * P], ident[:, :])
                        ins.then_inc(at_mm, 1)
                if last:
                    logits(0, nb, g - 2, 6)
                if cur:
                    pe.wait_ge(at_lo, KC * (g + 1))
                    for j in range(GT):
                        ins = mm3(ps[:, 2 + j // 2, (j % 2) * D:(j % 2 + 1) * D],
                                  [(na["t_hi"][:, c, j * P:(j + 1) * P], na["t_lo"][:, c, j * P:(j + 1) * P],
                                    wc_hi[:, c, :], wc_lo[:, c, :]) for c in range(KC)])
                        if j % 2:
                            ins.then_inc(cc_mm, 1)
                if prev:
                    transpose_group(nb, g - 1, 4)

            pe.wait_ge(ws0_lo, 3)
            project(0, prev=False, last=False)
            project(1, last=False)
            with pe.Fori(2, NG) as g:
                project(g)
            project(NG, cur=False)
            project(NG + 1, cur=False, prev=False)

            def count(n, r):
                pe.wait_ge(r["msk"], 1)
                m2 = msk[:, :, :].rearrange("p t e -> p (t e)")
                mm(ps[:, 0, 0:P], upperb[:, :], m2, True, True)
                mm(ps[:, 0, P:2 * P], onesb[:, :], m2, True, True).then_inc(r["mm"], 1)
                if n == 0:
                    pe.wait_ge(ws_ok, 1)
                    mm(ps[:, 1, 0:E], ones[:, :], wsum[:, :], True, True).then_inc(ws_mm, 1)
            def invert(r, parts):
                for t in range(NT):
                    if t % (NT // 2) == 0:
                        pe.wait_ge(r["ohb"], 2 + 4 * t // NT)
                        pe.wait_ge(r["oha"], 1 + 2 * t // NT)
                    for c in range(2):
                        ins = mm(ps[:, 2, 0:parts * SH], ohb[:, c, t, :],
                                 oha[:, c, t, 0:parts, :].rearrange("p k a -> p (k a)"),
                                 t == 0 and c == 0, t == NT - 1 and c == 1)
                ins.then_inc(r["inv"], 1)

            count(0, r0)
            invert(r0, 1)

            def transpose_x(f, p):
                for c in range(KC):
                    for half in range(2):
                        ins = T.transpose(ps[:, 6 + p, c * FT + half * P:c * FT + (half + 1) * P],
                                          xr[:, p, half, c * P:(c + 1) * P], ident[:, :])
                ins.then_inc(f["xt_mm"], 1)

            def transpose0(t):
                pe.wait_ge(x0_in, 32 * (t + 1))
                transpose_x(f0, 0)

            def gate_up(wb, bg, bu, p):
                for which, bk_ in ((0, bg), (1, bu)):
                    for j in range(2):
                        cols = [slice(c * 512 + which * 256 + j * P, c * 512 + which * 256 + (j + 1) * P) for c in range(KC)]
                        ins = mm3(ps[:, bk_, j * FT:(j + 1) * FT],
                                  [(w_hi[:, wb, cols[c]], w_lo[:, wb, cols[c]], xe_hi[:, p, c, :], xe_lo[:, p, c, :])
                                   for c in range(KC)])
                return ins

            def down(k, half, wb, start, stop, row=None):
                q, j = k // 2 if row is None else row, k % 2
                out, hs = ps[:, 4 + half, 0:D], slice(half * P, (half + 1) * P)
                ws = slice((k % 4) * D, (k % 4 + 1) * D)
                mm(out, h_hi[:, q, j, hs], w_hi[:, wb, ws], start, False)
                mm(out, h_hi[:, q, j, hs], w_lo[:, wb, ws], False, False)
                return mm(out, h_lo[:, q, j, hs], w_hi[:, wb, ws], False, stop)

            def tile0(t, first=False, more=True):
                pe.wait_ge(f0["xt_lo"], t + 1)
                for q in range(G0):
                    pe.wait_ge(f0["w_lo"], NB0 * t + q + 1)
                    if not first or q >= 2:
                        pe.wait_ge(f0["h_mul"], G0 * t + q - 1)
                    gate_up(q, q % 2, 2 + q % 2, 0).then_inc(f0["gu_mm"], 1)
                if more:
                    transpose0(t + 1)
                pe.wait_ge(f0["w_lo"], NB0 * t + NB0)
                if not first:
                    pe.wait_ge(f0["y_ok"], 2 * t)
                for part in (range(0, 6), range(6, 8)):
                    for half in range(2):
                        for k in part:
                            pe.wait_ge(f0["h_lo"], G0 * t + k // 2 + 1)
                            ins = down(k, half, G0 + k // 4, k == 0, k == 7)
                        if k == 7:
                            ins.then_inc(f0["d_mm"], 1)

            transpose0(0)
            tile0(0, first=True)
            with pe.Fori(1, ST - 1) as t:
                tile0(t)
            tile0(ST - 1, more=False)

            pe.wait_ge(wss_lo, 1)
            pe.wait_ge(g_ls, 1 + KC)

            def group1(g, a=True, b=True, d=True):
                bt = g // (NG // BATCH)
                thi, tlo = na["t_hi"], na["t_lo"]

                def shared(c):
                    for which in range(2):
                        ins = mm3(ps[:, 4 + 2 * c + which, :],
                                  [(ws_hi[:, which, k, c * P:(c + 1) * P], ws_lo[:, which, k, c * P:(c + 1) * P],
                                    nb["t_hi"][:, k, :], nb["t_lo"][:, k, :]) for k in range(KC)])
                    ins.then_inc(sgu_mm, 1)

                def scores():
                    pe.wait_ge(na["lo"], KC * (NG + g + 1))
                    for j in range(GT):
                        out = ps[:, 0, j * KP:(j + 1) * KP]
                        mm(out, ones[0:1, :], c0[:, ds(bt, 1), :].rearrange("p a n -> p (a n)"), True, False)
                        for c in range(KC):
                            gh = g_hi[:, c, ds(bt, 1), :].rearrange("p a n -> p (a n)")
                            gl = g_lo[:, c, ds(bt, 1), :].rearrange("p a n -> p (a n)")
                            mm(out, thi[:, c, j * P:(j + 1) * P], gh, False, False)
                            mm(out, thi[:, c, j * P:(j + 1) * P], gl, False, False)
                            ins = mm(out, tlo[:, c, j * P:(j + 1) * P], gh, False, c == KC - 1)
                    ins.then_inc(l_mm, 1)

                def shared_down():
                    pe.wait_ge(sh_lo, KC * (g - 1))
                    for j in range(GT):
                        ins = mm3(ps[:, 4 + j // 2, (j % 2) * D:(j % 2 + 1) * D],
                                  [(hs_hi[:, c, j * P:(j + 1) * P], hs_lo[:, c, j * P:(j + 1) * P],
                                    ws_hi[:, 2, c, :], ws_lo[:, 2, c, :]) for c in range(KC)])
                        if j % 2:
                            ins.then_inc(sd_mm, 1)

                if a:
                    if b:
                        pe.wait_ge(x3_ok, GT * g)
                    transpose_group(na, NG + g, 0)
                if d:
                    shared_down()
                if a:
                    scores()
                if b:
                    if d:
                        pe.wait_ge(lg_ok, NG + g - 1)
                    transpose_group(nb, NG + g - 1, 2)
                if a:
                    pe.wait_ge(l_exp, GT * (g + 1))
                    for j in range(GT):
                        ins = T.transpose(ps[0:NKEY, 1, j * P:(j + 1) * P], p1[:, j, 0:NKEY], ident[:, :])
                    ins.then_inc(p1_mm, 1)
                if b:
                    pe.wait_ge(nb["lo"], KC * (NG + g))
                    if not a:
                        logits(1, nb, NG + g - 1, 2)
                    if d:
                        pe.wait_ge(so_ok, 2 * (g - 1))
                    shared(0)
                if a:
                    pe.wait_ge(p1_ls, g + 1)
                    for j in range(GT):
                        out = ps[:, j // 2, (j % 2) * D:(j % 2 + 1) * D]
                        vh = vp_hi[:, ds(bt, 1), :].rearrange("p a n -> p (a n)")
                        vl = vp_lo[:, ds(bt, 1), :].rearrange("p a n -> p (a n)")
                        mm(out, pt1_hi[:, j, :], vh, True, False)
                        mm(out, pt1_hi[:, j, :], vl, False, False)
                        mm(out, pt1_lo[:, j, :], vh, False, True).then_inc(o1_mm, 1)
                if b:
                    shared(1)
                    if a:
                        logits(1, nb, NG + g - 1, 2)

            group1(0, b=False, d=False)
            group1(1, d=False)
            with pe.Fori(2, NG) as g:
                group1(g)
            group1(NG, a=False)
            count(1, r1)
            group1(NG + 1, a=False, b=False)
            invert(r1, 3)

            def transpose1(t, p):
                for h in range(2):
                    pe.wait_ge(x_sc[h], t + 1)
                transpose_x(f1, p)

            def down1(t, p, first=False):
                pe.wait_ge(f1["h_lo"], t + 1)
                pe.wait_ge(wd_lo, t + 1)
                if not first:
                    pe.wait_ge(f1["y_ok"], 2 * t)
                for half in range(2):
                    for k in range(2):
                        ins = down(k, half, 2 * p + 1, k == 0, k == 1, row=p)
                    ins.then_inc(f1["d_mm"], 1)

            def tile1(t, p, start=False, more=True):
                pe.wait_ge(f1["xt_lo"], t + 1)
                pe.wait_ge(f1["w_lo"], t + 1)
                if not start:
                    pe.wait_ge(f1["h_mul"], t - 1)
                gate_up(2 * p, 2 * p, 2 * p + 1, p).then_inc(f1["gu_mm"], 1)
                if more:
                    transpose1(t + 2, p)

            transpose1(0, 0)
            transpose1(1, 1)
            tile1(0, 0, start=True)
            tile1(1, 1, start=True)
            down1(0, 0, first=True)
            with pe.Fori(1, (ST - 3) // 2) as i:
                tile1(2 * i, 0)
                down1(2 * i - 1, 1)
                tile1(2 * i + 1, 1)
                down1(2 * i, 0)
            tile1(ST - 3, 0)
            down1(ST - 4, 1)
            tile1(ST - 2, 1, more=False)
            down1(ST - 3, 0)
            tile1(ST - 1, 0, more=False)
            down1(ST - 2, 1)
            down1(ST - 1, 0)


def kernel(**inputs):
    import numpy as _np
    import concourse.bacc as _bacc
    from concourse import mybir as _mybir
    from concourse.bass_utils import run_bass_kernel_spmd as _run

    a = {k: _np.asarray(v) for k, v in inputs.items()}

    def parts(w):
        return w.reshape(KC, P, -1).transpose(1, 0, 2)

    def expert_up(gate, up, groups):
        w = _np.stack([gate, up], axis=1).reshape(E, 2, KC, P, groups, 2 * P)
        return w.transpose(0, 4, 3, 2, 1, 5).reshape(E, groups, P, -1)

    def expert_down(w, groups):
        return w.reshape(E, groups, -1, P, D).transpose(0, 1, 3, 2, 4).reshape(E, groups, P, -1)

    up0 = expert_up(a["L0_ffn_gate_w"].transpose(0, 2, 1), a["L0_ffn_up_w"].transpose(0, 2, 1), G0)
    down0 = expert_down(a["L0_ffn_down_w"].transpose(0, 2, 1), NB0 - G0)
    arrays = {
        "x": a["x"].reshape(NT, P, D).transpose(1, 0, 2),
        "ctxT": parts(a["ctx_1024"].reshape(BATCH * NKEY, D).T),
        "wkv": parts(a["L0_xattn_w_kv"]),
        "wq": parts(a["L0_xattn_w_q"]),
        "wc": parts(a["L0_xattn_w_concat"]),
        "rw": _np.stack([parts(a["L0_ffn_router_w"].T), parts(a["L1_ffn_gate_w"].T)], axis=1),
        "w1k": parts(a["L1_xattn_Wk"]),
        "w1qT": parts(a["L1_xattn_Wq"].T),
        "w1v": parts(a["L1_xattn_Wv"]),
        "bk": a["L1_xattn_bk"].reshape(KC, P).T,
        "bq": a["L1_xattn_bq"].reshape(KC, P).T,
        "bv": a["L1_xattn_bv"].reshape(1, D),
        "w0": _np.concatenate([up0, down0], axis=1).reshape(E * NB0 * P, WB),
        "w1gu": expert_up(a["L1_ffn_w1"], a["L1_ffn_w3"], 1).reshape(E * P, WB),
        "w1d": expert_down(a["L1_ffn_w2"], 1).reshape(E * P, WB // 2),
        "ws": _np.stack([parts(a["L1_ffn_w1s"][0]), parts(a["L1_ffn_w3s"][0]), parts(a["L1_ffn_w2s"][0])], axis=1),
    }
    arrays = {k: _np.ascontiguousarray(v) for k, v in arrays.items()}
    nc = _bacc.Bacc("TRN2", target_bir_lowering=False, num_devices=1)
    A = {k: nc.dram_tensor(f"in_{k}", v.shape, _mybir.dt.from_np(v.dtype), kind="ExternalInput").ap()
         for k, v in arrays.items()}
    A["out"] = nc.dram_tensor("out", (ROWS, D), _mybir.dt.float32, kind="ExternalOutput").ap()
    build_program(nc, A)
    r = _run(nc, [{f"in_{k}": v for k, v in arrays.items()}], core_ids=[0])
    return r.results[0]["out"][:NT * P].reshape(BATCH, SEQ, D)
```

```python
import numpy as np
import concourse.bass as bass
from concourse import mybir
from contextlib import ExitStack

P = 128
D = 256
KC = D // P
BATCH, SEQ, NKEY = 2, 1024, 77
NT = BATCH * SEQ // P
GT = 4
NG = NT // GT
GW = GT * P
HEADS, DH = 16, 16
UH = 8
UW = UH * NKEY
HB = UW // 2
NW = -(-UW // P)
VW = DH + 2
WINH = 3
KP = NKEY + 1
E = 8
FT = 256
ST = (NT * P * 2 + E * (FT - 1)) // FT
SH = ST * 2
ROWS = NT * P + 2 * P
F0, F1 = 1024, 256
G0 = F0 // (2 * P)
WB = 1024
NB0 = 6
EPS = 1e-5


class Count:

    def __init__(self, sem):
        self.sem, self.base, self.n, self.start = sem, 0, 0, 0

    def up(self, k=1):
        self.n += k
        return self.base + self.n

    def enter(self, i, per, first=0):
        self.start = self.base + self.n
        self.per, self.base, self.n = per, (i - first) * per + self.start, 0

    def leave(self, trips):
        assert self.n == self.per, (self.n, self.per)
        self.base, self.n = self.start + trips * self.per, 0


def build_program(nc, A):
    f32, f32r, bf16, i32 = (mybir.dt.float32, mybir.dt.float32r, mybir.dt.bfloat16, mybir.dt.int32)
    ALU, ACT, AX = mybir.AluOpType, mybir.ActivationFunctionType, mybir.AxisListType
    ds = bass.ds
    ctx = ExitStack()
    with ctx:
        sem = lambda name: ctx.enter_context(nc.semaphore(name))

        kblk_d = nc.dram_tensor("kblk_d", [BATCH, P, UW], f32).ap()
        vblk_d = nc.dram_tensor("vblk_d", [BATCH, NW * P, UH * VW], f32).ap()
        xn_d = nc.dram_tensor("xn_d", [NT * P, D], f32).ap()
        xm_d = nc.dram_tensor("xm_d", [NT * P, D], f32).ap()
        res_d = nc.dram_tensor("res_d", [ROWS, D], f32).ap()
        out_d = A["out"]

        def sb(name, shape, dt=f32, stack=ctx):
            return stack.enter_context(nc.sbuf_tensor(name, shape, dt))

        ident = sb("ident", [P, P])
        iota_p = sb("iota_p", [P, P])
        iota_h = sb("iota_h", [P, SH])
        tok1 = sb("tok1", [P, NT])
        rank_e = sb("rank_e", [P, NT, E])
        step_k = sb("step_k", [P, E, E])
        tile_t = sb("tile_t", [P, ST + 1, E - 1])
        pad_row = sb("pad_row", [P, ST, 2])
        ones = sb("ones", [P, P])
        upper = sb("upper", [P, P])
        onesb = sb("onesb", [P, P], bf16)
        upperb = sb("upperb", [P, P], bf16)
        nege = sb("nege", [UH, UW])
        neg_head = sb("neg_head", [UH, UW], f32r)
        zeros = sb("zeros", [P, 2 * NW * UH * VW])

        ctxT = sb("ctxT", [P, KC, BATCH * NKEY])
        wkv = sb("wkv", [P, KC, 2 * DH])
        wraw = sb("wraw", [P, KC, D])
        wq_hi, wq_lo = sb("wq_hi", [P, KC, D], f32r), sb("wq_lo", [P, KC, D], f32r)
        wraw2 = sb("wraw2", [P, KC, D])
        wc_hi, wc_lo = sb("wc_hi", [P, KC, D], f32r), sb("wc_lo", [P, KC, D], f32r)
        rw = sb("rw", [P, 2, KC, E])
        rw_hi, rw_lo = sb("rw_hi", [P, 2, KC, E], f32r), sb("rw_lo", [P, 2, KC, E], f32r)
        bk = sb("bk", [P, KC])
        bq = sb("bq", [P, KC])
        bv = sb("bv", [1, D])
        g_hi, g_lo = sb("g_hi", [P, KC, BATCH, KP], f32r), sb("g_lo", [P, KC, BATCH, KP], f32r)
        c0 = sb("c0", [NKEY, BATCH])
        lgT = sb("lgT", [E, GW])
        vp_hi, vp_lo = sb("vp_hi", [NKEY, BATCH, D], f32r), sb("vp_lo", [NKEY, BATCH, D], f32r)

        x_all = sb("x_all", [P, NT, D])
        lg = sb("lg", [P, NT, E])
        mhalf = sb("mhalf", [P, GT])

        def norm_set(n):
            d = {k: sb(f"{k}_{n}", shape, dt) for k, shape, dt in (
                ("st", [P, GT, 6], f32), ("mv", [P, GT, 2], f32), ("rs", [P, GT], f32), ("x", [P, GT, D], f32),
                ("t_hi", [P, KC, GW], f32r), ("t_lo", [P, KC, GW], f32r))}
            d.update({k: sem(f"n{n}_{k}") for k in ("var", "rstd", "xn", "mm", "hi", "lo")})
            return d

        na, nb = norm_set("a"), norm_set("b")

        mx = sb("mx", [P, NT])
        pr = sb("pr", [P, NT, E])
        key = sb("key", [P, NT, E])
        top = sb("top", [P, 2, NT])
        oh = sb("oh", [P, 2, NT, E])
        msk = sb("msk", [P, NT, E], bf16)
        tmp3 = sb("tmp3", [P, NT, E])
        tot = sb("tot", [P, E, NT])
        cum = sb("cum", [P, E, NT])
        n_e = sb("n_e", [P, E])
        c_e = sb("c_e", [P, E])
        cb_e = sb("cb_e", [P, E])
        d_e = sb("d_e", [P, E])
        cmp_k = sb("cmp_k", [P, E, E])
        slot = sb("slot", [P, NT, E])
        slot2 = sb("slot2", [P, 2, NT])
        slot_i = sb("slot_i", [P, 2, NT], i32)
        sa_i = sb("sa_i", [P, 2, NT], i32)
        sb_i = sb("sb_i", [P, 2, NT], i32)
        sa_f = sb("sa_f", [P, 2, NT])
        sb_f = sb("sb_f", [P, 2, NT])
        cmp_t = sb("cmp_t", [P, ST + 1, E - 1])
        eid_f = sb("eid_f", [P, ST + 1])
        eid = [sb(f"eid{n}", [1, ST + 1], i32) for n in range(2)]
        inv = sb("inv", [P, 3, SH])
        gat_f = sb("gat_f", [P, SH])
        gat = [sb(f"gat{n}", [P, SH], i32) for n in range(2)]
        sca = [sb(f"sca{n}", [P, SH], i32) for n in range(2)]
        score = sb("score", [P, SH])
        s_hi, s_lo = sb("s_hi", [P, 2, NT], f32r), sb("s_lo", [P, 2, NT], f32r)
        wts = sb("wts", [P, 2, NT])
        wsum = sb("wsum", [P, E])
        mw_e = sb("mw_e", [P, E])
        mw_t = sb("mw_t", [P, ST + 1])
        cmp_m = sb("cmp_m", [P, ST + 1, E])
        iota_m = sb("iota_m", [P, ST + 1, E])

        zpad = sb("zpad", [P, BATCH])

        a0 = ExitStack()
        q_all = sb("q_all", [P, 4, NT * P], f32r, a0)
        a_all = sb("a_all", [P, NT, D], f32, a0)
        a_cur = sb("a_cur", [P, GT, D], f32, a0)
        qc = [sb(f"qc{u}", [P, 2, P], f32r, a0) for u in range(2)]
        pb_ = sb("pb_", [P, 2, UW], f32, a0)
        pt_hi, pt_lo = sb("pt_hi", [P, NW, P], f32r, a0), sb("pt_lo", [P, NW, P], f32r, a0)
        m_u = sb("m_u", [P, 2, UH], f32, a0)
        mT = sb("mT", [UH, 2, P], f32r, a0)
        rden = sb("rden", [P, 2, UH], f32, a0)
        kraw = sb("kraw", [P, BATCH, UW], f32, a0)
        k_hi, k_lo = sb("k_hi", [P, BATCH, UW], f32r, a0), sb("k_lo", [P, BATCH, UW], f32r, a0)
        vraw = sb("vraw", [P, BATCH, NW, UH * VW], f32, a0)
        v_hi, v_lo = (sb("v_hi", [P, BATCH, NW, UH * VW], f32r, a0), sb("v_lo", [P, BATCH, NW, UH * VW], f32r, a0))
        ksb = sb("ksb", [DH, BATCH, NKEY], f32, a0)
        vsb = sb("vsb", [NKEY, BATCH, VW], f32, a0)
        w1qT = sb("w1qT", [P, KC, D], f32, a0)
        w1k = sb("w1k", [P, KC, D], f32, a0)
        w1v = sb("w1v", [P, KC, D], f32, a0)
        kpT = sb("kpT", [P, KC, BATCH * NKEY], f32, a0)
        a0.close()
        rt = ExitStack()
        ohb = sb("ohb", [P, 2, NT, P], f32r, rt)
        oha = sb("oha", [P, 2, NT, 3, SH], f32r, rt)
        oh_a = sb("oh_a", [P, 2, NT, SH], f32, rt)
        rt.close()

        xr = sb("xr", [P, 2, 2, D])
        xe_hi, xe_lo = sb("xe_hi", [P, 2, KC, FT], f32r), sb("xe_lo", [P, 2, KC, FT], f32r)
        sg = sb("sg", [P, 2, 512])
        hf = sb("hf", [P, 2, 512])
        h_hi, h_lo = sb("h_hi", [P, G0, 2, FT], f32r), sb("h_lo", [P, G0, 2, FT], f32r)
        ye = sb("ye", [P, 2, 2, D])
        gidx, sidx = sb("gidx", [P, 2, 2], i32), sb("sidx", [P, 2, 2], i32)
        wr = sb("wr", [P, NB0, WB])

        t1 = ExitStack()
        pt1_hi, pt1_lo = sb("pt1_hi", [NKEY, GT, P], f32r, t1), sb("pt1_lo", [NKEY, GT, P], f32r, t1)
        p1 = sb("p1", [P, GT, KP], f32, t1)
        sT = sb("sT", [NKEY, GW], f32, t1)
        m1 = sb("m1", [P, GT], f32, t1)
        den1 = sb("den1", [P, GT], f32, t1)
        ws_hi, ws_lo = sb("ws_hi", [P, 3, KC, D], f32r, t1), sb("ws_lo", [P, 3, KC, D], f32r, t1)
        sgs = sb("sgs", [P, KC, GW], f32, t1)
        hfs = sb("hfs", [P, KC, GW], f32, t1)
        hs_hi, hs_lo = sb("hs_hi", [P, KC, GW], f32r, t1), sb("hs_lo", [P, KC, GW], f32r, t1)
        t1.close()
        w_hi, w_lo = sb("w_hi", [P, NB0, WB], f32r), sb("w_lo", [P, NB0, WB], f32r)
        wsr = wr[:, 0:2, :].rearrange("p b n -> p (b n)")[:, 0:3 * KC * D].rearrange("p (w c n) -> p w c n", w=3, c=KC)

        ps = ctx.enter_context(nc.psum_tensor("ps", [P, 8, 512], f32))

        x_first, x_in, c_in, w_in0, wc_in, l1_in, ws_in = sem("x_first"), sem("x_in"), sem("c_in"), sem("w_in0"), sem("wc_in"), sem("l1_in"), sem("ws_in")
        zeros_ok, ident_ok, const_ok = sem("zeros_ok"), sem("ident_ok"), sem("const_ok")
        pool_ch, dve_ch = sem("pool_ch"), sem("dve_ch")
        zero_st, pad_st, kv_mm, kv_sb, kv_st, kv_ld, kv_hi, kv_lo = (sem(n) for n in (
            "zero_st", "pad_st", "kv_mm", "kv_sb", "kv_st", "kv_ld", "kv_hi", "kv_lo"))
        ws0_hi, ws0_lo = sem("ws0_hi"), sem("ws0_lo")
        kp_mm, kp_sb, g_mm, v1_mm, vg_hi, vg_lo = (sem(n) for n in (
            "kp_mm", "kp_sb", "g_mm", "v1_mm", "vg_hi", "vg_lo"))

        q_mm, q_hi, q_lo = sem("q_mm"), sem("q_hi"), sem("q_lo")
        q_cp, s_mm, s_max, pt0_mm, pt1_mm, mt_mm, mt_ok, pt_hs, pt_ls, sh_mm, s_exp, pv_mm, a_ok = (sem(n) for n in (
            "q_cp", "s_mm", "s_max", "pt0_mm", "pt1_mm", "mt_mm", "mt_ok", "pt_hs", "pt_ls", "sh_mm", "s_exp",
            "pv_mm", "a_ok"))
        ac_ok, at_mm, at_hi, at_lo, cc_mm, x1_ok, x1_st, xn_st, xm_st = (sem(n) for n in (
            "ac_ok", "at_mm", "at_hi", "at_lo", "cc_mm", "x1_ok", "x1_st", "xn_st", "xm_st"))
        lg_mm, lg_ok = sem("lg_mm"), sem("lg_ok")

        def route_sems(n):
            return {k: sem(f"r{n}_{k}") for k in ("sub", "exp", "msk", "mm", "place", "ohb", "oha", "inv", "eid", "tab")}

        r0, r1 = route_sems(0), route_sems(1)
        ws_ok, ws_mm, mw_ok = sem("ws_ok"), sem("ws_mm"), sem("mw_ok")
        lt_mm, lt_cp, st_mm, st_cp = sem("lt_mm"), sem("lt_cp"), sem("st_mm"), sem("st_cp")
        x2_in = sem("x2_in")
        l_mm, l_max, l_exp, p1_mm, p1_hs, p1_ls, o1_mm, x3_ok = (sem(n) for n in (
            "l_mm", "l_max", "l_exp", "p1_mm", "p1_hs", "p1_ls", "o1_mm", "x3_ok"))
        sgu_mm, ss_ok, shf_ok, sh_hi, sh_lo, sd_mm, so_ok, so_st, wss_hi, wss_lo = (sem(n) for n in (
            "sgu_mm", "ss_ok", "shf_ok", "sh_hi", "sh_lo", "sd_mm", "so_ok", "so_st", "wss_hi", "wss_lo"))

        def ffn_sems(n):
            return {k: sem(f"f{n}_{k}") for k in ("idx", "w_hi", "w_lo", "xt_mm", "xt_hi", "xt_lo", "gu_mm",
                                                  "silu", "h_mul", "h_hi", "h_lo", "d_mm", "y_ok", "y_st")}

        f0, f1 = ffn_sems(0), ffn_sems(1)
        w_in = [sem(f"w_in_{b}") for b in range(NB0)]
        x0_in, x1_in = sem("x0_in"), [sem(f"x1_in{p}") for p in range(2)]
        x_sc = [sem(f"x_sc{h}") for h in range(2)]
        wd_hi, wd_lo = sem("wd_hi"), sem("wd_lo")
        passed = sem("passed")
        block = ctx.enter_context(nc.Block())

        def mm(out, w, x, start, stop):
            return nc.tensor.matmul(out, w, x, start=start, stop=stop, skip_group_check=True)

        def mm3(out, pairs):
            for n, (wh, wl, xh, xl) in enumerate(pairs):
                mm(out, wh, xh, n == 0, False)
                mm(out, wh, xl, False, False)
                last = mm(out, wl, xh, False, n == len(pairs) - 1)
            return last

        def win(j):
            return min(P * j, UW - P)

        def head(j):
            return min(win(j) // NKEY, UH - WINH)

        def group(t, g):
            return t[:, ds(g * GT, GT), :]

        def rows(t, g):
            return t[ds(g * GW, GW), :].rearrange("(t p) d -> p t d", p=P)

        def batch_of(g):
            assert NG // BATCH == 2 and BATCH == 2
            return g // (NG // BATCH) if isinstance(g, int) else BATCH - 1

        def b_tile(a, n=E):
            return a.rearrange("p (t o) -> p t o", o=1).to_broadcast([P, a.shape[1], n])

        def b_row(a, n):
            return a.rearrange("p (o e) -> p o e", o=1).to_broadcast([P, n, a.shape[1]])

        def q_rows(g):
            return (na, nb)[g % 2]

        def q_bank(g):
            return (2, 6)[g % 2]

        def alone(engine):
            engine.sem_inc(passed, 1)

        @block.sync
        def _(sp):
            def load_x(g):
                sp.dma_start(x_all[:, g * GT:(g + 1) * GT, :], A["x"][:, g * GT:(g + 1) * GT, :]
                             ).then_inc(x_in if g else x_first, 16)

            sp.dma_start(ctxT[:, :, :], A["ctxT"]).then_inc(c_in, 16)
            sp.dma_start(wkv[:, :, :], A["wkv"]).then_inc(c_in, 16)
            load_x(0)
            for dst, name in ((w1k, "w1k"), (w1qT, "w1qT"), (w1v, "w1v")):
                sp.dma_start(dst[:, :, :], A[name]).then_inc(l1_in, 16)
            sp.dma_start(bk[:, :], A["bk"]).then_inc(l1_in, 16)
            sp.dma_start(bq[:, :], A["bq"]).then_inc(l1_in, 16)
            sp.dma_start(bv[:, :], A["bv"]).then_inc(l1_in, 16)
            sp.dma_start(wraw[:, :, :], A["wq"]).then_inc(w_in0, 16)
            for g in range(1, NG):
                load_x(g)
            sp.wait_ge(zeros_ok, 1)
            sp.dma_start(kblk_d.rearrange("b p n -> p b n"),
                         zeros[:, 0:BATCH * UW].rearrange("p (b n) -> p b n", b=BATCH)).then_inc(zero_st, 16)
            sp.dma_start(vblk_d.rearrange("b (j p) n -> p (b j) n", p=P),
                         zeros[:, :].rearrange("p (b n) -> p b n", n=UH * VW)).then_inc(zero_st, 16)
            sp.dma_start(res_d[NT * P:ROWS, :].rearrange("(h p) d -> p h d", p=P),
                         zeros[:, 0:2 * D].rearrange("p (h d) -> p h d", h=2)).then_inc(pad_st, 16)
            sp.dma_start(out_d[NT * P:ROWS, :].rearrange("(h p) d -> p h d", p=P),
                         zeros[:, 0:2 * D].rearrange("p (h d) -> p h d", h=2)).then_inc(pad_st, 16)
            sp.dma_start(wraw2[:, :, :], A["wc"]).then_inc(wc_in, 16)
            sp.dma_start(rw[:, :, :, :], A["rw"]).then_inc(wc_in, 16)
            sp.wait_ge(zero_st, 32)
            sp.wait_ge(kv_sb, 2)
            cut = 4 * P - 6 * NKEY
            skip = NW * P - UW
            for b in range(BATCH):
                kd = bass.AP(tensor=kblk_d.tensor, offset=b * P * UW, ap=[[UW, DH], [DH * UW + NKEY, UH], [1, NKEY]])
                sp.dma_start(kd, ksb[:, b:b + 1, :].to_broadcast([DH, UH, NKEY])).then_inc(kv_st, 16)
                base, w = b * NW * P * UH * VW, UH * VW
                vd = bass.AP(tensor=vblk_d.tensor, offset=base, ap=[[w, NKEY], [NKEY * w + VW, 6], [1, VW]])
                sp.dma_start(vd, vsb[:, b:b + 1, :].to_broadcast([NKEY, 6, VW])).then_inc(kv_st, 16)
                for head_, k0, k1, up in ((6, 0, cut, 0), (6, cut, NKEY, skip), (7, 0, NKEY, skip)):
                    r = head_ * NKEY + up
                    sp.dma_start(vblk_d[b, r + k0:r + k1, head_ * VW:(head_ + 1) * VW],
                                 vsb[k0:k1, b, :]).then_inc(kv_st, 16)
            sp.wait_ge(kv_st, 16 * 5 * BATCH)
            sp.dma_start(kraw[:, :, :], kblk_d.rearrange("b p n -> p b n")).then_inc(kv_ld, 16)
            sp.dma_start(vraw[:, :, :, :], vblk_d.rearrange("b (j p) n -> p b j n", p=P)).then_inc(kv_ld, 16)

            with sp.Fori(0, NG) as g:
                sp.wait_ge(x1_ok, 2 * g + 2)
                sp.dma_start(rows(res_d, g), group(x_all, g)).then_inc(x1_st, 16)
                sp.wait_ge(nb["xn"], g + 1)
                sp.dma_start(rows(xn_d, g), nb["x"][:, :, :]).then_inc(xn_st, 16)

            sp.wait_ge(r0["eid"], 1)

            def load0(t, first=False):
                e = sp.value_load(eid[0][0:1, ds(t, 1)], min_val=0, max_val=E - 1)
                for b in range(NB0):
                    if not first:
                        sp.wait_ge(f0["w_lo"], (t - 1) * NB0 + b + 1)
                    sp.dma_start(wr[:, b, :], A["w0"][ds(e * (NB0 * P) + b * P, P), :]).then_inc(w_in[b], 16)

            load0(0, True)
            with sp.Fori(1, ST) as t:
                load0(t)

            sp.wait_ge(f0["w_lo"], NB0 * ST)
            sp.dma_start(wsr, A["ws"]).then_inc(ws_in, 16)
            sp.wait_ge(f0["y_st"], 32 * ST)
            for g in range(NG):
                sp.dma_start(group(x_all, g), rows(res_d, g)).then_inc((x_first, x_in)[g] if g < 2 else x2_in, 16)
            with sp.Fori(0, NG) as g:
                sp.wait_ge(nb["xn"], NG + g + 1)
                sp.dma_start(rows(xm_d, g), nb["x"][:, :, :]).then_inc(xm_st, 16)
            for g in range(NG - 1):
                sp.wait_ge(so_ok, 2 * g + 2)
                sp.dma_start(rows(out_d, g), group(x_all, g)).then_inc(so_st, 16)

            sp.wait_ge(r1["eid"], 1)

            def load1(t, p, first=False):
                e = sp.value_load(eid[1][0:1, ds(t, 1)], min_val=0, max_val=E - 1)
                for b, (name, n, lo) in enumerate((("w1gu", WB, f1["w_lo"]), ("w1d", WB // 2, wd_lo))):
                    if not first:
                        sp.wait_ge(lo, t - 1)
                    sp.dma_start(wr[:, 2 * p + b, 0:n], A[name][ds(e * P, P), :]).then_inc(w_in[2 * p + b], 16)

            load1(0, 0, True)
            load1(1, 1, True)
            sp.wait_ge(so_ok, 2 * NG)
            sp.dma_start(rows(out_d, NG - 1), group(x_all, NG - 1)).then_inc(so_st, 16)
            with sp.Fori(1, ST // 2) as i:
                load1(2 * i, 0)
                load1(2 * i + 1, 1)
            load1(ST - 1, 0)
            for s, v in ((f1["y_st"], 32 * ST), (so_st, 16 * NG), (pad_st, 32), (xm_st, 16 * NG), (xn_st, 16 * NG),
                         (x1_st, 16 * NG)):
                sp.wait_ge(s, v)

        @block.gpsimd
        def _(pool):
            g = nc.gpsimd
            ch = Count(pool_ch)

            def link(ins):
                ins.then_inc(ch.sem, 1)
                pool.wait_ge(ch.sem, ch.up())

            def root(n, k):
                pool.wait_ge(n["var"], k + 1)
                alone(pool)
                link(g.tensor_scalar(n["rs"][:, :], n["mv"][:, :, 1], EPS, None, ALU.add))
                g.tensor_tensor(n["rs"][:, :], n["rs"][:, :], mhalf[:, :], ALU.pow).then_inc(n["rstd"], 1)

            link(g.memset(ones[:, :], 1.0))
            g.affine_select(out=ident[:, :], in_=ones[:, :], compare_op=ALU.is_equal, fill=0.0, base=0,
                            pattern=[[1, P]], channel_multiplier=-1)
            g.memset(mhalf[:, :], -0.5).then_inc(ident_ok, 1)
            g.memset(zeros[:, :], 0.0).then_inc(zeros_ok, 1)
            link(g.memset(nege[:, :], -1.0))
            root(na, 0)
            link(g.affine_select(out=upper[:, :], in_=ones[:, :], compare_op=ALU.is_gt, fill=0.0, base=0,
                                 pattern=[[1, P]], channel_multiplier=-1))
            link(g.affine_select(out=nege[:, :], in_=nege[:, :], compare_op=ALU.is_ge, fill=0.0, base=0,
                                 pattern=[[1, UW]], channel_multiplier=-NKEY))
            link(g.affine_select(out=nege[:, :], in_=nege[:, :], compare_op=ALU.is_gt, fill=0.0, base=NKEY,
                                 pattern=[[-1, UW]], channel_multiplier=NKEY))
            g.tensor_copy(neg_head[:, :], nege[:, :])
            g.tensor_copy(onesb[:, :], ones[:, :])
            g.tensor_copy(upperb[:, :], upper[:, :])
            io = dict(allow_small_or_imprecise_dtypes=True)
            g.iota(iota_p[:, :], pattern=[[1, P]], base=0, channel_multiplier=0, **io)
            g.iota(iota_h[:, :], pattern=[[1, SH]], base=0, channel_multiplier=0, **io)
            g.iota(tok1[:, :], pattern=[[P, NT]], base=1, channel_multiplier=1, **io)
            g.iota(rank_e[:, :, :], pattern=[[0, NT], [-1, E]], base=E, channel_multiplier=0, **io)
            g.iota(step_k[:, :, :], pattern=[[0, E], [FT, E]], base=0, channel_multiplier=0, **io)
            g.iota(tile_t[:, :, :], pattern=[[1, ST + 1], [0, E - 1]], base=0, channel_multiplier=0, **io)
            g.iota(iota_m[:, :, :], pattern=[[0, ST + 1], [1, E]], base=0, channel_multiplier=0, **io)
            g.iota(pad_row[:, :, :], pattern=[[0, ST], [P, 2]], base=NT * P, channel_multiplier=1, **io).then_inc(const_ok, 1)

            with pool.Fori(1, NG) as gr:
                ch.enter(gr, 1, 1)
                root(na, gr)
                ch.leave(NG - 1)

            def copy_q(i, u, first=False):
                if not first:
                    pool.wait_ge(s_mm, 2 * i + u - 1)
                g.tensor_copy(qc[u][:, :, :], q_all[:, 2 * u:2 * u + 2, ds(i * P, P)]).then_inc(q_cp, 1)

            pool.wait_ge(q_lo, KC)
            copy_q(0, 0, True)
            copy_q(0, 1, True)
            pool.wait_ge(q_lo, KC * NG)
            with pool.Fori(1, NT) as i:
                copy_q(i, 0)
                copy_q(i, 1)

            with pool.Fori(0, NG) as gr:
                ch.enter(gr, 1)
                root(nb, gr)
                ch.leave(NG)

            s_hi32 = s_hi[:, :, :].bitcast(f32)

            def weigh_one_hots(n, r):
                for h in range(2):
                    pool.wait_ge(r["place"], h + 1)
                    ts = slice(h * NT // 2, (h + 1) * NT // 2)
                    for c in range(2):
                        for k, val in enumerate((tok1[:, ts], s_hi32[:, c, ts])[:1 if n == 0 else 2]):
                            ins = g.tensor_tensor(oha[:, c, ts, k, :], oh_a[:, c, ts, :], b_tile(val, SH), ALU.mult)
                    ins.then_inc(r["oha"], 1)

            def indices(idx, dst, src, t):
                g.tensor_copy(dst, src[:, ds(2 * t, 2)]).then_inc(idx.sem, 1)
                pool.wait_ge(idx.sem, idx.up())

            def gather(src, p, s):
                for half in range(2):
                    alone(pool)
                    pool.indirect_dma_start(xr[:, p, half, :], None, src,
                                            bass.IndirectOffsetOnAxis(ap=gidx[:, p, half:half + 1], axis=0)
                                            ).then_inc(s, 16)

            def scatter_add(dst, p, f):
                for half in range(2):
                    alone(pool)
                    pool.indirect_dma_start(dst, bass.IndirectOffsetOnAxis(ap=sidx[:, p, half:half + 1], axis=0),
                                            ye[:, p, half, :], None, compute_op=ALU.add).then_inc(f["y_st"], 16)

            weigh_one_hots(0, r0)
            pool.wait_ge(r0["tab"], 1)
            pool.wait_ge(xn_st, 16 * NG)
            pool.wait_ge(x1_st, 16 * NG)
            pool.wait_ge(pad_st, 32)
            idx = Count(f0["idx"])

            def fetch0(t, first=False):
                if not first:
                    pool.wait_ge(x0_in, 32 * t)
                    pool.wait_ge(f0["xt_mm"], t)
                indices(idx, gidx[:, 0, :], gat[0], t)
                gather(xn_d, 0, x0_in)

            def add0(t, first=False):
                if not first:
                    pool.wait_ge(f0["y_st"], 32 * t)
                indices(idx, sidx[:, 0, :], sca[0], t)
                pool.wait_ge(f0["y_ok"], 2 * t + 2)
                scatter_add(res_d, 0, f0)

            fetch0(0, True)
            fetch0(1)
            pool.wait_ge(r0["tab"], 2)
            add0(0, True)
            with pool.Fori(1, ST - 1) as t:
                idx.enter(t, 2, 1)
                fetch0(t + 1)
                add0(t)
                idx.leave(ST - 2)
            add0(ST - 1)

            root(na, NG)
            root(na, NG + 1)
            with pool.Fori(0, NG - 2) as gr:
                ch.enter(gr, 2)
                root(nb, NG + gr)
                root(na, NG + gr + 2)
                ch.leave(NG - 2)
            root(nb, 2 * NG - 2)
            root(nb, 2 * NG - 1)

            weigh_one_hots(1, r1)
            pool.wait_ge(r1["tab"], 1)
            pool.wait_ge(xm_st, 16 * NG)
            idx = Count(f1["idx"])

            def fetch1(i, p, first=False):
                t = 2 * i + p
                if not first:
                    pool.wait_ge(x1_in[p], 32 * i)
                    pool.wait_ge(f1["xt_mm"], t - 1)
                indices(idx, gidx[:, p, :], gat[1], t)
                gather(xm_d, p, x1_in[p])

            def add1(i, p, first=False):
                t = 2 * i + p
                indices(idx, sidx[:, p, :], sca[1], t)
                pool.wait_ge(f1["y_ok"], 2 * t + 2)
                if not first:
                    pool.wait_ge(f1["y_st"], 32 * t)
                scatter_add(out_d, p, f1)

            for t in range(5):
                fetch1(t // 2, t % 2, t < 2)
            pool.wait_ge(r1["tab"], 2)
            pool.wait_ge(so_st, 16 * NG)
            fetch1(2, 1)
            add1(0, 0, True)
            fetch1(3, 0)
            add1(0, 1)
            with pool.Fori(1, (ST - 5) // 2) as i:
                idx.enter(i, 4, 1)
                fetch1(i + 2, 1)
                add1(i, 0)
                fetch1(i + 3, 0)
                add1(i, 1)
                idx.leave((ST - 5) // 2 - 1)
            for t in range(ST - 5, ST):
                add1(t // 2, t % 2)

        @block.scalar
        def _(act):
            s = nc.scalar

            def copy(o, i):
                return s.activation(o, i, ACT.Copy)

            def split_hi(n, k, b0, to=None):
                for c in range(KC):
                    act.wait_ge(n["mm"], KC * k + c + 1)
                    copy((to or n)["t_hi"][:, c, :], ps[:, b0 + c, :]).then_inc(n["hi"], 1)

            act.wait_ge(w_in0, 16)
            copy(wq_hi[:, :, :], wraw[:, :, :]).then_inc(ws0_hi, 1)

            split_hi(na, 0, 0, q_rows(0))
            split_hi(na, 1, 0, q_rows(1))
            for g in range(NG):
                if g == NG - 2:
                    act.wait_ge(kv_ld, 32)
                    copy(k_hi[:, :, :], kraw[:, :, :]).then_inc(kv_hi, 1)
                    copy(v_hi[:, :, :, :], vraw[:, :, :, :]).then_inc(kv_hi, 1)
                for c in range(KC):
                    act.wait_ge(q_mm, KC * g + c + 1)
                    copy(q_all[:, 2 * c, g * GW:(g + 1) * GW], ps[:, q_bank(g) + c, :]).then_inc(q_hi, 1)
                if g < NG - 2:
                    split_hi(na, g + 2, 0, q_rows(g + 2))

            def step(n, u, prev=True, cur=True):
                if prev:
                    act.wait_ge(pt0_mm, n)
                    copy(pt_hi[:, 0:3, :], ps[:, 4, 0:3 * P]).then_inc(pt_hs, 1)
                if cur:
                    act.wait_ge(mt_mm, n + 1)
                    copy(mT[:, u, :], ps[0:UH, 5, 3 * P:4 * P]).then_inc(mt_ok, 1)
                if prev:
                    act.wait_ge(pt1_mm, n)
                    copy(pt_hi[:, 3:5, :], ps[:, 5, 0:2 * P]).then_inc(pt_hs, 1)
                if cur:
                    act.wait_ge(sh_mm, n + 1)
                    s.activation(pb_[:, u, :].rearrange("p (a n) -> p a n", a=2),
                                 ps[:, 2 * u:2 * u + 2, 0:HB], ACT.Exp, scale=DH ** -0.5).then_inc(s_exp, 1)

            step(0, 0, prev=False)
            act.wait_ge(v1_mm, 1)
            copy(vp_hi[:, :, :], ps[0:NKEY, 4, :].rearrange("p (b n) -> p b n", b=BATCH)).then_inc(vg_hi, 1)
            act.wait_ge(g_mm, KC)
            for c in range(KC):
                copy(g_hi[:, c, :, 0:NKEY], ps[:, 6 + c, 0:BATCH * NKEY].rearrange("p (b k) -> p b k", b=BATCH)
                     ).then_inc(vg_hi, 1)
            step(1, 1)
            act.wait_ge(wc_in, 32)
            copy(wc_hi[:, :, :], wraw2[:, :, :]).then_inc(ws0_hi, 1)
            copy(rw_hi[:, :, :, :], rw[:, :, :, :]).then_inc(ws0_hi, 1)
            with act.Fori(1, NT) as i:
                step(2 * i, 0)
                step(2 * i + 1, 1)
            step(2 * NT, 0, cur=False)

            act.wait_ge(a_ok, 2 * GT)
            def copy_a(g):
                copy(a_cur[:, :, :], group(a_all, g)).then_inc(ac_ok, 1)

            def copy_logits(k, bank_):
                act.wait_ge(lt_mm, k + 1)
                copy(lgT[:, :], ps[0:E, bank_, :]).then_inc(lt_cp, 1)

            def project(g, cur=True, prev=True, more=True, last=True):
                if cur:
                    for c in range(KC):
                        act.wait_ge(at_mm, KC * g + c + 1)
                        copy(na["t_hi"][:, c, :], ps[:, c, :]).then_inc(at_hi, 1)
                    if more:
                        copy_a(g + 1)
                if last:
                    copy_logits(g - 2, 6)
                if prev:
                    split_hi(nb, g - 1, 4)

            copy_a(0)
            act.wait_ge(a_ok, 2 * NT)
            alone(act)
            project(0, prev=False, last=False)
            project(1, last=False)
            with act.Fori(2, NG - 1) as g:
                project(g)
            project(NG - 1, more=False)
            project(NG, cur=False)
            project(NG + 1, cur=False, prev=False)

            def route(r):
                act.wait_ge(r["sub"], 1)
                s.activation(pr[:, :, :], pr[:, :, :], ACT.Exp).then_inc(r["exp"], 1)

            route(r0)

            def w0_hi(t, b):
                act.wait_ge(w_in[b], 16 * (t + 1))
                copy(w_hi[:, b, :], wr[:, b, :]).then_inc(f0["w_hi"], 1)

            def x_hi(f, t, p=0):
                act.wait_ge(f["xt_mm"], t + 1)
                copy(xe_hi[:, p, :, :].rearrange("p c n -> p (c n)"), ps[:, 6 + p, :]).then_inc(f["xt_hi"], 1)

            def tile0(t, first=False, more=True):
                for q in range(G0):
                    act.wait_ge(f0["gu_mm"], G0 * t + q + 1)
                    s.activation(sg[:, q % 2, :], ps[:, q % 2, :], ACT.Silu).then_inc(f0["silu"], 1)
                    if more and q < G0 - 1:
                        w0_hi(t + 1, q)
                    act.wait_ge(f0["h_mul"], G0 * t + q + 1)
                    copy(h_hi[:, q, :, :].rearrange("p c n -> p (c n)"), hf[:, q % 2, :]).then_inc(f0["h_hi"], 1)
                if more:
                    w0_hi(t + 1, G0 - 1)
                    x_hi(f0, t + 1)
                if first:
                    act.wait_ge(mw_ok, 1)
                else:
                    act.wait_ge(f0["y_st"], 32 * t)
                for half in range(2):
                    act.wait_ge(f0["d_mm"], 2 * t + half + 1)
                    alone(act)
                    s.activation(ye[:, 0, half, :], ps[:, 4 + half, 0:D], ACT.Copy,
                                 scale=mw_t[:, ds(t, 1)]).then_inc(f0["y_ok"], 1)
                if more:
                    w0_hi(t + 1, G0)
                    w0_hi(t + 1, G0 + 1)

            for b in range(NB0):
                w0_hi(0, b)
            x_hi(f0, 0)
            tile0(0, first=True)
            with act.Fori(1, ST - 1) as t:
                tile0(t)
            tile0(ST - 1, more=False)

            act.wait_ge(ws_in, 16)
            copy(ws_hi[:, :, :, :], wsr).then_inc(wss_hi, 1)

            def group1(g, a=True, b=True, c=True, d=True):
                bt = batch_of(g)
                if b and d:
                    copy_logits(NG + g - 2, 2)
                if a:
                    act.wait_ge(st_mm, g + 1)
                    s.activation(sT[:, :], ps[0:NKEY, 0, :], ACT.Identity, bias=c0[:, bt:bt + 1]).then_inc(st_cp, 1)
                    act.wait_ge(l_max, g + 1)
                    for j in range(GT):
                        s.activation(p1[:, j, 0:NKEY], ps[:, 0, j * KP:j * KP + NKEY], ACT.Exp, bias=m1[:, j:j + 1],
                                     scale=D ** -0.5, accum_out=den1[:, j:j + 1]).then_inc(l_exp, 1)
                if b:
                    split_hi(nb, NG + g - 1, 2)
                if a:
                    act.wait_ge(p1_mm, g + 1)
                    copy(pt1_hi[:, :, :].rearrange("p c n -> p (c n)"), ps[0:NKEY, 1, :]).then_inc(p1_hs, 1)
                if not a:
                    copy_logits(2 * NG - 1, 2)
                    route(r1)
                if b:
                    for i in range(KC):
                        act.wait_ge(sgu_mm, KC * (g - 1) + i + 1)
                        s.activation(sgs[:, i, :], ps[:, 4 + 2 * i, :], ACT.Silu).then_inc(ss_ok, 1)
                if c:
                    split_hi(na, NG + g + 1, 0)
                if b:
                    for i in range(KC):
                        act.wait_ge(shf_ok, KC * (g - 1) + i + 1)
                        copy(hs_hi[:, i, :], hfs[:, i, :]).then_inc(sh_hi, 1)

            split_hi(na, NG, 0)
            group1(0, b=False, d=False)
            group1(1, d=False)
            with act.Fori(2, NG - 1) as g:
                group1(g)
            group1(NG - 1, c=False)
            group1(NG, a=False, c=False)

            def w1_hi(i, p, b):
                act.wait_ge(w_in[2 * p + b], 16 * (ST + i + 1))
                n = WB if b == 0 else WB // 2
                copy(w_hi[:, 2 * p + b, 0:n], wr[:, 2 * p + b, 0:n]).then_inc((f1["w_hi"], wd_hi)[b], 1)

            def scale1(i, p):
                act.wait_ge(x1_in[p], 32 * (i + 1))
                alone(act)
                s.activation(xr[:, p, 0, :], xr[:, p, 0, :], ACT.Copy, scale=score[:, ds(4 * i + 2 * p, 1)]
                             ).then_inc(x_sc[0], 1)

            def y1(t, p, first=False):
                if not first:
                    act.wait_ge(f1["y_st"], 32 * (t - 1))
                for half in range(2):
                    act.wait_ge(f1["d_mm"], 2 * t + half + 1)
                    copy(ye[:, p, half, :], ps[:, 4 + half, 0:D]).then_inc(f1["y_ok"], 1)

            def tile1(i, p, x1=True, x2=True, x3=True, prev=1):
                t, o = 2 * i + p, 1 - p
                act.wait_ge(f1["gu_mm"], t + 1)
                s.activation(sg[:, p, :], ps[:, 2 * p, :], ACT.Silu).then_inc(f1["silu"], 1)
                if x2:
                    x_hi(f1, t + 2, p)
                act.wait_ge(f1["h_mul"], t + 1)
                copy(h_hi[:, p, :, :].rearrange("p c n -> p (c n)"), hf[:, p, :]).then_inc(f1["h_hi"], 1)
                if x2:
                    w1_hi(i + 1, p, 0)
                if prev:
                    y1(t - 1, o, first=prev == 2)
                if x1:
                    w1_hi(i + p, o, 1)
                if x3:
                    scale1(i + 1 + p, o)

            act.wait_ge(sd_mm, 2 * NG)
            w1_hi(0, 0, 0)
            w1_hi(0, 1, 0)
            w1_hi(0, 0, 1)
            act.wait_ge(r1["tab"], 2)
            scale1(0, 0)
            scale1(0, 1)
            x_hi(f1, 0, 0)
            x_hi(f1, 1, 1)
            scale1(1, 0)
            tile1(0, 0, prev=0)
            tile1(0, 1, prev=2)
            tile1(1, 0, prev=2)
            tile1(1, 1)
            with act.Fori(2, (ST - 3) // 2) as i:
                tile1(i, 0)
                tile1(i, 1)
            tile1((ST - 3) // 2, 0, x3=False)
            tile1((ST - 3) // 2, 1, x2=False, x3=False)
            tile1(ST // 2, 0, x1=False, x2=False, x3=False)
            y1(ST - 1, 0)

        @block.vector
        def _(dve):
            v = nc.vector
            ch = Count(dve_ch)

            def link(ins):
                ins.then_inc(ch.sem, 1)
                dve.wait_ge(ch.sem, ch.up())

            def sub(o, a, b):
                return v.tensor_tensor(o, a, b, ALU.subtract)

            def statistics(n, src):
                alone(dve)
                for j in range(GT):
                    ins = v.bn_stats(n["st"][:, j, :], src(j))
                link(ins)
                alone(dve)
                for j in range(GT):
                    ins = v.bn_aggr(n["mv"][:, j, :], n["st"][:, j, :])
                ins.then_inc(n["var"], 1)

            def normalise(n, k, src):
                dve.wait_ge(n["rstd"], k + 1)
                for j in range(GT):
                    ins = v.tensor_scalar(n["x"][:, j, :], src(j), n["mv"][:, j, 0:1], n["rs"][:, j:j + 1],
                                          ALU.subtract, ALU.mult)
                ins.then_inc(n["xn"], 1)

            def split_lo(n, k, b0, to=None):
                d = to or n
                for c in range(KC):
                    dve.wait_ge(n["hi"], KC * k + c + 1)
                    sub(d["t_lo"][:, c, :], ps[:, b0 + c, :], d["t_hi"][:, c, :]).then_inc(n["lo"], 1)

            def tile_of(g):
                return lambda j: x_all[:, ds(g * GT + j, 1), :].rearrange("p a d -> p (a d)")

            dve.wait_ge(x_first, 16)
            statistics(na, tile_of(0))
            v.memset(vsb[:, :, :], 0.0)
            link(v.memset(zpad[:, :], 0.0))
            link(v.memset(vsb[:, :, DH:DH + 1], 1.0))
            dve.wait_ge(kv_mm, 1)
            v.tensor_copy(ksb[:, :, :], ps[0:DH, 0, 0:BATCH * NKEY].rearrange("p (b k) -> p b k", b=BATCH)).then_inc(kv_sb, 1)
            v.tensor_copy(vsb[:, :, 0:DH], ps[0:NKEY, 0, 2 * P:2 * P + BATCH * DH].rearrange("p (b k) -> p b k", b=BATCH)
                          ).then_inc(kv_sb, 1)
            dve.wait_ge(kp_mm, KC)
            for c in range(KC):
                v.tensor_scalar(kpT[:, c, :], ps[:, 4 + c, 0:BATCH * NKEY], bk[:, c:c + 1], None, ALU.add).then_inc(kp_sb, 1)
            normalise(na, 0, tile_of(0))
            dve.wait_ge(ws0_hi, 1)
            sub(wq_lo[:, :, :], wraw[:, :, :], wq_hi[:, :, :]).then_inc(ws0_lo, 1)

            def next_rows(g):
                dve.wait_ge(na["mm"], KC * g)
                normalise(na, g, tile_of(g))

            dve.wait_ge(x_in, 16 * (NG - 1))
            statistics(na, tile_of(1))
            split_lo(na, 0, 0, q_rows(0))
            next_rows(1)
            for g in range(NG):
                if g < NG - 2:
                    statistics(na, tile_of(g + 2))
                if g < NG - 1:
                    split_lo(na, g + 1, 0, q_rows(g + 1))
                if g < NG - 2:
                    next_rows(g + 2)
                if g == NG - 2:
                    dve.wait_ge(kv_hi, 2)
                    sub(k_lo[:, :, :], kraw[:, :, :], k_hi[:, :, :]).then_inc(kv_lo, 1)
                    sub(v_lo[:, :, :, :], vraw[:, :, :, :], v_hi[:, :, :, :]).then_inc(kv_lo, 1)
                for c in range(KC):
                    dve.wait_ge(q_hi, KC * g + c + 1)
                    sub(q_all[:, 2 * c + 1, g * GW:(g + 1) * GW], ps[:, q_bank(g) + c, :], q_all[:, 2 * c, g * GW:(g + 1) * GW]
                        ).then_inc(q_lo, 1)

            def top_of(n, u):
                dve.wait_ge(s_mm, n + 1)
                v.tensor_reduce(m_u[:, u, :].rearrange("p (a h) -> p a h", a=2),
                                ps[:, 2 * u:2 * u + 2, 0:HB].rearrange("p a (h k) -> p a h k", k=NKEY),
                                AX.X, ALU.max).then_inc(s_max, 1)

            def step(n, u, i1, prev=True, nxt=True):
                w = 1 - u
                if prev:
                    dve.wait_ge(pt_hs, 2 * n - 1)
                    sub(pt_lo[:, 0:3, :], ps[:, 4, 0:3 * P].rearrange("p (c n) -> p c n", c=3), pt_hi[:, 0:3, :]).then_inc(pt_ls, 1)
                    dve.wait_ge(pt_hs, 2 * n)
                    sub(pt_lo[:, 3:5, :], ps[:, 5, 0:2 * P].rearrange("p (c n) -> p c n", c=2), pt_hi[:, 3:5, :]).then_inc(pt_ls, 1)
                if nxt:
                    top_of(n + 1, w)
                if prev:
                    dve.wait_ge(pv_mm, n)
                    o = ps[:, 6 + w, 0:UH * VW].rearrange("p (h c) -> p h c", c=VW)
                    link(v.reciprocal(rden[:, w, :], o[:, :, DH:DH + 1].rearrange("p h c -> p (h c)")))
                    v.tensor_tensor(a_all[:, ds(i1, 1), w * P:(w + 1) * P].rearrange("p a (h c) -> p (a h) c", c=DH),
                                    o[:, :, 0:DH], rden[:, w, :].rearrange("p (h o) -> p h o", o=1).to_broadcast([P, UH, DH]),
                                    ALU.mult).then_inc(a_ok, 1)

            top_of(0, 0)
            step(0, 0, 0, prev=False)
            dve.wait_ge(vg_hi, 1)
            sub(vp_lo[:, :, :], ps[0:NKEY, 4, :].rearrange("p (b n) -> p b n", b=BATCH), vp_hi[:, :, :]).then_inc(vg_lo, 1)
            dve.wait_ge(vg_hi, 1 + KC)
            for c in range(KC):
                sub(g_lo[:, c, :, 0:NKEY], ps[:, 6 + c, 0:BATCH * NKEY].rearrange("p (b k) -> p b k", b=BATCH),
                    g_hi[:, c, :, 0:NKEY])
            v.tensor_copy(c0[:, :], ps[0:NKEY, 6, 2 * P:2 * P + BATCH]).then_inc(vg_lo, 1)
            for c in range(KC):
                v.tensor_copy(g_lo[:, c, :, NKEY:KP], zpad[:, 0:BATCH].rearrange("p (b k) -> p b k", b=BATCH))
                v.tensor_copy(g_hi[:, c, :, NKEY:KP], zpad[:, 0:BATCH].rearrange("p (b k) -> p b k", b=BATCH)
                              ).then_inc(vg_lo, 1)
            step(1, 1, 0)
            dve.wait_ge(ws0_hi, 3)
            sub(wc_lo[:, :, :], wraw2[:, :, :], wc_hi[:, :, :]).then_inc(ws0_lo, 1)
            sub(rw_lo[:, :, :, :], rw[:, :, :, :], rw_hi[:, :, :, :]).then_inc(ws0_lo, 1)
            with dve.Fori(1, NT - 1) as i:
                ch.enter(i, 2, 1)
                step(2 * i, 0, i - 1)
                step(2 * i + 1, 1, i)
                ch.leave(NT - 2)
            step(2 * NT - 2, 0, NT - 2)
            step(2 * NT - 1, 1, NT - 1, nxt=False)
            step(2 * NT, 0, NT - 1, nxt=False)

            def project(g, cur=True, prev=True, last=True):
                if cur:
                    for c in range(KC):
                        dve.wait_ge(at_hi, KC * g + c + 1)
                        sub(na["t_lo"][:, c, :], ps[:, c, :], na["t_hi"][:, c, :]).then_inc(at_lo, 1)
                if prev:
                    dve.wait_ge(x1_ok, 2 * g)
                    statistics(nb, tile_of(g - 1))
                    if last:
                        dve.wait_ge(xn_st, 16 * (g - 1))
                    normalise(nb, g - 1, tile_of(g - 1))
                if last:
                    dve.wait_ge(lg_mm, g - 1)
                    v.tensor_copy(group(lg, g - 2), ps[:, 6, 0:GT * E].rearrange("p (t e) -> p t e", e=E)
                                  ).then_inc(lg_ok, 1)
                if cur:
                    for h in range(2):
                        dve.wait_ge(cc_mm, 2 * g + h + 1)
                        x2t = x_all[:, ds(g * GT + 2 * h, 2), :]
                        v.tensor_tensor(x2t, ps[:, 2 + h, :].rearrange("p (t d) -> p t d", t=2), x2t, ALU.add
                                        ).then_inc(x1_ok, 1)
                if prev:
                    split_lo(nb, g - 1, 4)

            project(0, prev=False, last=False)
            project(1, last=False)
            with dve.Fori(2, NG) as g:
                ch.enter(g, 1, 2)
                project(g)
                ch.leave(NG - 2)
            project(NG, cur=False)
            dve.wait_ge(lg_mm, NG)
            v.tensor_copy(lg[:, (NG - 1) * GT:NG * GT, :], ps[:, 6, 0:GT * E].rearrange("p (t e) -> p t e", e=E)
                          ).then_inc(lg_ok, 1)

            s_lo32 = s_lo[:, :, :].bitcast(f32)

            def choose(n, r):
                link(v.tensor_reduce(mx[:, :], lg[:, :, :], AX.X, ALU.max))
                sub(pr[:, :, :], lg[:, :, :], b_tile(mx[:, :])).then_inc(r["sub"], 1)
                dve.wait_ge(r["exp"], 1)
                link(v.tensor_reduce(mx[:, :], pr[:, :, :], AX.X, ALU.add))
                link(v.reciprocal(mx[:, :], mx[:, :]))
                link(v.tensor_tensor(pr[:, :, :], pr[:, :, :], b_tile(mx[:, :]), ALU.mult))
                for c in range(2):
                    link(v.tensor_reduce(top[:, c, :], pr[:, :, :], AX.X, ALU.max))
                    link(v.tensor_tensor(key[:, :, :], pr[:, :, :], b_tile(top[:, c, :]), ALU.is_equal))
                    link(v.tensor_tensor(key[:, :, :], key[:, :, :], rank_e[:, :, :], ALU.mult))
                    link(v.tensor_reduce(mx[:, :], key[:, :, :], AX.X, ALU.max))
                    link(v.tensor_tensor(oh[:, c, :, :], key[:, :, :], b_tile(mx[:, :]), ALU.is_equal))
                    if c == 0:
                        link(v.scalar_tensor_tensor(pr[:, :, :], oh[:, 0, :, :], -2.0, pr[:, :, :], ALU.mult, ALU.add))
                v.tensor_tensor(msk[:, :, :], oh[:, 0, :, :], oh[:, 1, :, :], ALU.add).then_inc(r["msk"], 1)
                if n == 1:
                    link(v.tensor_copy(s_hi[:, :, :], top[:, :, :]))
                    link(sub(s_lo[:, :, :], top[:, :, :], s_hi[:, :, :]))

            def place(n, r):
                dve.wait_ge(r["mm"], 1)
                link(v.tensor_copy(tot[:, :, :], ps[:, 0, P:2 * P].rearrange("p (t e) -> p e t", e=E)))
                link(v.tensor_tensor_scan(cum[:, :, :].rearrange("p e t -> p (e t)"), ones[:, :],
                                          tot[:, :, :].rearrange("p e t -> p (e t)"), 0.0, ALU.mult, ALU.add))
                link(v.tensor_reduce(n_e[:, :], tot[:, :, :], AX.X, ALU.add))
                link(v.tensor_tensor(cmp_k[:, :, :], b_tile(n_e[:, :]), step_k[:, :, :], ALU.is_gt))
                link(v.tensor_reduce(c_e[:, :], cmp_k[:, :, :], AX.X, ALU.add))
                link(v.tensor_tensor_scan(cb_e[:, :], ones[:, 0:E], c_e[:, :], 0.0, ALU.mult, ALU.add))
                link(sub(d_e[:, :], cb_e[:, :], c_e[:, :]))
                link(v.scalar_tensor_tensor(d_e[:, :], d_e[:, :], float(FT),
                                            cum[:, :, NT - 1:NT].rearrange("p e o -> p (e o)"), ALU.mult, ALU.subtract))
                link(v.tensor_tensor(d_e[:, :], d_e[:, :], n_e[:, :], ALU.add))
                link(sub(cum[:, :, :], cum[:, :, :], tot[:, :, :]))
                link(v.tensor_tensor(cum[:, :, :], cum[:, :, :], b_tile(d_e[:, :], NT), ALU.add))
                link(v.tensor_tensor(slot[:, :, :], ps[:, 0, 0:P].rearrange("p (t e) -> p t e", e=E),
                                     cum[:, :, :].rearrange("p e t -> p t e"), ALU.add))
                for c in range(2):
                    link(v.tensor_tensor(key[:, :, :], oh[:, c, :, :], slot[:, :, :], ALU.mult))
                    link(v.tensor_reduce(slot2[:, c, :], key[:, :, :], AX.X, ALU.add))
                link(v.tensor_copy(slot_i[:, :, :], slot2[:, :, :]))
                v.tensor_scalar(sb_i[:, :, :], slot_i[:, :, :], P - 1, None, ALU.bitwise_and)
                link(v.tensor_scalar(sa_i[:, :, :], slot_i[:, :, :], 7, None, ALU.arith_shift_right))
                v.tensor_copy(sb_f[:, :, :], sb_i[:, :, :])
                link(v.tensor_copy(sa_f[:, :, :], sa_i[:, :, :]))
                for h in range(2):
                    ts = slice(h * NT // 2, (h + 1) * NT // 2)
                    for c in range(2):
                        ins = v.tensor_tensor(oh_a[:, c, ts, :], b_row(iota_h[:, :], NT // 2), b_tile(sa_f[:, c, ts], SH),
                                              ALU.is_equal)
                    ins.then_inc(r["place"], 1)
                link(v.tensor_tensor(cmp_t[:, :, :], tile_t[:, :, :], b_row(cb_e[:, 0:E - 1], ST + 1), ALU.is_ge))
                link(v.tensor_reduce(eid_f[:, :], cmp_t[:, :, :], AX.X, ALU.add))
                v.tensor_copy(eid[n][:, :], eid_f[0:1, :]).then_inc(r["eid"], 1)
                for h in range(NG):
                    ts = slice(h * GT, (h + 1) * GT)
                    for c in range(2):
                        if n == 1:
                            v.tensor_tensor(oha[:, c, ts, 2, :], oh_a[:, c, ts, :], b_tile(s_lo32[:, c, ts], SH), ALU.mult)
                        v.tensor_tensor(ohb[:, c, ts, :], b_row(iota_p[:, :], GT), b_tile(sb_f[:, c, ts], P),
                                        ALU.is_equal).then_inc(r["ohb"], 1)
                if n == 0:
                    link(v.tensor_tensor(mx[:, :], top[:, 0, :], top[:, 1, :], ALU.add))
                    link(v.reciprocal(mx[:, :], mx[:, :]))
                    for c in range(2):
                        link(v.tensor_tensor(wts[:, c, :], top[:, c, :], mx[:, :], ALU.mult))
                    link(v.tensor_tensor(key[:, :, :], oh[:, 0, :, :], b_tile(wts[:, 0, :]), ALU.mult))
                    link(v.tensor_tensor(tmp3[:, :, :], oh[:, 1, :, :], b_tile(wts[:, 1, :]), ALU.mult))
                    link(v.tensor_tensor(key[:, :, :], key[:, :, :], tmp3[:, :, :], ALU.add))
                    v.tensor_reduce(wsum[:, :], key[:, :, :].rearrange("p t e -> p e t"), AX.X, ALU.add).then_inc(ws_ok, 1)

            def mean_weights():
                dve.wait_ge(ws_mm, 1)
                link(v.tensor_scalar(d_e[:, :], n_e[:, :], 1.0, None, ALU.max))
                link(v.reciprocal(d_e[:, :], d_e[:, :]))
                link(v.tensor_tensor(mw_e[:, :], ps[:, 7, 0:E], d_e[:, :], ALU.mult))
                link(v.tensor_tensor(cmp_m[:, :, :], iota_m[:, :, :], b_tile(eid_f[:, :]), ALU.is_equal))
                link(v.tensor_tensor(cmp_m[:, :, :], cmp_m[:, :, :], b_row(mw_e[:, :], ST + 1), ALU.mult))
                v.tensor_reduce(mw_t[:, :], cmp_m[:, :, :], AX.X, ALU.add).then_inc(mw_ok, 1)

            def tables(n, r):
                parts = 1 if n == 0 else 3
                dve.wait_ge(r["inv"], 1)
                link(v.tensor_copy(inv[:, 0:parts, :], ps[:, 2, 0:parts * SH].rearrange("p (k a) -> p k a", k=parts)))
                v.tensor_scalar(gat[n][:, :], inv[:, 0, :], -1.0, 0.0, ALU.add, ALU.max).then_inc(r["tab"], 1)
                if n == 1:
                    v.tensor_tensor(score[:, :], inv[:, 1, :], inv[:, 2, :], ALU.add)
                v.tensor_scalar(gat_f[:, :], inv[:, 0, :], -1.0, 0.0, ALU.add, ALU.max)
                link(v.tensor_scalar(inv[:, 0, :], inv[:, 0, :], 0.0, None, ALU.is_equal))
                link(v.tensor_tensor(inv[:, 0, :], inv[:, 0, :], pad_row[:, :, :].rearrange("p t h -> p (t h)"), ALU.mult))
                v.tensor_tensor(sca[n][:, :], gat_f[:, :], inv[:, 0, :], ALU.add).then_inc(r["tab"], 1)

            dve.wait_ge(lg_ok, NG)
            choose(0, r0)
            place(0, r0)
            tables(0, r0)

            def w0_lo(t, b):
                dve.wait_ge(f0["w_hi"], NB0 * t + b + 1)
                sub(w_lo[:, b, :], wr[:, b, :], w_hi[:, b, :]).then_inc(f0["w_lo"], 1)

            def x_lo(f, t, p=0):
                dve.wait_ge(f["xt_hi"], t + 1)
                sub(xe_lo[:, p, :, :].rearrange("p c n -> p (c n)"), ps[:, 6 + p, :],
                    xe_hi[:, p, :, :].rearrange("p c n -> p (c n)")).then_inc(f["xt_lo"], 1)

            def tile0(t, more=True):
                for q in range(G0):
                    dve.wait_ge(f0["silu"], G0 * t + q + 1)
                    v.tensor_tensor(hf[:, q % 2, :], ps[:, 2 + q % 2, :], sg[:, q % 2, :], ALU.mult).then_inc(f0["h_mul"], 1)
                    if more and q < G0 - 1:
                        w0_lo(t + 1, q)
                    dve.wait_ge(f0["h_hi"], G0 * t + q + 1)
                    sub(h_lo[:, q, :, :].rearrange("p c n -> p (c n)"), hf[:, q % 2, :],
                        h_hi[:, q, :, :].rearrange("p c n -> p (c n)")).then_inc(f0["h_lo"], 1)
                if more:
                    w0_lo(t + 1, G0 - 1)
                    x_lo(f0, t + 1)
                    w0_lo(t + 1, G0)
                    w0_lo(t + 1, G0 + 1)

            for b in range(NB0):
                w0_lo(0, b)
                if b == 1:
                    x_lo(f0, 0)
            mean_weights()
            with dve.Fori(0, ST - 1) as t:
                tile0(t)
            tile0(ST - 1, more=False)

            dve.wait_ge(wss_hi, 1)
            sub(ws_lo[:, :, :, :], wsr, ws_hi[:, :, :, :]).then_inc(wss_lo, 1)

            def gated(g, i):
                dve.wait_ge(ss_ok, KC * (g - 1) + i + 1)
                v.tensor_tensor(hfs[:, i, :], ps[:, 5 + 2 * i, :], sgs[:, i, :], ALU.mult).then_inc(shf_ok, 1)

            def copy_logits(g):
                dve.wait_ge(lg_mm, NG + g + 1)
                v.tensor_copy(group(lg, g), ps[:, 2, 0:GT * E].rearrange("p (t e) -> p t e", e=E)).then_inc(lg_ok, 1)

            def split_gated(g):
                for i in range(KC):
                    dve.wait_ge(sh_hi, KC * (g - 1) + i + 1)
                    sub(hs_lo[:, i, :], hfs[:, i, :], hs_hi[:, i, :]).then_inc(sh_lo, 1)

            def group1(g, a=True, b=True, c=True, d=True):
                if b and d:
                    copy_logits(g - 2)
                if b:
                    if d:
                        dve.wait_ge(xm_st, 16 * (g - 1))
                    normalise(nb, NG + g - 1, tile_of(g - 1))
                if a:
                    dve.wait_ge(l_mm, g + 1)
                    link(v.tensor_reduce(m1[:, :], ps[:, 0, 0:GT * KP].rearrange("p (t k) -> p t k", k=KP)[:, :, 0:NKEY],
                                         AX.X, ALU.max))
                    v.tensor_scalar(m1[:, :], m1[:, :], -(D ** -0.5), None, ALU.mult).then_inc(l_max, 1)
                if c:
                    dve.wait_ge(x2_in if b else x_in, 16 * (NG - 2) if b else 16 * NG)
                    statistics(na, tile_of(g + 1))

                def add_shared(h):
                    dve.wait_ge(sd_mm, 2 * (g - 2) + h + 1)
                    x2t = x_all[:, ds((g - 2) * GT + 2 * h, 2), :]
                    v.tensor_tensor(x2t, ps[:, 6 + h, :].rearrange("p (t d) -> p t d", t=2), x2t, ALU.add
                                    ).then_inc(so_ok, 1)

                if b:
                    split_lo(nb, NG + g - 1, 2)
                if d:
                    add_shared(0)
                    add_shared(1)
                if a:
                    dve.wait_ge(l_exp, GT * (g + 1))
                    dve.wait_ge(p1_hs, g + 1)
                    sub(pt1_lo[:, :, :].rearrange("p c n -> p (c n)"), ps[0:NKEY, 1, :],
                        pt1_hi[:, :, :].rearrange("p c n -> p (c n)")).then_inc(p1_ls, 1)
                    link(v.reciprocal(den1[:, :], den1[:, :]))
                if c:
                    normalise(na, NG + g + 1, tile_of(g + 1))
                if b and a:
                    gated(g, 0)
                if a:
                    for j in range(GT):
                        dve.wait_ge(o1_mm, GT * g + 2 * (j // 2) + 2)
                        xt = tile_of(g)(j)
                        v.scalar_tensor_tensor(xt, ps[:, j // 2, (j % 2) * D:(j % 2 + 1) * D], den1[:, j:j + 1], xt,
                                               ALU.mult, ALU.add).then_inc(x3_ok, 1)
                if a:
                    dve.wait_ge(x3_ok, GT * (g + 1))
                    statistics(nb, tile_of(g))
                if b and a:
                    gated(g, 1)
                if c:
                    split_lo(na, NG + g + 1, 0)
                if b and a:
                    split_gated(g)
                if b and not a:
                    copy_logits(g - 1)

            dve.wait_ge(x_first, 32)
            statistics(na, tile_of(0))
            normalise(na, NG, tile_of(0))
            split_lo(na, NG, 0)
            group1(0, b=False, d=False)
            group1(1, d=False)
            with dve.Fori(2, NG - 1) as g:
                ch.enter(g, 4, 2)
                group1(g)
                ch.leave(NG - 3)
            group1(NG - 1, c=False)
            group1(NG, a=False, c=False)
            dve.wait_ge(lg_ok, 2 * NG)
            choose(1, r1)
            gated(NG, 0)
            gated(NG, 1)
            split_gated(NG)
            place(1, r1)
            group1(NG + 1, a=False, b=False, c=False)
            tables(1, r1)
            def scale1(i, p):
                dve.wait_ge(x1_in[p], 32 * (i + 1))
                v.tensor_scalar(xr[:, p, 1, :], xr[:, p, 1, :], score[:, ds(4 * i + 2 * p + 1, 1)], None,
                                ALU.mult).then_inc(x_sc[1], 1)

            def w1_lo(t, p, b):
                dve.wait_ge((f1["w_hi"], wd_hi)[b], t + 1)
                n = WB if b == 0 else WB // 2
                sub(w_lo[:, 2 * p + b, 0:n], wr[:, 2 * p + b, 0:n], w_hi[:, 2 * p + b, 0:n]
                    ).then_inc((f1["w_lo"], wd_lo)[b], 1)

            def tile1(i, p, x1=True, x2=True, x3=True):
                t, o = 2 * i + p, 1 - p
                dve.wait_ge(f1["silu"], t + 1)
                v.tensor_tensor(hf[:, p, :], ps[:, 2 * p + 1, :], sg[:, p, :], ALU.mult).then_inc(f1["h_mul"], 1)
                if x2:
                    x_lo(f1, t + 2, p)
                dve.wait_ge(f1["h_hi"], t + 1)
                sub(h_lo[:, p, :, :].rearrange("p c n -> p (c n)"), hf[:, p, :],
                    h_hi[:, p, :, :].rearrange("p c n -> p (c n)")).then_inc(f1["h_lo"], 1)
                if x2:
                    w1_lo(t + 2, p, 0)
                if x3:
                    scale1(i + 1 + p, o)
                if x1:
                    w1_lo(t + 1, o, 1)

            w1_lo(0, 0, 0)
            w1_lo(1, 1, 0)
            scale1(0, 0)
            scale1(0, 1)
            x_lo(f1, 0, 0)
            w1_lo(0, 0, 1)
            x_lo(f1, 1, 1)
            scale1(1, 0)
            with dve.Fori(0, (ST - 3) // 2) as i:
                tile1(i, 0)
                tile1(i, 1)
            tile1((ST - 3) // 2, 0, x3=False)
            tile1((ST - 3) // 2, 1, x2=False, x3=False)
            tile1(ST // 2, 0, x1=False, x2=False, x3=False)

        @block.tensor
        def _(pe):
            T = nc.tensor

            def transpose_group(n, k, b0):
                pe.wait_ge(n["xn"], k + 1)
                for c in range(KC):
                    for j in range(GT):
                        ins = T.transpose(ps[:, b0 + c, j * P:(j + 1) * P], n["x"][:, j, c * P:(c + 1) * P], ident[:, :])
                    ins.then_inc(n["mm"], 1)

            def w3(wh, wl, xh, xl, cols_w, cols_x):
                return [(wh[:, c, cols_w], wl[:, c, cols_w], xh[:, c, cols_x], xl[:, c, cols_x]) for c in range(KC)]

            pe.wait_ge(c_in, 32)
            for c in range(KC):
                mm(ps[0:DH, 0, 0:BATCH * NKEY], wkv[:, c, 0:DH], ctxT[:, c, :], c == 0, c == KC - 1)
            for b in range(BATCH):
                for c in range(KC):
                    ins = mm(ps[0:NKEY, 0, 2 * P + b * DH:2 * P + (b + 1) * DH], ctxT[:, c, b * NKEY:(b + 1) * NKEY],
                             wkv[:, c, DH:2 * DH], c == 0, c == KC - 1)
            ins.then_inc(kv_mm, 1)
            pe.wait_ge(l1_in, 96)
            for e in range(KC):
                for c in range(KC):
                    ins = mm(ps[:, 4 + e, 0:BATCH * NKEY], w1k[:, c, e * P:(e + 1) * P], ctxT[:, c, :], c == 0, c == KC - 1)
                ins.then_inc(kp_mm, 1)
            pe.wait_ge(ident_ok, 1)
            pe.wait_ge(kv_sb, 2)

            def layer1_values():
                for b in range(BATCH):
                    out = ps[0:NKEY, 4, b * D:(b + 1) * D]
                    mm(out, ones[0:1, 0:NKEY], bv[:, :], True, False)
                    for c in range(KC):
                        ins = mm(out, ctxT[:, c, b * NKEY:(b + 1) * NKEY], w1v[:, c, :], False, c == KC - 1)
                ins.then_inc(v1_mm, 1)

            def layer1_keys():
                for b in range(BATCH):
                    for e in range(KC):
                        mm(ps[0:NKEY, 6, 2 * P + b:2 * P + b + 1], kpT[:, e, b * NKEY:(b + 1) * NKEY], bq[:, e:e + 1],
                           e == 0, e == KC - 1)
                for c in range(KC):
                    for e in range(KC):
                        ins = mm(ps[:, 6 + c, 0:BATCH * NKEY], w1qT[:, e, c * P:(c + 1) * P], kpT[:, e, :], e == 0, e == KC - 1)
                    ins.then_inc(g_mm, 1)

            pe.wait_ge(ws0_lo, 1)
            transpose_group(na, 0, 0)
            for g in range(NG):
                pe.wait_ge(na["lo"], KC * (g + 1))
                if g < NG - 1:
                    transpose_group(na, g + 1, 0)
                t = q_rows(g)
                for hc in range(2):
                    mm3(ps[:, q_bank(g) + hc, :], w3(wq_hi, wq_lo, t["t_hi"], t["t_lo"], slice(hc * P, (hc + 1) * P), slice(0, GW))
                        ).then_inc(q_mm, 1)

            def scores(n, u, i):
                b = i // (NT // BATCH)
                pe.wait_ge(q_cp, n + 1)
                for half in range(2):
                    out = ps[:, 2 * u + half, 0:HB]
                    kh = k_hi[:, ds(b, 1), half * HB:(half + 1) * HB].rearrange("p a n -> p (a n)")
                    kl = k_lo[:, ds(b, 1), half * HB:(half + 1) * HB].rearrange("p a n -> p (a n)")
                    mm(out, qc[u][:, 0, :], kh, True, False)
                    mm(out, qc[u][:, 0, :], kl, False, False)
                    ins = mm(out, qc[u][:, 1, :], kh, False, False)
                ins.then_inc(s_mm, 1)

            def step(n, u, i1, i2, prev=True, cur=True, nxt=True):
                w = 1 - u
                if prev:
                    pe.wait_ge(s_exp, n)
                    for j in range(3):
                        ins = T.transpose(ps[:, 4, j * P:(j + 1) * P], pb_[:, w, win(j):win(j) + P], ident[:, :])
                    ins.then_inc(pt0_mm, 1)
                    for j in range(3, NW):
                        ins = T.transpose(ps[:, 5, (j - 3) * P:(j - 2) * P], pb_[:, w, win(j):win(j) + P], ident[:, :])
                    ins.then_inc(pt1_mm, 1)
                if cur:
                    pe.wait_ge(s_max, n + 1)
                    T.transpose(ps[0:UH, 5, 3 * P:4 * P], m_u[:, u, :], ident[:, :]).then_inc(mt_mm, 1)
                if nxt:
                    scores(n + 1, w, i2)
                if cur:
                    pe.wait_ge(mt_ok, n + 1)
                    for half in range(2):
                        ins = mm(ps[:, 2 * u + half, 0:HB], mT[:, u, :], neg_head[:, half * HB:(half + 1) * HB], False, True)
                    ins.then_inc(sh_mm, 1)
                if prev:
                    b = i1 // (NT // BATCH)
                    for j in range(NW):
                        pe.wait_ge(pt_ls, 2 * n - 1 if j < 3 else 2 * n)
                        cols = slice(head(j) * VW, (head(j) + WINH) * VW)
                        vh = v_hi[:, ds(b, 1), j, cols].rearrange("p a n -> p (a n)")
                        vl = v_lo[:, ds(b, 1), j, cols].rearrange("p a n -> p (a n)")
                        out = ps[:, 6 + w, cols]
                        mm(out, pt_hi[:, j, :], vh, j == 0, False)
                        mm(out, pt_hi[:, j, :], vl, False, False)
                        ins = mm(out, pt_lo[:, j, :], vh, False, j == NW - 1)
                    ins.then_inc(pv_mm, 1)

            pe.wait_ge(kv_lo, 2)
            scores(0, 0, 0)
            pe.wait_ge(kp_sb, KC)
            layer1_values()
            pe.wait_ge(const_ok, 1)
            pe.wait_ge(q_lo, KC * NG)
            step(0, 0, 0, 0, prev=False)
            layer1_keys()
            pe.wait_ge(vg_lo, 2)
            step(1, 1, 0, 1)
            with pe.Fori(1, NT - 1) as i:
                step(2 * i, 0, i - 1, i)
                step(2 * i + 1, 1, i, i + 1)
            step(2 * NT - 2, 0, NT - 2, NT - 1)
            step(2 * NT - 1, 1, NT - 1, NT - 1, nxt=False)
            step(2 * NT, 0, NT - 1, NT - 1, cur=False, nxt=False)

            def logits(L, n, k, bank_):
                pe.wait_ge(n["lo"], KC * (k + 1))
                mm3(ps[0:E, bank_, :], [(rw_hi[:, L, c, :], rw_lo[:, L, c, :], n["t_hi"][:, c, :], n["t_lo"][:, c, :])
                                        for c in range(KC)]).then_inc(lt_mm, 1)

            def logits_back(L, g, bank_):
                pe.wait_ge(lt_cp, L * NG + g + 1)
                alone(pe)
                for j in range(GT):
                    ins = T.transpose(ps[:, bank_, j * E:(j + 1) * E], lgT[:, j * P:(j + 1) * P], ident[0:E, 0:E])
                ins.then_inc(lg_mm, 1)

            def project(g, cur=True, prev=True, last=True):
                if cur:
                    pe.wait_ge(ac_ok, g + 1)
                    for c in range(KC):
                        for j in range(GT):
                            ins = T.transpose(ps[:, c, j * P:(j + 1) * P], a_cur[:, j, c * P:(c + 1) * P], ident[:, :])
                        ins.then_inc(at_mm, 1)
                if last:
                    logits(0, nb, g - 2, 6)
                    if not cur:
                        logits_back(0, g - 2, 6)
                if cur:
                    pe.wait_ge(at_lo, KC * (g + 1))
                    for j in range(GT):
                        ins = mm3(ps[:, 2 + j // 2, (j % 2) * D:(j % 2 + 1) * D],
                                  [(na["t_hi"][:, c, j * P:(j + 1) * P], na["t_lo"][:, c, j * P:(j + 1) * P],
                                    wc_hi[:, c, :], wc_lo[:, c, :]) for c in range(KC)])
                        if j % 2:
                            ins.then_inc(cc_mm, 1)
                if last and cur:
                    logits_back(0, g - 2, 6)
                if prev:
                    transpose_group(nb, g - 1, 4)

            pe.wait_ge(ws0_lo, 3)
            project(0, prev=False, last=False)
            project(1, last=False)
            with pe.Fori(2, NG) as g:
                project(g)
            project(NG, cur=False)
            project(NG + 1, cur=False, prev=False)

            def count(n, r):
                pe.wait_ge(r["msk"], 1)
                m2 = msk[:, :, :].rearrange("p t e -> p (t e)")
                mm(ps[:, 0, 0:P], upperb[:, :], m2, True, True)
                mm(ps[:, 0, P:2 * P], onesb[:, :], m2, True, True).then_inc(r["mm"], 1)
            def invert(r, parts):
                for t in range(NT):
                    if t % GT == 0:
                        pe.wait_ge(r["ohb"], 2 + 2 * t // GT)
                    if t % (NT // 2) == 0:
                        pe.wait_ge(r["oha"], 1 + 2 * t // NT)
                    for c in range(2):
                        ins = mm(ps[:, 2, 0:parts * SH], ohb[:, c, t, :],
                                 oha[:, c, t, 0:parts, :].rearrange("p k a -> p (k a)"),
                                 t == 0 and c == 0, t == NT - 1 and c == 1)
                ins.then_inc(r["inv"], 1)

            count(0, r0)
            invert(r0, 1)
            pe.wait_ge(ws_ok, 1)
            mm(ps[:, 7, 0:E], ones[:, :], wsum[:, :], True, True).then_inc(ws_mm, 1)

            def transpose_x(f, p):
                for c in range(KC):
                    for half in range(2):
                        ins = T.transpose(ps[:, 6 + p, c * FT + half * P:c * FT + (half + 1) * P],
                                          xr[:, p, half, c * P:(c + 1) * P], ident[:, :])
                ins.then_inc(f["xt_mm"], 1)

            def transpose0(t):
                pe.wait_ge(x0_in, 32 * (t + 1))
                transpose_x(f0, 0)

            def gate_up(wb, bg, bu, p):
                for which, bk_ in ((0, bg), (1, bu)):
                    for j in range(2):
                        cols = [slice(c * 512 + which * 256 + j * P, c * 512 + which * 256 + (j + 1) * P) for c in range(KC)]
                        ins = mm3(ps[:, bk_, j * FT:(j + 1) * FT],
                                  [(w_hi[:, wb, cols[c]], w_lo[:, wb, cols[c]], xe_hi[:, p, c, :], xe_lo[:, p, c, :])
                                   for c in range(KC)])
                return ins

            def down(k, half, wb, start, stop, row=None):
                q, j = k // 2 if row is None else row, k % 2
                out, hs = ps[:, 4 + half, 0:D], slice(half * P, (half + 1) * P)
                ws = slice((k % 4) * D, (k % 4 + 1) * D)
                mm(out, h_hi[:, q, j, hs], w_hi[:, wb, ws], start, False)
                mm(out, h_hi[:, q, j, hs], w_lo[:, wb, ws], False, False)
                return mm(out, h_lo[:, q, j, hs], w_hi[:, wb, ws], False, stop)

            def tile0(t, first=False, more=True):
                pe.wait_ge(f0["xt_lo"], t + 1)
                for q in range(G0):
                    pe.wait_ge(f0["w_lo"], NB0 * t + q + 1)
                    if not first or q >= 2:
                        pe.wait_ge(f0["h_mul"], G0 * t + q - 1)
                    gate_up(q, q % 2, 2 + q % 2, 0).then_inc(f0["gu_mm"], 1)
                if more:
                    transpose0(t + 1)
                pe.wait_ge(f0["w_lo"], NB0 * t + NB0)
                if not first:
                    pe.wait_ge(f0["y_ok"], 2 * t)
                for part in (range(0, 6), range(6, 8)):
                    for half in range(2):
                        for k in part:
                            pe.wait_ge(f0["h_lo"], G0 * t + k // 2 + 1)
                            ins = down(k, half, G0 + k // 4, k == 0, k == 7)
                        if k == 7:
                            ins.then_inc(f0["d_mm"], 1)

            transpose0(0)
            tile0(0, first=True)
            with pe.Fori(1, ST - 1) as t:
                tile0(t)
            tile0(ST - 1, more=False)

            pe.wait_ge(wss_lo, 1)
            pe.wait_ge(vg_lo, 2 + KC)

            def group1(g, a=True, b=True, d=True):
                bt = batch_of(g)

                def shared(c):
                    for which in range(2):
                        ins = mm3(ps[:, 4 + 2 * c + which, :],
                                  [(ws_hi[:, which, k, c * P:(c + 1) * P], ws_lo[:, which, k, c * P:(c + 1) * P],
                                    nb["t_hi"][:, k, :], nb["t_lo"][:, k, :]) for k in range(KC)])
                    ins.then_inc(sgu_mm, 1)

                def scores():
                    pe.wait_ge(na["lo"], KC * (NG + g + 1))
                    mm3(ps[0:KP, 0, :], [(g_hi[:, c, bt, :], g_lo[:, c, bt, :], na["t_hi"][:, c, :], na["t_lo"][:, c, :])
                                         for c in range(KC)]).then_inc(st_mm, 1)

                def scores_back():
                    pe.wait_ge(st_cp, g + 1)
                    for j in range(GT):
                        ins = T.transpose(ps[:, 0, j * KP:j * KP + NKEY], sT[:, j * P:(j + 1) * P], ident[0:NKEY, 0:NKEY])
                    ins.then_inc(l_mm, 1)

                def shared_down(h):
                    if h == 0:
                        pe.wait_ge(sh_lo, KC * (g - 1))
                    for j in (2 * h, 2 * h + 1):
                        ins = mm3(ps[:, 6 + h, (j % 2) * D:(j % 2 + 1) * D],
                                  [(hs_hi[:, c, j * P:(j + 1) * P], hs_lo[:, c, j * P:(j + 1) * P],
                                    ws_hi[:, 2, c, :], ws_lo[:, 2, c, :]) for c in range(KC)])
                    ins.then_inc(sd_mm, 1)

                if a:
                    if b:
                        pe.wait_ge(x3_ok, GT * g)
                    transpose_group(na, NG + g, 0)
                if d and b:
                    logits(1, nb, NG + g - 2, 2)
                if a:
                    scores()
                if b and d:
                    logits_back(1, g - 2, 2)
                if d:
                    shared_down(0)
                if a:
                    scores_back()
                if b:
                    if d:
                        pe.wait_ge(lg_ok, NG + g - 1)
                    transpose_group(nb, NG + g - 1, 2)
                if d:
                    shared_down(1)
                if a:
                    pe.wait_ge(l_exp, GT * (g + 1))
                    for j in range(GT):
                        ins = T.transpose(ps[0:NKEY, 1, j * P:(j + 1) * P], p1[:, j, 0:NKEY], ident[:, :])
                    ins.then_inc(p1_mm, 1)
                if b:
                    pe.wait_ge(nb["lo"], KC * (NG + g))
                    if not a:
                        logits(1, nb, NG + g - 1, 2)
                        logits_back(1, NG - 1, 2)
                    shared(0)
                if a:
                    pe.wait_ge(p1_ls, g + 1)
                    for j in range(GT):
                        out = ps[:, j // 2, (j % 2) * D:(j % 2 + 1) * D]
                        vh, vl = vp_hi[:, bt, :], vp_lo[:, bt, :]
                        mm(out, pt1_hi[:, j, :], vh, True, False)
                        mm(out, pt1_hi[:, j, :], vl, False, False)
                        mm(out, pt1_lo[:, j, :], vh, False, True).then_inc(o1_mm, 1)
                if b:
                    if d:
                        pe.wait_ge(so_ok, 2 * (g - 1))
                    shared(1)

            group1(0, b=False, d=False)
            group1(1, d=False)
            with pe.Fori(2, NG) as g:
                group1(g)
            group1(NG, a=False)
            count(1, r1)
            group1(NG + 1, a=False, b=False)
            invert(r1, 3)

            def transpose1(t, p):
                for h in range(2):
                    pe.wait_ge(x_sc[h], t + 1)
                transpose_x(f1, p)

            def down1(t, p, first=False):
                pe.wait_ge(f1["h_lo"], t + 1)
                pe.wait_ge(wd_lo, t + 1)
                if not first:
                    pe.wait_ge(f1["y_ok"], 2 * t)
                for half in range(2):
                    for k in range(2):
                        ins = down(k, half, 2 * p + 1, k == 0, k == 1, row=p)
                    ins.then_inc(f1["d_mm"], 1)

            def tile1(t, p, start=False, more=True):
                pe.wait_ge(f1["xt_lo"], t + 1)
                pe.wait_ge(f1["w_lo"], t + 1)
                if not start:
                    pe.wait_ge(f1["h_mul"], t - 1)
                gate_up(2 * p, 2 * p, 2 * p + 1, p).then_inc(f1["gu_mm"], 1)
                if more:
                    transpose1(t + 2, p)

            transpose1(0, 0)
            transpose1(1, 1)
            tile1(0, 0, start=True)
            tile1(1, 1, start=True)
            down1(0, 0, first=True)
            with pe.Fori(1, (ST - 3) // 2) as i:
                tile1(2 * i, 0)
                down1(2 * i - 1, 1)
                tile1(2 * i + 1, 1)
                down1(2 * i, 0)
            tile1(ST - 3, 0)
            down1(ST - 4, 1)
            tile1(ST - 2, 1, more=False)
            down1(ST - 3, 0)
            tile1(ST - 1, 0, more=False)
            down1(ST - 2, 1)
            down1(ST - 1, 0)


def kernel(**inputs):
    import numpy as _np
    import concourse.bacc as _bacc
    from concourse import mybir as _mybir
    from concourse.bass_utils import run_bass_kernel_spmd as _run

    a = {k: _np.asarray(v) for k, v in inputs.items()}

    def parts(w):
        return w.reshape(KC, P, -1).transpose(1, 0, 2)

    def expert_up(gate, up, groups):
        w = _np.stack([gate, up], axis=1).reshape(E, 2, KC, P, groups, 2 * P)
        return w.transpose(0, 4, 3, 2, 1, 5).reshape(E, groups, P, -1)

    def expert_down(w, groups):
        return w.reshape(E, groups, -1, P, D).transpose(0, 1, 3, 2, 4).reshape(E, groups, P, -1)

    up0 = expert_up(a["L0_ffn_gate_w"].transpose(0, 2, 1), a["L0_ffn_up_w"].transpose(0, 2, 1), G0)
    down0 = expert_down(a["L0_ffn_down_w"].transpose(0, 2, 1), NB0 - G0)
    arrays = {
        "x": a["x"].reshape(NT, P, D).transpose(1, 0, 2),
        "ctxT": parts(a["ctx_1024"].reshape(BATCH * NKEY, D).T),
        "wkv": parts(a["L0_xattn_w_kv"]),
        "wq": parts(a["L0_xattn_w_q"]),
        "wc": parts(a["L0_xattn_w_concat"]),
        "rw": _np.stack([parts(a["L0_ffn_router_w"].T), parts(a["L1_ffn_gate_w"].T)], axis=1),
        "w1k": parts(a["L1_xattn_Wk"]),
        "w1qT": parts(a["L1_xattn_Wq"].T),
        "w1v": parts(a["L1_xattn_Wv"]),
        "bk": a["L1_xattn_bk"].reshape(KC, P).T,
        "bq": a["L1_xattn_bq"].reshape(KC, P).T,
        "bv": a["L1_xattn_bv"].reshape(1, D),
        "w0": _np.concatenate([up0, down0], axis=1).reshape(E * NB0 * P, WB),
        "w1gu": expert_up(a["L1_ffn_w1"], a["L1_ffn_w3"], 1).reshape(E * P, WB),
        "w1d": expert_down(a["L1_ffn_w2"], 1).reshape(E * P, WB // 2),
        "ws": _np.stack([parts(a["L1_ffn_w1s"][0]), parts(a["L1_ffn_w3s"][0]), parts(a["L1_ffn_w2s"][0])], axis=1),
    }
    arrays = {k: _np.ascontiguousarray(v) for k, v in arrays.items()}
    nc = _bacc.Bacc("TRN2", target_bir_lowering=False, num_devices=1)
    A = {k: nc.dram_tensor(f"in_{k}", v.shape, _mybir.dt.from_np(v.dtype), kind="ExternalInput").ap()
         for k, v in arrays.items()}
    A["out"] = nc.dram_tensor("out", (ROWS, D), _mybir.dt.float32, kind="ExternalOutput").ap()
    build_program(nc, A)
    r = _run(nc, [{f"in_{k}": v for k, v in arrays.items()}], core_ids=[0])
    return r.results[0]["out"][:NT * P].reshape(BATCH, SEQ, D)
```
